# Optimizing a Trainium2 kernel written in Bass

```python
import numpy as np
import jax
import jax.numpy as jnp

def _softmax(x, axis=-1):
    return jax.nn.softmax(x, axis=axis)

def _gelu(x):
    return jax.nn.gelu(x, approximate=True)

def _silu(x):
    return jax.nn.silu(x)

def _sigmoid(x):
    return jax.nn.sigmoid(x)

def _layernorm(x, axis=-1, eps=1e-05):
    m = jnp.mean(x, axis=axis, keepdims=True)
    v = jnp.var(x, axis=axis, keepdims=True)
    return (x - m) / jnp.sqrt(v + eps)

def _scatter_add(tgt, idx, src, axis=0):
    return tgt.at[idx].add(src)

def _segment_sum(src, seg, n):
    return jax.ops.segment_sum(src, seg, n)
kernel_name = 'mk_gnn_preln_d2_gnn_r32_1cfdfe'

def setup_inputs(seed: int=0):
    np.random.seed(seed)
    _w = jnp.asarray

    def _rec_inputs():
        import jax
        import jax.numpy as jnp
        _gk = jax.random.key(seed)
        x = -0.000202 + 1 * jax.random.normal(jax.random.fold_in(_gk, 1), (3125, 128), jnp.float32)
        _s = jax.random.randint(jax.random.fold_in(_gk, 2), (25000,), 0, 3125, jnp.int32)
        _d = jax.random.randint(jax.random.fold_in(_gk, 3), (25000,), 0, 3125, jnp.int32)
        _loop = jnp.arange(3125, dtype=jnp.int32)
        src = jnp.concatenate([_s, _d, _loop])
        dst = jnp.concatenate([_d, _s, _loop])
        _o = jnp.argsort(dst, stable=True)
        src = src[_o]
        dst = dst[_o]
        edge_attr_32 = 0.000196303 + 1.00016 * jax.random.normal(jax.random.fold_in(_gk, 11), (53125, 32), jnp.float32)
        return (x, src, dst, edge_attr_32)
    x, src, dst, edge_attr_32 = _rec_inputs()

    def _L0_gnn_setup():
        import jax, jax.numpy as jnp
        import numpy as np
        N_NODES = 50000
        N_EDGES = 25000
        IN_F = 128
        OUT_F = 128
        HEADS = 8
        HEAD_DIM = OUT_F // HEADS
        EDGE_F = 32
        key = jax.random.key(seed)
        ks = jax.random.split(key, 14)
        s = lambda fan_in: 1.0 / np.sqrt(fan_in)
        return {'node_features': jax.random.normal(ks[0], (N_NODES, IN_F), jnp.float32), 'edge_index': jax.random.randint(ks[1], (2, N_EDGES), 0, N_NODES, jnp.int64), 'edge_features': jax.random.normal(ks[2], (N_EDGES, EDGE_F), jnp.float32), 'Wq': jax.random.uniform(ks[3], (IN_F, OUT_F), jnp.float32, -s(IN_F), s(IN_F)), 'bq': jnp.zeros((OUT_F,), jnp.float32), 'Wk': jax.random.uniform(ks[4], (IN_F, OUT_F), jnp.float32, -s(IN_F), s(IN_F)), 'bk': jnp.zeros((OUT_F,), jnp.float32), 'Wv': jax.random.uniform(ks[5], (IN_F, OUT_F), jnp.float32, -s(IN_F), s(IN_F)), 'bv': jnp.zeros((OUT_F,), jnp.float32), 'We': jax.random.uniform(ks[6], (EDGE_F, HEADS), jnp.float32, -s(EDGE_F), s(EDGE_F)), 'be': jnp.zeros((HEADS,), jnp.float32), 'Wo': jax.random.uniform(ks[7], (OUT_F, OUT_F), jnp.float32, -s(OUT_F), s(OUT_F)), 'bo': jnp.zeros((OUT_F,), jnp.float32)}
    _L0_gnn_all = _L0_gnn_setup()
    _L0_gnn_in = {k: v for k, v in _L0_gnn_all.items() if k in ('Wq', 'bq', 'Wk', 'bk', 'Wv', 'bv', 'We', 'be', 'Wo', 'bo')}
    del _L0_gnn_all

    def _L1_gnn_setup():
        import jax, jax.numpy as jnp
        import numpy as np
        EPS = 1e-15
        MAX_TANH_ARG = 1.0 - 1e-05

        def logmap0(x):
            norm = jnp.linalg.norm(x, axis=-1, keepdims=True)
            norm_c = jnp.clip(norm, EPS, MAX_TANH_ARG)
            scale = jnp.arctanh(norm_c) / jnp.maximum(norm, EPS)
            return scale * x

        def expmap0(v):
            norm = jnp.linalg.norm(v, axis=-1, keepdims=True)
            scale = jnp.tanh(norm) / jnp.maximum(norm, EPS)
            return scale * v
        key = jax.random.key(seed)
        k1, k2, k3, k4 = jax.random.split(key, 4)
        N, E, D_IN, D_OUT = (50000, 18750, 128, 128)
        x = jax.random.uniform(k1, (N, D_IN), dtype=jnp.float32)
        edge_index = jax.random.randint(k2, (2, E), 0, N, dtype=jnp.int32)
        W = jax.random.normal(k3, (D_OUT, D_IN), dtype=jnp.float32) / np.sqrt(D_IN)
        b = jax.random.normal(k4, (D_OUT,), dtype=jnp.float32) * 0.01
        return {'x': x, 'edge_index': edge_index, 'W': W, 'b': b}
    _L1_gnn_all = _L1_gnn_setup()
    _L1_gnn_in = {k: v for k, v in _L1_gnn_all.items() if k in ('W', 'b')}
    del _L1_gnn_all
    return {'x': x, 'src': src, 'dst': dst, 'edge_attr_32': edge_attr_32, 'L0_gnn_Wq': _L0_gnn_in['Wq'], 'L0_gnn_bq': _L0_gnn_in['bq'], 'L0_gnn_Wk': _L0_gnn_in['Wk'], 'L0_gnn_bk': _L0_gnn_in['bk'], 'L0_gnn_Wv': _L0_gnn_in['Wv'], 'L0_gnn_bv': _L0_gnn_in['bv'], 'L0_gnn_We': _L0_gnn_in['We'], 'L0_gnn_be': _L0_gnn_in['be'], 'L0_gnn_Wo': _L0_gnn_in['Wo'], 'L0_gnn_bo': _L0_gnn_in['bo'], 'L1_gnn_W': _L1_gnn_in['W'], 'L1_gnn_b': _L1_gnn_in['b']}

def reference(x, src, dst, edge_attr_32, L0_gnn_Wq, L0_gnn_bq, L0_gnn_Wk, L0_gnn_bk, L0_gnn_Wv, L0_gnn_bv, L0_gnn_We, L0_gnn_be, L0_gnn_Wo, L0_gnn_bo, L1_gnn_W, L1_gnn_b):
    import jax
    import jax.numpy as jnp

    def _L0_gnn_ref(node_features, edge_index, edge_features, Wq, bq, Wk, bk, Wv, bv, We, be, Wo, bo):
        import jax, jax.numpy as jnp
        import numpy as np
        N_NODES = 50000
        N_EDGES = 25000
        IN_F = 128
        OUT_F = 128
        HEADS = 8
        HEAD_DIM = OUT_F // HEADS
        EDGE_F = 32
        n_nodes = node_features.shape[0]
        n_edges = edge_index.shape[1]
        sources, targets = (edge_index[0], edge_index[1])
        scale = HEAD_DIM ** (-0.5)
        Q = (node_features @ Wq + bq).reshape(n_nodes, HEADS, HEAD_DIM)
        K = (node_features @ Wk + bk).reshape(n_nodes, HEADS, HEAD_DIM)
        V = (node_features @ Wv + bv).reshape(n_nodes, HEADS, HEAD_DIM)
        Q_t = Q[targets]
        K_s = K[sources]
        V_s = V[sources]
        scores = jnp.sum(Q_t * K_s, axis=-1) * scale
        scores = scores + (edge_features @ We + be)
        max_s = jax.ops.segment_max(scores, targets, num_segments=n_nodes)
        scores = scores - max_s[targets]
        exp_s = jnp.exp(scores)
        denom = jax.ops.segment_sum(exp_s, targets, num_segments=n_nodes) + 1e-10
        probs = exp_s / denom[targets]
        weighted_V = probs[:, :, None] * V_s
        aggregated = jax.ops.segment_sum(weighted_V.reshape(n_edges, -1), targets, num_segments=n_nodes)
        return aggregated @ Wo + bo

    def _L1_gnn_ref(x, edge_index, W, b):
        import jax, jax.numpy as jnp
        import numpy as np
        EPS = 1e-15
        MAX_TANH_ARG = 1.0 - 1e-05

        def logmap0(x):
            norm = jnp.linalg.norm(x, axis=-1, keepdims=True)
            norm_c = jnp.clip(norm, EPS, MAX_TANH_ARG)
            scale = jnp.arctanh(norm_c) / jnp.maximum(norm, EPS)
            return scale * x

        def expmap0(v):
            norm = jnp.linalg.norm(v, axis=-1, keepdims=True)
            scale = jnp.tanh(norm) / jnp.maximum(norm, EPS)
            return scale * v
        num_nodes = x.shape[0]
        src, dst = (edge_index[0], edge_index[1])
        x_tangent = logmap0(x)
        h = x_tangent @ W.T + b
        ones = jnp.ones(src.shape[0], dtype=jnp.float32)
        deg = jax.ops.segment_sum(ones, dst, num_segments=num_nodes) + jax.ops.segment_sum(ones, src, num_segments=num_nodes)
        deg = jnp.maximum(deg, 1.0)
        dinv = deg ** (-0.5)
        msg = h[src] * (dinv[src] * dinv[dst])[:, None]
        out = jax.ops.segment_sum(msg, dst, num_segments=num_nodes)
        return expmap0(out)
    edge_index = jnp.stack([src, dst])
    h = jnp.maximum(_layernorm(x, axis=-1), 0.0)
    x = x + _L0_gnn_ref(h, edge_index, edge_attr_32, L0_gnn_Wq, L0_gnn_bq, L0_gnn_Wk, L0_gnn_bk, L0_gnn_Wv, L0_gnn_bv, L0_gnn_We, L0_gnn_be, L0_gnn_Wo, L0_gnn_bo)
    h = jnp.maximum(_layernorm(x, axis=-1), 0.0)
    x = x + _L1_gnn_ref(h, edge_index, L1_gnn_W, L1_gnn_b)
    return x

_drawn_inputs = setup_inputs


def setup_inputs(seed=0):
    import zlib

    import numpy as np

    out = dict(_drawn_inputs(seed))
    spreads = {'L0_gnn_bq': (0.0, 0.8),
     'L0_gnn_bk': (0.0, 2.0),
     'L0_gnn_bv': (0.0, 0.1),
     'L0_gnn_be': (0.0, 2.0),
     'L0_gnn_bo': (0.0, 0.1)}
    factors = {'L0_gnn_Wq': 7.679, 'L0_gnn_Wk': 7.372, 'L1_gnn_b': 22.938}
    for name, (base, spread) in spreads.items():
        noise = np.random.default_rng([zlib.crc32(name.encode()), seed]).standard_normal(out[name].shape)
        drawn = base * np.exp(spread * noise) if base else spread * noise
        out[name] = jnp.asarray(drawn.astype(out[name].dtype))
    for name, factor in factors.items():
        out[name] = (out[name] * factor).astype(out[name].dtype)
    return out
```

```python
from contextlib import ExitStack

import numpy as np

import concourse.bass as bass
from concourse import mybir

F32 = mybir.dt.float32
BF16 = mybir.dt.bfloat16
I32 = mybir.dt.int32
ALU = mybir.AluOpType
ACT = mybir.ActivationFunctionType
AX_X = mybir.AxisListType.X

P = 128
N = 3125
NT = 25
NPAD = NT * P
E = 53125
T = 13
GE = P * T
GROUPS = -(-E // GE)
H = 8
DH = 16
D = 128
EF = 32
C = H * (DH + 1)
HT = H * T
BIG = -1.0e30
EPS_LN = 1e-5
ATANH_MAX = 1.0 - 1e-5
SERIES_BELOW = 0.125
HI, LO = 49, 64
HC = 26
HTURNS = GROUPS * T // HC
PCH = 5
CH = [(0, 4), (4, 8), (8, 12), (12, 13)]
NCH = len(CH)


class Steps:

    def __init__(self, nc, eng, sem, base):
        self.nc, self.eng, self.sem, self.base, self.k = nc, eng, sem, base, 0

    def mark(self, ins):
        self.k += 1
        ins.then_inc(self.sem, 1)

    def sync(self):
        self.eng.wait_ge(self.sem, self.base + self.k)

    def then(self, ins):
        self.mark(ins)
        self.eng.wait_ge(self.sem, self.base + self.k)

    def check(self, total):
        assert self.k == total, (self.k, total)


def wait_apart(eng, sem, value, passed):
    if not isinstance(value, int):
        value = eng.to_reg(value)
    eng.wait_ge(*passed)
    eng.wait_ge(sem, value)


RS = 11
NA = 11
NB = 47
N1 = 13


def rsqrt(link, y, v, t):
    nc_v = link.nc.vector
    link.then(nc_v.tensor_scalar(y.bitcast(I32), v.bitcast(I32), 1, None, ALU.logical_shift_right))
    link.then(nc_v.tensor_scalar(y.bitcast(I32), y.bitcast(I32), -1.0, float(0x5F3759DF), ALU.mult, ALU.add))
    for _ in range(3):
        link.then(nc_v.tensor_tensor(t, y, y, ALU.mult))
        link.then(nc_v.scalar_tensor_tensor(out=t, in0=t, scalar=-0.5, in1=v, op0=ALU.mult, op1=ALU.mult))
        link.then(nc_v.scalar_tensor_tensor(out=y, in0=t, scalar=1.5, in1=y, op0=ALU.add, op1=ALU.mult))


def build(nc, x, src_t, dst_t, dst_before, dst_after, dst_first, attr, wqkv, bqkv, we, be, wo, bo, w1t, b1,
          ident_in, iota_in, imj_in, out):
    q_tab = nc.dram_tensor("q_tab", (NPAD, D), F32, kind="Internal").ap()
    kv_tab = nc.dram_tensor("kv_tab", (NPAD, 2 * D), F32, kind="Internal").ap()
    x2_tab = nc.dram_tensor("x2_tab", (N, D + 1), F32, kind="Internal").ap()
    hs_tab = nc.dram_tensor("hs_tab", (N + 1, D), F32, kind="Internal").ap()
    od_tab = nc.dram_tensor("od_tab", (HI * LO, 1), F32, kind="Internal").ap()
    line_tab = nc.dram_tensor("line_tab", (2 * GROUPS, P), F32, kind="Internal").ap()

    with ExitStack() as ctx:
        def sb(name, shape, dt=F32):
            return ctx.enter_context(nc.sbuf_tensor(name, shape, dt))

        def pb(name, shape, dt=F32):
            return ctx.enter_context(nc.psum_tensor(name, shape, dt))

        def sem(name):
            return ctx.enter_context(nc.semaphore(name))

        ident = sb("ident", [P, P])
        iota = sb("iota", [P, P])
        imj = sb("imj", [P, P])
        iota_b = sb("iota_b", [P, LO], BF16)
        ones_row = sb("ones_row", [1, P])
        zero_row = sb("zero_row", [1, D])
        wqkv_s = sb("wqkv_s", [P, 3 * D])
        bqkv_s = sb("bqkv_s", [P, 3 * D])
        we4 = sb("we4", [P, 4 * H])
        be_r = sb("be_r", [1, T, H])
        be_s = sb("be_s", [1, H])
        wo_s = sb("wo_s", [P, D])
        bo_s = sb("bo_s", [1, D])
        w1_s = sb("w1_s", [P, D])
        b1_s = sb("b1_s", [P, D])
        dst_i = sb("dst_i", [P, GROUPS, T], I32)
        src_i = sb("src_i", [P, GROUPS, T], I32)
        before_i = sb("before_i", [P, GROUPS], I32)
        after_i = sb("after_i", [P, GROUPS], I32)
        first_i = sb("first_i", [P, GROUPS], I32)
        first_f = sb("first_f", [P, GROUPS])
        base_f = sb("base_f", [P, GROUPS])
        base_i = sb("base_i", [P, GROUPS], I32)
        delta = sb("delta", [P, GROUPS])
        ofirst = sb("ofirst", [P, GROUPS])
        dloc = sb("dloc", [P, GROUPS, T])
        fwd_reset = sb("fwd_reset", [P, GROUPS, T])
        bwd_reset = sb("bwd_reset", [P, GROUPS, T])
        fwd_reset8 = sb("fwd_reset8", [P, GROUPS, H, T])
        bwd_reset8 = sb("bwd_reset8", [P, GROUPS, H, T])
        fwd_mask = sb("fwd_mask", [P, GROUPS, T])
        bwd_mask = sb("bwd_mask", [P, GROUPS, T])
        part_reset = sb("part_reset", [P, 2, GROUPS])
        part_rows = sb("part_rows", [2 * GROUPS, P])
        line = sb("line", [H, 2 * GROUPS, P])
        lo_f = sb("lo_f", [P, GROUPS, T], BF16)
        hi_f = sb("hi_f", [P, GROUPS, T], BF16)
        od_s = sb("od_s", [HI, LO])
        oh_hi = sb("oh_hi", [P, 2, HC, HI], BF16)
        oh_lo = sb("oh_lo", [P, 2, HC, LO], BF16)
        xt = sb("xt", [P, NT, D])
        xn = sb("xn", [P, 2, D])
        hT = sb("hT", [P, 2, D])
        st6 = sb("st6", [P, NT, 6])
        mv = sb("mv", [P, NT, 2])
        ve = sb("ve", [P, NT])
        rs_a = sb("rs_a", [P, NT])
        rs_t = sb("rs_t", [P, NT])
        qkv = sb("qkv", [P, 2, PCH, 3 * D])
        idx = sb("idx", [P, 2, T], I32)
        attr_s = sb("attr_s", [P, 2, 4, P])
        qwin = sb("qwin", [P, 2, D])
        xwin = sb("xwin", [P, 2, D + 1])
        kv = sb("kv", [P, 2, T, 2 * D])
        S = sb("S", [P, 2, T, P])
        ST = sb("ST", [P, 2, T, P])
        prod = sb("prod", [P, 2, 4, D])
        part_i = prod[:].rearrange("p a t d -> p (a t d)").bitcast(I32)[:, 0:GROUPS * T].rearrange("p (g t) -> p g t", t=T)
        sc = sb("sc", [P, H, T])
        f1 = sb("f1", [P, H, T])
        f2 = sb("f2", [P, H, T])
        bx = sb("bx", [P, H, T])
        tmp8 = sb("tmp8", [P, H, T])
        c1 = sb("c1", [H, 2, P + 1])
        c2 = sb("c2", [H, P + 1])
        z = sb("z", [P, H, T])
        wv = sb("wv", [P, T, C + 1])
        dfac = sb("dfac", [H, 1])
        fac = sb("fac", [H, 1])
        facd = sb("facd", [H, H])
        isf = sb("isf", [H, P])
        shift = sb("shift", [P, 2, P])
        fb = sb("fb", [P, H])
        R = sb("R", [P, 2, C + 1])
        rden = sb("rden", [P, H])
        agn = sb("agn", [P, D])
        agT = sb("agT", [P, D])
        x2 = sb("x2", [P, 2, D + 1])
        bst = sb("bst", [P, 6])
        bmv = sb("bmv", [P, 2])
        v2 = sb("v2", [P, 2])
        y2 = sb("y2", [P, 2])
        t2 = sb("t2", [P, 2])
        xn2 = sb("xn2", [P, D])
        h2T = sb("h2T", [P, D])
        hsq = sb("hsq", [P, D])
        hsr = sb("hsr", [P, D])
        rat = sb("rat", [P, 1])
        ss = sb("ss", [P, 1])
        sm = sb("sm", [P, 16])
        lnv = sb("lnv", [P, 1])
        b1d = sb("b1d", [P, D])
        hs = sb("hs", [P, 2, D])
        y_out = hs
        th = sb("th", [P, 1])
        nrm = sb("nrm", [P, 1])

        ps_q = [pb(f"ps_q{i}", [P, 512]) for i in range(2)]
        ps_s = [pb(f"ps_s{i}", [P, 512]) for i in range(2)]
        ps_b = pb("ps_b", [P, 512])
        ps_r = pb("ps_r", [P, 512])
        ps_c = pb("ps_c", [P, 512])
        ps_f = pb("ps_f", [P, 512])
        p_bias = ps_b[:, 0:HT]
        p_v1 = ps_b[0:H, 128:256]
        p_c1 = ps_b[:, 256:256 + H]
        p_v2 = ps_b[0:H, 288:416]
        p_c2 = ps_b[:, 416:416 + H]
        p_rc = ps_c[:, 0:C + 1]
        p_fb = ps_c[:, 256:256 + H]

        s_in = sem("s_in")
        s_x = sem("s_x")
        s_od_st = sem("s_od_st")
        s_line_st = sem("s_line_st")
        s_line = sem("s_line")
        s_pool0 = sem("s_pool0")
        s_dv0 = sem("s_dv0")
        s_reset = sem("s_reset")
        s_reset8 = sem("s_reset8")
        s_base = sem("s_base")
        s_part = sem("s_part")
        s_partT = sem("s_partT")
        s_partrow = sem("s_partrow")
        s_ber = sem("s_ber")
        s_zero = sem("s_zero")
        s_xn = sem("s_xn")
        s_xnT = sem("s_xnT")
        s_hT = sem("s_hT")
        s_qkvp = sem("s_qkvp")
        s_qkv = sem("s_qkv")
        s_tab = [sem(f"s_tab{i}") for i in range(2)]
        s_oh = sem("s_oh")
        s_hist = sem("s_hist")
        s_od = sem("s_od")
        s_idx = sem("s_idx")
        s_attr = [sem(f"s_attr{i}") for i in range(2)]
        s_qwin = [sem(f"s_qwin{i}") for i in range(2)]
        s_xwin = [sem(f"s_xwin{i}") for i in range(2)]
        s_kv = [sem(f"s_kv{i}") for i in range(2)]
        s_S = sem("s_S")
        s_stp = sem("s_stp")
        s_st = sem("s_st")
        s_qt = sem("s_qt")
        s_prod = sem("s_prod")
        s_bias = sem("s_bias")
        s_sc = sem("s_sc")
        s_v1 = sem("s_v1")
        s_v1T = sem("s_v1T")
        s_cf = sem("s_cf")
        s_cfT = sem("s_cfT")
        s_v2 = sem("s_v2")
        s_v2T = sem("s_v2T")
        s_cb = sem("s_cb")
        s_cbT = sem("s_cbT")
        s_dfac = sem("s_dfac")
        s_fac = sem("s_fac")
        s_facd = sem("s_facd")
        s_z = sem("s_z")
        s_p = sem("s_p")
        s_wv = sem("s_wv")
        s_agg = sem("s_agg")
        s_rc = sem("s_rc")
        s_R = sem("s_R")
        s_agn = sem("s_agn")
        s_agTp = sem("s_agTp")
        s_agT = sem("s_agT")
        s_o = sem("s_o")
        s_x2 = sem("s_x2")
        s_x2st = sem("s_x2st")
        s_xn2 = sem("s_xn2")
        s_xn2T = sem("s_xn2T")
        s_h2T = sem("s_h2T")
        s_ss = sem("s_ss")
        s_h1 = sem("s_h1")
        s_nc = sem("s_nc")
        s_ln = sem("s_ln")
        s_dinv = sem("s_dinv")
        s_b1d = sem("s_b1d")
        s_hs = sem("s_hs")
        s_hsst = sem("s_hsst")
        s_dA = sem("s_dA")
        s_dB = sem("s_dB")
        s_aB = sem("s_aB")
        s_idx1 = sem("s_idx1")
        s_xw1 = [sem(f"s_xw1{i}") for i in range(2)]
        s_g1 = [sem(f"s_g1{i}") for i in range(2)]
        s_S1 = sem("s_S1")
        s_agg1 = sem("s_agg1")
        s_R1 = sem("s_R1")
        s_ss1 = sem("s_ss1")
        s_zz1 = sem("s_zz1")
        s_norm1 = sem("s_norm1")
        s_th1 = sem("s_th1")
        s_y1 = sem("s_y1")
        s_yst = sem("s_yst")
        s_d1 = sem("s_d1")

        block = ctx.enter_context(nc.Block())

        def node_rows(tab):
            return tab.rearrange("(p n) d -> p n d", n=NT)

        def known(g):
            return isinstance(g, int)

        @block.sync
        def _(sp):
            sp.dma_start(xt[:], node_rows(x)).then_inc(s_x, 16)
            for dst, src in ((ident[:], ident_in), (wqkv_s[:], wqkv), (bqkv_s[:], bqkv.partition_broadcast(P)),
                             (iota[:], iota_in), (imj[:], imj_in),
                             (dst_i[:].rearrange("p g t -> p (g t)"), dst_t),
                             (src_i[:].rearrange("p g t -> p (g t)"), src_t),
                             (before_i[:], dst_before), (after_i[:], dst_after),
                             (first_i[:], dst_first.partition_broadcast(P)), (be_s[:], be), (wo_s[:], wo),
                             (bo_s[:], bo), (w1_s[:], w1t), (b1_s[:], b1.partition_broadcast(P))):
                sp.dma_start(dst, src).then_inc(s_in, 16)
            sp.wait_ge(s_pool0, 1)
            for k in range(4):
                sp.dma_start(we4[EF * k:EF * k + EF, H * k:H * k + H], we).then_inc(s_in, 16)
            for c in range(NT // PCH):
                sp.wait_ge(s_qkv, PCH * (c + 1))
                rows = slice(PCH * c, PCH * c + PCH)
                sp.dma_start(node_rows(q_tab)[:, rows, :], qkv[:, c % 2, :, 0:D]).then_inc(s_tab[c % 2], 16)
                sp.dma_start(node_rows(kv_tab)[:, rows, :], qkv[:, c % 2, :, D:3 * D]).then_inc(s_tab[c % 2], 16)
            sp.wait_ge(s_partrow, 2)
            sp.dma_start(line_tab, part_rows[:]).then_inc(s_line_st, 16)
            sp.wait_ge(s_line_st, 16)
            sp.dma_start(line[:], line_tab.partition_broadcast(H)).then_inc(s_line, 16)
            sp.wait_ge(s_base, 1)
            sp.wait_ge(s_tab[0], 32 * 3)
            sp.wait_ge(s_tab[1], 32 * 2)

            def base_of(g):
                return sp.value_load(base_i[0:1, g:g + 1] if known(g) else base_i[0:1, bass.ds(g, 1)],
                                     min_val=0, max_val=N - P)

            def load_edges(g, b):
                if not (known(g) and g < 2):
                    wait_apart(sp, s_bias, g - 1, (s_base, 1))
                sp.dma_start(attr_s[:, b, 0:3, :],
                             attr[bass.ds(g, 1), 0:3 * P, :].rearrange("o (k p) e -> p (o k) e", p=P)).then_inc(s_attr[b], 16)
                sp.dma_start(attr_s[0:EF, b, 3, :],
                             attr[bass.ds(g, 1), 3 * P:T * EF, :].rearrange("o p e -> p (o e)")).then_inc(s_attr[b], 16)
                w = base_of(g)
                if not (known(g) and g < 2):
                    wait_apart(sp, s_qt, NCH * (g - 1), (s_base, 1))
                sp.dma_start(qwin[:, b, :], q_tab[bass.ds(w, P), :]).then_inc(s_qwin[b], 16)

            def load_nodes(g, b):
                w = base_of(g)
                if not (known(g) and g < 2):
                    wait_apart(sp, s_dinv, g - 1, (s_base, 1))
                sp.dma_start(xwin[:, b, 0:D], x[bass.ds(w, P), :]).then_inc(s_xwin[b], 16)
                sp.dma_start(xwin[:, b, D:D + 1], od_tab[bass.ds(w, P), :]).then_inc(s_xwin[b], 16)

            def store_nodes(g, b):
                w = base_of(g)
                wait_apart(sp, s_dinv, g + 1, (s_base, 1))
                if not (known(g) and g == 0):
                    wait_apart(sp, s_x2st, 16 * g, (s_base, 1))
                sp.dma_start(x2_tab[bass.ds(w, P), :], x2[:, b, :]).then_inc(s_x2st, 16)
                wait_apart(sp, s_hs, g + 1, (s_base, 1))
                if not (known(g) and g == 0):
                    wait_apart(sp, s_hsst, 16 * g + 16, (s_base, 1))
                sp.dma_start(hs_tab[bass.ds(w, P), :], hs[:, b, :]).then_inc(s_hsst, 16)

            sp.wait_ge(s_zero, 1)
            sp.dma_start(hs_tab[N:N + 1, :], zero_row[:]).then_inc(s_hsst, 16)
            load_edges(0, 0)
            load_edges(1, 1)
            sp.wait_ge(s_od, 1)
            sp.dma_start(od_tab.rearrange("(h l) o -> h (l o)", l=LO), od_s[:]).then_inc(s_od_st, 16)
            sp.wait_ge(s_od_st, 16)
            load_nodes(0, 0)
            load_nodes(1, 1)
            with sp.Fori(1, GROUPS // 2) as n:
                for b in range(2):
                    load_edges(2 * n + b, b)
                    store_nodes(2 * n + b - 2, b)
                    load_nodes(2 * n + b, b)
            store_nodes(GROUPS - 2, 0)
            store_nodes(GROUPS - 1, 1)

            sp.wait_ge(s_x2st, 16 * GROUPS)

            def load_window(g, b):
                w = base_of(g)
                if not (known(g) and g < 2):
                    wait_apart(sp, s_y1, g - 1, (s_base, 1))
                sp.dma_start(xwin[:, b, :], x2_tab[bass.ds(w, P), :]).then_inc(s_xw1[b], 16)

            def store_out(g, b):
                w = base_of(g)
                wait_apart(sp, s_y1, g + 1, (s_base, 1))
                if not (known(g) and g == 0):
                    wait_apart(sp, s_yst, 16 * g, (s_base, 1))
                sp.dma_start(out[bass.ds(w, P), :], y_out[:, b, :]).then_inc(s_yst, 16)

            load_window(0, 0)
            load_window(1, 1)
            with sp.Fori(1, GROUPS // 2) as n:
                for b in range(2):
                    store_out(2 * n + b - 2, b)
                    load_window(2 * n + b, b)
            store_out(GROUPS - 2, 0)
            store_out(GROUPS - 1, 1)
            sp.wait_ge(s_yst, 16 * GROUPS)

        @block.gpsimd
        def _(pool):
            nc.gpsimd.memset(we4[:], 0.0).then_inc(s_pool0, 1)
            pool.wait_ge(s_reset, 2)
            for h in range(H):
                nc.gpsimd.tensor_copy(fwd_reset8[:, :, h, :], fwd_reset[:]).then_inc(s_reset8, 1)
                nc.gpsimd.tensor_copy(bwd_reset8[:, :, h, :], bwd_reset[:, :, ::-1]).then_inc(s_reset8, 1)
            pool.wait_ge(s_tab[0], 32 * 3)
            pool.wait_ge(s_tab[1], 32 * 2)

            def gather(g, b):
                wait_apart(pool, s_idx, g + 1, (s_tab[0], 32 * 3))
                for t in range(T):
                    pool.indirect_dma_start(out=kv[:, b, t, :], out_offset=None, in_=kv_tab,
                                            in_offset=bass.IndirectOffsetOnAxis(ap=idx[:, b, t:t + 1], axis=0))\
                        .then_inc(s_kv[b], 16)

            gather(0, 0)
            gather(1, 1)
            with pool.Fori(1, GROUPS // 2) as n:
                gather(2 * n, 0)
                gather(2 * n + 1, 1)

            pool.wait_ge(s_hsst, 16 * GROUPS + 16)

            def gather1(g, b):
                wait_apart(pool, s_idx1, g + 1, (s_tab[0], 32 * 3))
                if not (known(g) and g < 2):
                    wait_apart(pool, s_agg1, g - 1, (s_tab[0], 32 * 3))
                for t in range(T):
                    pool.indirect_dma_start(out=kv[:, b, t, 0:D], out_offset=None, in_=hs_tab,
                                            in_offset=bass.IndirectOffsetOnAxis(ap=idx[:, b, t:t + 1], axis=0))\
                        .then_inc(s_g1[b], 16)

            gather1(0, 0)
            gather1(1, 1)
            with pool.Fori(1, GROUPS // 2) as n:
                gather1(2 * n, 0)
                gather1(2 * n + 1, 1)

        @block.vector
        def _(dve):
            V = nc.vector
            pre = Steps(nc, dve, s_dv0, 0)

            pre.mark(V.memset(ones_row[:], 1.0))
            V.memset(zero_row[:], 0.0).then_inc(s_zero, 1)
            pre.mark(V.memset(c1[:], BIG))
            pre.mark(V.memset(c2[:], BIG))
            pre.mark(V.memset(R[:], 0.0))
            pre.mark(V.memset(wv[:], 1.0))
            dve.wait_ge(s_x, 16)
            for i in range(NT):
                pre.mark(V.bn_stats(st6[:, i, :], xt[:, i, :]))
            pre.sync()
            for i in range(NT):
                pre.mark(V.bn_aggr(mv[:, i, :], st6[:, i, :]))
            pre.sync()
            pre.then(V.tensor_scalar(ve[:], mv[:, :, 1], EPS_LN, None, ALU.add))
            rsqrt(pre, rs_a[:], ve[:], rs_t[:])
            dve.wait_ge(s_in, 16 * 19)
            pre.mark(V.tensor_scalar(wqkv_s[:, 0:D], wqkv_s[:, 0:D], DH ** -0.5, None, ALU.mult))
            pre.then(V.tensor_scalar(bqkv_s[:, 0:D], bqkv_s[:, 0:D], DH ** -0.5, None, ALU.mult))

            def norm_tile(i):
                if i >= 2:
                    dve.wait_ge(s_xnT, i - 1)
                V.tensor_scalar(xn[:, i % 2, :], xt[:, i, :], mv[:, i, 0:1], rs_a[:, i:i + 1],
                                ALU.subtract, ALU.mult).then_inc(s_xn, 1)

            def qkv_tile(i):
                c = i // PCH
                dve.wait_ge(s_qkvp, i + 1)
                if i % PCH == 0 and c >= 2:
                    dve.wait_ge(s_tab[c % 2], 32 * (c // 2))
                V.tensor_tensor(qkv[:, c % 2, i % PCH, :], ps_q[i % 2][:, 0:3 * D], bqkv_s[:],
                                ALU.add).then_inc(s_qkv, 1)

            norm_tile(0)
            for i in range(NT):
                if i + 1 < NT:
                    norm_tile(i + 1)
                qkv_tile(i)

            GT3 = [P, GROUPS, T]
            pre.then(V.tensor_copy(first_f[:], first_i[:]))
            pre.then(V.tensor_scalar(base_f[:], first_f[:], float(N - P), None, ALU.min))
            V.tensor_copy(base_i[:], base_f[:]).then_inc(s_base, 1)
            pre.mark(V.memset(delta[:, 0:1], 0.0))
            pre.mark(V.tensor_tensor(delta[:, 1:], base_f[:, 1:], base_f[:, :-1], ALU.subtract))
            pre.mark(V.tensor_tensor(ofirst[:], first_f[:], base_f[:], ALU.subtract))
            pre.mark(V.tensor_tensor(dloc[:], dst_i[:], base_f[:].unsqueeze(2).to_broadcast(GT3), ALU.subtract))
            pre.mark(V.tensor_tensor(part_reset[:, 0, :], dst_i[:, :, T - 1], before_i[:], ALU.not_equal))
            pre.mark(V.tensor_tensor(part_reset[:, 1, :], dst_i[:, :, 0], after_i[:], ALU.not_equal))
            pre.mark(V.tensor_tensor(fwd_reset[:, :, 1:], dst_i[:, :, 1:], dst_i[:, :, :-1], ALU.not_equal))
            pre.mark(V.memset(fwd_reset[:, :, 0:1], 1.0))
            pre.mark(V.tensor_tensor(bwd_reset[:, :, :-1], dst_i[:, :, 1:], dst_i[:, :, :-1], ALU.not_equal))
            pre.mark(V.memset(bwd_reset[:, :, T - 1:T], 1.0))
            pre.mark(V.tensor_tensor(fwd_mask[:], dst_i[:], before_i[:].unsqueeze(2).to_broadcast(GT3), ALU.not_equal))
            pre.then(V.tensor_tensor(bwd_mask[:], dst_i[:], after_i[:].unsqueeze(2).to_broadcast(GT3), ALU.not_equal))
            V.tensor_scalar(part_reset[:], part_reset[:], BIG, None, ALU.mult).then_inc(s_part, 1)
            V.tensor_scalar(fwd_reset[:], fwd_reset[:], BIG, None, ALU.mult).then_inc(s_reset, 1)
            V.tensor_scalar(bwd_reset[:], bwd_reset[:], BIG, None, ALU.mult).then_inc(s_reset, 1)
            pre.mark(V.tensor_scalar(fwd_mask[:], fwd_mask[:], BIG, None, ALU.mult))
            pre.then(V.tensor_scalar(bwd_mask[:], bwd_mask[:], BIG, None, ALU.mult))

            def set_idx(g, b, ready):
                V.tensor_copy(idx[:, b, :], src_i[:, g, :] if known(g) else
                              src_i[:, bass.ds(g, 1), :].rearrange("p g t -> p (g t)")).then_inc(ready, 1)

            set_idx(0, 0, s_idx)
            set_idx(1, 1, s_idx)

            def col(tile, g):
                return tile[:, g:g + 1] if known(g) else tile[:, bass.ds(g, 1)]

            def col3(tile, g):
                return (tile[:, g:g + 1, :] if known(g) else tile[:, bass.ds(g, 1), :]).rearrange("p g t -> p (g t)")

            def one_hots(g, b, used, ready):
                if not (known(g) and g < 2):
                    dve.wait_ge(used, g - 1)
                V.tensor_scalar(shift[:, b, :], imj[:], col(delta, g), None, ALU.is_equal).then_inc(ready, 1)
                V.tensor_tensor(S[:, b], col3(dloc, g).unsqueeze(2).to_broadcast([P, T, P]),
                                iota[:].unsqueeze(1).to_broadcast([P, T, P]), ALU.is_equal).then_inc(ready, 1)

            one_hots(0, 0, None, s_S)
            dve.wait_ge(s_partT, 1)
            V.tensor_copy(part_rows[0:GROUPS, :], ps_b[0:GROUPS, 0:P]).then_inc(s_partrow, 1)
            V.tensor_copy(part_rows[GROUPS:, :], ps_b[GROUPS:2 * GROUPS, 0:P][:, ::-1]).then_inc(s_partrow, 1)
            pre.mark(V.tensor_copy(iota_b[:], iota[:, 0:LO]))
            pre.then(V.tensor_scalar(part_i, src_i[:], 6, None, ALU.logical_shift_right))
            pre.then(V.tensor_copy(hi_f[:], part_i))
            pre.then(V.tensor_scalar(part_i, src_i[:], LO - 1, None, ALU.bitwise_and))
            pre.then(V.tensor_copy(lo_f[:], part_i))
            for k in range(HTURNS):
                for oh, part, m in ((oh_hi, hi_f, HI), (oh_lo, lo_f, LO)):
                    if k >= 2:
                        dve.wait_ge(s_hist, k - 1)
                    V.tensor_tensor(oh[:, k % 2], part[:].rearrange("p g t -> p (g t)")[:, HC * k:HC * k + HC]
                                    .unsqueeze(2).to_broadcast([P, HC, m]),
                                    iota_b[:, 0:m].unsqueeze(1).to_broadcast([P, HC, m]), ALU.is_equal).then_inc(s_oh, 1)
            dve.wait_ge(s_hist, HTURNS)
            V.tensor_copy(od_s[:], ps_r[0:HI, 0:LO]).then_inc(s_od, 1)
            dve.wait_ge(s_reset8, 2 * H)
            dve.wait_ge(s_line, 16)

            def flat(tile):
                return tile[:].rearrange("p h t -> p (h t)")

            def reset8(tile, g):
                return (tile[:, g:g + 1] if known(g) else tile[:, bass.ds(g, 1)]).rearrange("p g h t -> p (g h t)")

            def lines(g):
                return (line[:, g:g + 1, :] if known(g) else line[:, bass.ds(g, 1), :]).rearrange("p g t -> p (g t)")

            def mask8(tile, g):
                return col3(tile, g).unsqueeze(1).to_broadcast([P, H, T])

            def scores(g, b, st):
                n = (g - b) // 2 if known(g) else None
                dve.wait_ge(s_kv[b], 16 * T * (n + 1) if known(g) else (g + (2 - b)) * (8 * T))
                for c, (t0, t1) in enumerate(CH):
                    w = t1 - t0
                    dve.wait_ge(s_qt, NCH * g + c + 1)
                    V.tensor_tensor(prod[:, c % 2, 0:w, :], kv[:, b, t0:t1, 0:D],
                                    ps_q[c % 2][:, 0:w * D].rearrange("p (t d) -> p t d", d=D), ALU.mult).then_inc(s_prod, 1)
                    dve.wait_ge(s_prod, NCH * g + c + 1)
                    st.mark(V.tensor_reduce(sc[:, :, t0:t1].rearrange("p h t -> p t h"),
                                            prod[:, c % 2, 0:w, :].rearrange("p t (h d) -> p t h d", d=DH),
                                            AX_X, ALU.add))
                st.sync()
                dve.wait_ge(s_bias, g + 1)
                V.tensor_tensor(sc[:], sc[:], p_bias.rearrange("p (t h) -> p h t", h=H), ALU.add).then_inc(s_sc, 1)
                dve.wait_ge(s_sc, g + 1)
                V.tensor_tensor_scan(out=flat(f1), data0=reset8(fwd_reset8, g), data1=flat(sc), initial=BIG,
                                     op0=ALU.add, op1=ALU.max).then_inc(s_v1, 1)

            def scan_partitions(g, b, st):
                dve.wait_ge(s_v1T, g + 1)
                if not (known(g) and g < 2):
                    dve.wait_ge(s_cfT, g - 1)
                st.mark(V.tensor_copy(c1[:, b, 0:1], c1[:, 1 - b, P:P + 1]))
                V.tensor_tensor_scan(out=c1[:, b, 1:P + 1], data0=lines(g), data1=p_v1, initial=c1[:, 1 - b, P:P + 1],
                                     op0=ALU.add, op1=ALU.max).then_inc(s_cf, 1)

            def backward(g, b, st):
                dve.wait_ge(s_cfT, g + 1)
                st.then(V.tensor_tensor(tmp8[:], mask8(fwd_mask, g), p_c1.unsqueeze(2).to_broadcast([P, H, T]), ALU.add))
                st.then(V.tensor_tensor(f2[:], f1[:], tmp8[:], ALU.max))
                V.tensor_tensor_scan(out=flat(bx)[:, ::-1], data0=reset8(bwd_reset8, g), data1=flat(f2)[:, ::-1],
                                     initial=BIG, op0=ALU.add, op1=ALU.max).then_inc(s_v2, 1)

            def scan_partitions_back(g, b, st):
                dve.wait_ge(s_v2T, g + 1)
                V.tensor_tensor_scan(out=c2[:, 0:P][:, ::-1], data0=lines(g + GROUPS), data1=p_v2[:, ::-1],
                                     initial=BIG, op0=ALU.add, op1=ALU.max).then_inc(s_cb, 1)
                dve.wait_ge(s_cb, g + 1)
                st.then(V.tensor_tensor(dfac[:], c1[:, b, 0:1], c2[:, 0:1], ALU.subtract))
                V.tensor_scalar(dfac[:], dfac[:], 0.0, None, ALU.min).then_inc(s_dfac, 1)

            def shifted(g, b, st):
                dve.wait_ge(s_cbT, g + 1)
                st.then(V.tensor_tensor(tmp8[:], mask8(bwd_mask, g), p_c2.unsqueeze(2).to_broadcast([P, H, T]), ALU.add))
                st.then(V.tensor_tensor(tmp8[:], bx[:], tmp8[:], ALU.max))
                V.tensor_tensor(z[:], sc[:], tmp8[:], ALU.subtract).then_inc(s_z, 1)
                if not (known(g) and g == 0):
                    dve.wait_ge(s_rc, g)
                st.mark(V.tensor_scalar(isf[:], iota[0:H, :], col(ofirst[0:H], g), None, ALU.is_equal))
                dve.wait_ge(s_fac, g + 1)
                V.scalar_tensor_tensor(out=facd[:], in0=ident[0:H, 0:H], scalar=fac[:], in1=ident[0:H, 0:H],
                                       op0=ALU.mult, op1=ALU.subtract).then_inc(s_facd, 1)

            def weigh(g, b):
                dve.wait_ge(s_p, g + 1)
                w4 = wv[:, :, 0:C].rearrange("p t (h e) -> p t h e", e=DH + 1)
                V.tensor_tensor(w4[:, :, :, 0:DH], kv[:, b, :, D:2 * D].rearrange("p t (h d) -> p t h d", d=DH),
                                w4[:, :, :, DH:DH + 1].to_broadcast([P, T, H, DH]), ALU.mult).then_inc(s_wv, 1)
                dve.wait_ge(s_wv, g + 1)

            def combine(g, b, st):
                dve.wait_ge(s_rc, g + 1)
                st.mark(V.tensor_scalar(fb[:], p_fb, 1.0, None, ALU.add))
                st.then(V.tensor_copy(R[:, b, C:C + 1], p_rc[:, C:C + 1]))
                st.then(V.tensor_tensor(R[:, b, 0:C].rearrange("p (h e) -> p h e", h=H),
                                        p_rc[:, 0:C].rearrange("p (h e) -> p h e", h=H),
                                        fb[:].unsqueeze(2).to_broadcast([P, H, DH + 1]), ALU.mult))
                V.tensor_tensor(R[:, b, :], R[:, b, :], ps_r[:, 0:C + 1], ALU.add).then_inc(s_R, 1)
                dve.wait_ge(s_R, g + 1)
                r3 = R[:, b, 0:C].rearrange("p (h e) -> p h e", h=H)
                st.then(V.tensor_scalar(rden[:].unsqueeze(2), r3[:, :, DH:DH + 1], 1e-10, None, ALU.add))
                st.then(V.reciprocal(rden[:], rden[:]))
                V.tensor_tensor(agn[:].rearrange("p (h d) -> p h d", h=H), r3[:, :, 0:DH],
                                rden[:].unsqueeze(2).to_broadcast([P, H, DH]), ALU.mult).then_inc(s_agn, 1)

            def renorm(g, b, st):
                dve.wait_ge(s_o, g + 1)
                dve.wait_ge(s_xwin[b], 32 * ((g - b) // 2 + 1) if known(g) else (g + (2 - b)) * 16)
                if not (known(g) and g < 2):
                    dve.wait_ge(s_x2st, 16 * (g - 1))
                V.tensor_tensor(x2[:, b, 0:D], ps_f[:, D:2 * D], xwin[:, b, 0:D], ALU.add).then_inc(s_x2, 1)
                dve.wait_ge(s_x2, g + 1)
                st.mark(V.bn_stats(bst[:], x2[:, b, 0:D]))
                wait_apart(dve, s_dB, st.base + st.k, (s_x, 16))
                st.then(V.bn_aggr(bmv[:], bst[:]))
                st.mark(V.tensor_scalar(v2[:, 0:1], bmv[:, 1:2], EPS_LN, None, ALU.add))
                st.then(V.tensor_tensor(v2[:, 1:2], R[:, b, C:C + 1], xwin[:, b, D:D + 1], ALU.add))
                st.then(V.tensor_scalar(v2[:, 1:2], v2[:, 1:2], 1.0, None, ALU.max))
                rsqrt(st, y2[:], v2[:], t2[:])
                V.tensor_scalar(xn2[:], x2[:, b, 0:D], bmv[:, 0:1], y2[:, 0:1], ALU.subtract, ALU.mult).then_inc(s_xn2, 1)
                V.tensor_copy(x2[:, b, D:D + 1], y2[:, 1:2]).then_inc(s_dinv, 1)

            s_ = [sm[:, i:i + 1] for i in range(8)]
            v_, y_, t_, nc_, q_, ser, at_, a_ = s_

            def log_map(g, b, st):
                dve.wait_ge(s_ss, g + 1)
                st.then(V.tensor_scalar(v_, ss[:], 1e-30, None, ALU.max))
                rsqrt(st, y_, v_, t_)
                st.then(V.tensor_scalar(t_, ss[:], y_, 1e-15, ALU.mult, ALU.max))
                st.then(V.tensor_scalar(nc_, t_, ATANH_MAX, None, ALU.min))
                st.mark(V.tensor_tensor(q_, nc_, nc_, ALU.mult))
                st.then(V.tensor_scalar(t_, nc_, -1.0, 1.0, ALU.mult, ALU.add))
                st.mark(V.tensor_scalar(ser, q_, 1.0 / 9, 1.0 / 7, ALU.mult, ALU.add))
                st.then(V.reciprocal(t_, t_))
                V.scalar_tensor_tensor(out=rat[:], in0=nc_, scalar=2.0, in1=t_, op0=ALU.mult, op1=ALU.mult).then_inc(s_nc, 1)
                st.then(V.tensor_scalar(ser, ser, q_, 1.0 / 5, ALU.mult, ALU.add))
                st.then(V.tensor_scalar(ser, ser, q_, 1.0 / 3, ALU.mult, ALU.add))
                st.then(V.tensor_scalar(ser, ser, q_, 1.0, ALU.mult, ALU.add))
                st.then(V.tensor_tensor(ser, ser, nc_, ALU.mult))

            def tangent(g, b, st):
                dve.wait_ge(s_ln, g + 1)
                st.then(V.scalar_tensor_tensor(out=t_, in0=lnv[:], scalar=-0.5, in1=ser, op0=ALU.mult, op1=ALU.add))
                st.then(V.scalar_tensor_tensor(out=t_, in0=nc_, scalar=SERIES_BELOW, in1=t_, op0=ALU.is_lt, op1=ALU.mult))
                st.then(V.scalar_tensor_tensor(out=at_, in0=lnv[:], scalar=0.5, in1=t_, op0=ALU.mult, op1=ALU.add))
                st.then(V.tensor_scalar(a_, at_, y_, y2[:, 1:2], ALU.mult, ALU.mult))
                dve.wait_ge(s_h1, g + 1)
                dve.wait_ge(s_b1d, g + 1)
                if not (known(g) and g < 2):
                    dve.wait_ge(s_hsst, 16 * g)
                V.scalar_tensor_tensor(out=hs[:, b, :], in0=ps_f[:, 3 * D:4 * D], scalar=a_, in1=b1d[:],
                                       op0=ALU.mult, op1=ALU.add).then_inc(s_hs, 1)

            def step(g, b, edges=True, nodes=True, more=True, far=True):
                A = Steps(nc, dve, s_dA, NA * g)
                B = Steps(nc, dve, s_dB, NB * (g - 1))
                if edges:
                    scores(g, b, A)
                if nodes:
                    combine(g - 1, 1 - b, B)
                if edges:
                    scan_partitions(g, b, A)
                    if more:
                        one_hots(g + 1, 1 - b, s_rc, s_S)
                if nodes:
                    renorm(g - 1, 1 - b, B)
                if edges:
                    backward(g, b, A)
                if nodes:
                    log_map(g - 1, 1 - b, B)
                if edges:
                    scan_partitions_back(g, b, A)
                if nodes:
                    tangent(g - 1, 1 - b, B)
                if edges:
                    shifted(g, b, A)
                    weigh(g, b)
                    if far:
                        set_idx(g + 2, b, s_idx)
                    A.check(NA)
                if nodes:
                    B.check(NB)

            step(0, 0, nodes=False)
            step(1, 1)
            with dve.Fori(1, GROUPS // 2 - 1) as n:
                step(2 * n, 0)
                step(2 * n + 1, 1)
            step(GROUPS - 2, 0, far=False)
            step(GROUPS - 1, 1, more=False, far=False)
            step(GROUPS, 0, edges=False)

            set_idx(0, 0, s_idx1)
            set_idx(1, 1, s_idx1)
            V.memset(R[:, 1, :], 0.0).then_inc(s_R1, 1)
            one_hots(0, 0, None, s_S1)
            one_hots(1, 1, None, s_S1)

            def out_rows(g, b, more=True):
                st = Steps(nc, dve, s_d1, N1 * g)
                dve.wait_ge(s_agg1, g + 1)
                V.tensor_copy(R[:, b, 0:D], [ps_r, ps_c][b][:, 0:D]).then_inc(s_R1, 1)
                dve.wait_ge(s_R1, g + 2)
                dve.wait_ge(s_xw1[b], 16 * ((g - b) // 2 + 1) if known(g) else (g + (2 - b)) * 8)
                V.tensor_scalar(agn[:], R[:, b, 0:D], xwin[:, b, D:D + 1], None, ALU.mult).then_inc(s_zz1, 1)
                if more:
                    one_hots(g + 2, b, s_agg1, s_S1)
                    dve.wait_ge(s_g1[b], 16 * T * ((g - b) // 2 + 1) if known(g) else (g + (2 - b)) * (8 * T))
                    set_idx(g + 2, b, s_idx1)
                dve.wait_ge(s_ss1, g + 1)
                st.then(V.tensor_scalar(v_, ss[:], 1e-30, None, ALU.max))
                rsqrt(st, y_, v_, t_)
                V.tensor_tensor(nrm[:], ss[:], y_, ALU.mult).then_inc(s_norm1, 1)
                dve.wait_ge(s_th1, g + 1)
                st.then(V.tensor_scalar(a_, y_, 1e15, th[:], ALU.min, ALU.mult))
                if not (known(g) and g < 2):
                    dve.wait_ge(s_yst, 16 * (g - 1))
                V.scalar_tensor_tensor(out=y_out[:, b, :], in0=agn[:], scalar=a_, in1=xwin[:, b, 0:D],
                                       op0=ALU.mult, op1=ALU.add).then_inc(s_y1, 1)
                st.check(N1)

            out_rows(0, 0)
            out_rows(1, 1)
            with dve.Fori(1, GROUPS // 2 - 1) as n:
                out_rows(2 * n, 0)
                out_rows(2 * n + 1, 1)
            out_rows(GROUPS - 2, 0, more=False)
            out_rows(GROUPS - 1, 1, more=False)

        @block.scalar
        def _(act):
            A = nc.scalar
            for i in range(NT):
                act.wait_ge(s_xnT, i + 1)
                if i >= 2:
                    act.wait_ge(s_qkvp, i - 1)
                A.activation(hT[:, i % 2, :], ps_s[i % 2][:, 0:D], ACT.Relu).then_inc(s_hT, 1)
            act.wait_ge(s_in, 16 * 19)
            for t in range(T):
                A.copy(be_r[:, t, :], be_s[:]).then_inc(s_ber, 1)

            def turn_copies(g, b):
                if not (known(g) and g < 2):
                    act.wait_ge(s_qt, NCH * (g - 1))
                for c, (t0, t1) in enumerate(CH):
                    w = (t1 - t0) * P
                    act.wait_ge(s_stp, NCH * g + c + 1)
                    A.copy(ST[:, b, t0:t1, :].rearrange("p t e -> p (t e)"), ps_s[c % 2][:, 0:w]).then_inc(s_st, 1)

            def node_part(g, b):
                act.wait_ge(s_agTp, g + 1)
                A.copy(agT[:], ps_f[:, 0:D]).then_inc(s_agT, 1)
                act.wait_ge(s_xn2, g + 1)
                A.activation(hsq[:], xn2[:], ACT.Relu).then_inc(s_aB, 1)
                act.wait_ge(s_aB, g + 1)
                act.wait_ge(s_xn2T, g + 1)
                A.activation(h2T[:], ps_f[:, 2 * D:3 * D], ACT.Relu).then_inc(s_h2T, 1)
                A.activation(hsr[:], hsq[:], ACT.Square, accum_out=ss[:]).then_inc(s_ss, 1)
                act.wait_ge(s_dinv, g + 1)
                if not (known(g) and g == 0):
                    act.wait_ge(s_hs, g)
                A.activation(b1d[:], b1_s[:], ACT.Copy, scale=y2[:, 1:2]).then_inc(s_b1d, 1)
                act.wait_ge(s_nc, g + 1)
                A.activation(lnv[:], rat[:], ACT.Ln, bias=1.0).then_inc(s_ln, 1)

            def edge_part(g, b):
                act.wait_ge(s_dfac, g + 1)
                A.activation(fac[:], dfac[:], ACT.Exp).then_inc(s_fac, 1)
                act.wait_ge(s_z, g + 1)
                if not (known(g) and g == 0):
                    act.wait_ge(s_agg, g)
                A.activation(wv[:, :, 0:C].rearrange("p t (h e) -> p h t e", e=DH + 1)[:, :, :, DH], z[:], ACT.Exp)\
                    .then_inc(s_p, 1)

            turn_copies(0, 0)
            edge_part(0, 0)
            turn_copies(1, 1)
            node_part(0, 0)
            edge_part(1, 1)
            turn_copies(2, 0)
            with act.Fori(1, GROUPS // 2 - 1) as n:
                node_part(2 * n - 1, 1)
                edge_part(2 * n, 0)
                turn_copies(2 * n + 1, 1)
                node_part(2 * n, 0)
                edge_part(2 * n + 1, 1)
                turn_copies(2 * n + 2, 0)
            node_part(GROUPS - 3, 1)
            edge_part(GROUPS - 2, 0)
            turn_copies(GROUPS - 1, 1)
            node_part(GROUPS - 2, 0)
            edge_part(GROUPS - 1, 1)
            node_part(GROUPS - 1, 1)

            def norm_part(g):
                act.wait_ge(s_zz1, g + 1)
                A.activation(hsq[:], agn[:], ACT.Square, accum_out=ss[:]).then_inc(s_ss1, 1)
                act.wait_ge(s_norm1, g + 1)
                A.activation(th[:], nrm[:], ACT.Tanh).then_inc(s_th1, 1)

            norm_part(0)
            norm_part(1)
            with act.Fori(1, GROUPS // 2) as n:
                norm_part(2 * n)
                norm_part(2 * n + 1)

        @block.tensor
        def _(pe):
            M = nc.tensor
            pe.wait_ge(s_in, 16 * 19)

            def turn_tile(i):
                pe.wait_ge(s_xn, i + 1)
                if i >= 2:
                    pe.wait_ge(s_hT, i - 1)
                M.transpose(ps_s[i % 2][:, 0:D], xn[:, i % 2, :], ident[:]).then_inc(s_xnT, 1)

            turn_tile(0)
            for i in range(NT):
                if i + 1 < NT:
                    turn_tile(i + 1)
                pe.wait_ge(s_hT, i + 1)
                if i >= 2:
                    pe.wait_ge(s_qkv, i - 1)
                M.matmul(ps_q[i % 2][:, 0:3 * D], hT[:, i % 2, :], wqkv_s[:], start=True, stop=True).then_inc(s_qkvp, 1)
            pe.wait_ge(s_part, 1)
            M.transpose(ps_b[0:2 * GROUPS, 0:P], part_reset[:].rearrange("p k g -> p (k g)"), ident[:]).then_inc(s_partT, 1)

            def turn(g, b):
                pe.wait_ge(s_S, 2 * g + 2)
                for c, (t0, t1) in enumerate(CH):
                    if not (known(g) and g == 0 and c < 2):
                        pe.wait_ge(s_st, NCH * g + c - 1)
                    for t in range(t0, t1):
                        mm = M.transpose(ps_s[c % 2][:, (t - t0) * P:(t - t0 + 1) * P], S[:, b, t, :], ident[:])
                    mm.then_inc(s_stp, 1)

            def bias(g, b):
                pe.wait_ge(s_attr[b], 32 * ((g - b) // 2 + 1) if known(g) else (g + (2 - b)) * 16)
                if not (known(g) and g == 0):
                    pe.wait_ge(s_sc, g)
                for k in range(4):
                    r, w = (P, 4 * H) if k < 3 else (EF, H)
                    part = slice(4 * H * k, 4 * H * k + w)
                    M.matmul(p_bias[:, part], ones_row[:], be_r[:].rearrange("p t h -> p (t h)")[:, part],
                             start=True, stop=False)
                    mm = M.matmul(p_bias[:, part], attr_s[0:r, b, k, :], we4[0:r, 0:w], start=False, stop=True)
                mm.then_inc(s_bias, 1)

            def query(g, b, chunks):
                if 0 in chunks:
                    pe.wait_ge(s_qwin[b], 16 * ((g - b) // 2 + 1) if known(g) else (g + (2 - b)) * 8)
                for c in chunks:
                    t0, t1 = CH[c]
                    pe.wait_ge(s_st, NCH * g + c + 1)
                    if not (known(g) and g == 0 and c < 2):
                        pe.wait_ge(s_prod, NCH * g + c - 1)
                    for t in range(t0, t1):
                        mm = M.matmul(ps_q[c % 2][:, (t - t0) * D:(t - t0 + 1) * D], ST[:, b, t, :], qwin[:, b, :],
                                      start=True, stop=True)
                    mm.then_inc(s_qt, 1)

            def step(g, b, edges=True, nodes=True, more=True):
                if edges:
                    bias(g, b)
                    query(g, b, (2, 3))
                    pe.wait_ge(s_v1, g + 1)
                    M.transpose(p_v1, f1[:, :, T - 1], ident[:]).then_inc(s_v1T, 1)
                if nodes:
                    pe.wait_ge(s_agn, g)
                    M.transpose(ps_f[:, 0:D], agn[:], ident[:]).then_inc(s_agTp, 1)
                if edges:
                    wait_apart(pe, s_cf, g + 1, (s_part, 1))
                    M.transpose(p_c1, c1[:, b, 0:P], ident[0:H, 0:H]).then_inc(s_cfT, 1)
                if nodes:
                    pe.wait_ge(s_agT, g)
                    M.matmul(ps_f[:, D:2 * D], ones_row[:], bo_s[:], start=True, stop=False)
                    M.matmul(ps_f[:, D:2 * D], agT[:], wo_s[:], start=False, stop=True).then_inc(s_o, 1)
                    pe.wait_ge(s_xn2, g)
                    M.transpose(ps_f[:, 2 * D:3 * D], xn2[:], ident[:]).then_inc(s_xn2T, 1)
                if edges:
                    pe.wait_ge(s_v2, g + 1)
                    M.transpose(p_v2, bx[:, :, 0], ident[:]).then_inc(s_v2T, 1)
                if nodes:
                    pe.wait_ge(s_h2T, g)
                    M.matmul(ps_f[:, 3 * D:4 * D], h2T[:], w1_s[:], start=True, stop=True).then_inc(s_h1, 1)
                if edges:
                    wait_apart(pe, s_cb, g + 1, (s_part, 1))
                    M.transpose(p_c2, c2[:, 1:P + 1], ident[0:H, 0:H]).then_inc(s_cbT, 1)
                    if more:
                        turn(g + 1, 1 - b)
                        query(g + 1, 1 - b, (0, 1))
                    pe.wait_ge(s_wv, g + 1)
                    for t in range(T):
                        mm = M.matmul(ps_r[:, 0:C + 1], S[:, b, t, :], wv[:, t, :], start=(t == 0), stop=(t == T - 1))
                    mm.then_inc(s_agg, 1)
                    M.matmul(p_rc, shift[:, b, :], R[:, 1 - b, :], start=True, stop=True)
                    pe.wait_ge(s_facd, g + 1)
                    M.matmul(p_fb, isf[:], facd[:], start=True, stop=True).then_inc(s_rc, 1)

            for k in range(HTURNS):
                pe.wait_ge(s_oh, 2 * k + 2)
                for c in range(HC):
                    mm = M.matmul(ps_r[0:HI, 0:LO], oh_hi[:, k % 2, c, :], oh_lo[:, k % 2, c, :],
                                  start=(k == 0 and c == 0), stop=(k == HTURNS - 1 and c == HC - 1))
                mm.then_inc(s_hist, 1)
            pe.wait_ge(s_od, 1)
            pe.wait_ge(s_ber, T)
            turn(0, 0)
            query(0, 0, (0, 1))
            step(0, 0, nodes=False)
            step(1, 1)
            with pe.Fori(1, GROUPS // 2 - 1) as n:
                step(2 * n, 0)
                step(2 * n + 1, 1)
            step(GROUPS - 2, 0)
            step(GROUPS - 1, 1, more=False)
            step(GROUPS, 0, edges=False)

            def sums(g, b):
                pe.wait_ge(s_S1, 2 * g + 2)
                pe.wait_ge(s_g1[b], 16 * T * ((g - b) // 2 + 1) if known(g) else (g + (2 - b)) * (8 * T))
                bank = [ps_r, ps_c][b]
                for t in range(T):
                    M.matmul(bank[:, 0:D], S[:, b, t, :], kv[:, b, t, 0:D], start=(t == 0), stop=False)
                pe.wait_ge(s_R1, g + 1)
                M.matmul(bank[:, 0:D], shift[:, b, :], R[:, 1 - b, 0:D], start=False, stop=True).then_inc(s_agg1, 1)

            sums(0, 0)
            sums(1, 1)
            with pe.Fori(1, GROUPS // 2) as n:
                sums(2 * n, 0)
                sums(2 * n + 1, 1)


def kernel(**inputs):
    import concourse.bacc as _bacc
    from concourse.bass_utils import run_bass_kernel_spmd as _run

    a = {k: np.ascontiguousarray(v) for k, v in inputs.items()}

    def filled(v, rows, value=0):
        full = np.full((rows,) + v.shape[1:], value, v.dtype)
        full[:len(v)] = v
        return full

    def lanes(v):
        return v.reshape(GROUPS, P, T).transpose(1, 0, 2)

    src = filled(a["src"], GROUPS * GE, N)
    dst = filled(a["dst"], GROUPS * GE, N)
    runs = dst.reshape(GROUPS * P, T)
    before = np.concatenate([np.full(1, -1, np.int32), runs[:-1, T - 1]]).reshape(GROUPS, P).T
    after = np.concatenate([runs[1:, 0], np.full(1, -1, np.int32)]).reshape(GROUPS, P).T
    attr = filled(a["edge_attr_32"], GROUPS * GE).reshape(GROUPS, P, T * EF).transpose(0, 2, 1)
    rows, cols = np.indices((P, P)).astype(np.float32)
    ins = {
        "x": filled(a["x"], NPAD),
        "src_t": lanes(src).reshape(P, GROUPS * T),
        "dst_t": lanes(dst).reshape(P, GROUPS * T),
        "dst_before": before, "dst_after": after,
        "dst_first": dst[::GE][None, :],
        "attr": attr,
        "wqkv": np.concatenate([a["L0_gnn_Wq"], a["L0_gnn_Wk"], a["L0_gnn_Wv"]], axis=1),
        "bqkv": np.concatenate([a["L0_gnn_bq"], a["L0_gnn_bk"], a["L0_gnn_bv"]])[None, :],
        "we": a["L0_gnn_We"], "be": a["L0_gnn_be"][None, :],
        "wo": a["L0_gnn_Wo"], "bo": a["L0_gnn_bo"][None, :],
        "w1t": a["L1_gnn_W"].T, "b1": a["L1_gnn_b"][None, :],
        "ident_in": np.eye(P, dtype=np.float32), "iota_in": cols, "imj_in": rows - cols,
    }
    ins = {k: np.ascontiguousarray(v) for k, v in ins.items()}
    nc = _bacc.Bacc("TRN2", target_bir_lowering=False, num_devices=1)
    aps = {k: nc.dram_tensor(f"in_{k}", v.shape, mybir.dt.from_np(v.dtype), kind="ExternalInput").ap()
           for k, v in ins.items()}
    out = nc.dram_tensor("out", (N, D), F32, kind="ExternalOutput").ap()
    build(nc, out=out, **aps)
    r = _run(nc, [{f"in_{k}": v for k, v in ins.items()}], core_ids=[0])
    return r.results[0]["out"]
```

```python
from contextlib import ExitStack

import numpy as np

import concourse.bass as bass
from concourse import mybir

F32 = mybir.dt.float32
BF16 = mybir.dt.bfloat16
I32 = mybir.dt.int32
ALU = mybir.AluOpType
ACT = mybir.ActivationFunctionType
AX_X = mybir.AxisListType.X

P = 128
N = 3125
NT = 25
NPAD = NT * P
E = 53125
T = 13
GE = P * T
GROUPS = -(-E // GE)
H = 8
DH = 16
D = 128
EF = 32
C = H * (DH + 1)
HT = H * T
BIG = -1.0e30
EPS_LN = 1e-5
ATANH_MAX = 1.0 - 1e-5
SERIES_BELOW = 0.125
HI, LO = 50, 64
PCH = 5
CH = [(0, 4), (4, 8), (8, 12), (12, 13)]
NCH = len(CH)
TA = CH[2][1]


class Steps:

    def __init__(self, nc, eng, sem, base):
        self.nc, self.eng, self.sem, self.base, self.k = nc, eng, sem, base, 0

    def mark(self, ins):
        self.k += 1
        ins.then_inc(self.sem, 1)

    def sync(self):
        self.eng.wait_ge(self.sem, self.base + self.k)

    def then(self, ins):
        self.mark(ins)
        self.eng.wait_ge(self.sem, self.base + self.k)

    def check(self, total):
        assert self.k == total, (self.k, total)


def wait_apart(eng, sem, value, passed):
    if not isinstance(value, int):
        value = eng.to_reg(value)
    eng.wait_ge(*passed)
    eng.wait_ge(sem, value)


NA = 11
NB = 5
N1 = 13


def rsqrt(link, y, v, t):
    nc_v = link.nc.vector
    link.then(nc_v.tensor_scalar(y.bitcast(I32), v.bitcast(I32), 1, None, ALU.logical_shift_right))
    link.then(nc_v.tensor_scalar(y.bitcast(I32), y.bitcast(I32), -1.0, float(0x5F3759DF), ALU.mult, ALU.add))
    for _ in range(3):
        link.then(nc_v.tensor_tensor(t, y, y, ALU.mult))
        link.then(nc_v.scalar_tensor_tensor(out=t, in0=t, scalar=-0.5, in1=v, op0=ALU.mult, op1=ALU.mult))
        link.then(nc_v.scalar_tensor_tensor(out=y, in0=t, scalar=1.5, in1=y, op0=ALU.add, op1=ALU.mult))


def build(nc, x, src_t, dst_t, dst_before, dst_after, dst_first, attr, wqkv, bqkv, we, be, wo, bo, w1t, b1,
          ident_in, iota_in, imj_in, out):
    q_tab = nc.dram_tensor("q_tab", (NPAD, D), F32, kind="Internal").ap()
    kv_tab = nc.dram_tensor("kv_tab", (NPAD, 2 * D), F32, kind="Internal").ap()
    x2_tab = nc.dram_tensor("x2_tab", (NPAD, D + 1), F32, kind="Internal").ap()
    hs_tab = nc.dram_tensor("hs_tab", (NPAD, D), F32, kind="Internal").ap()
    dinv_tab = nc.dram_tensor("dinv_tab", (NPAD, 1), F32, kind="Internal").ap()
    od_tab = nc.dram_tensor("od_tab", (NPAD, 1), F32, kind="Internal").ap()
    line_tab = nc.dram_tensor("line_tab", (2 * GROUPS, P), F32, kind="Internal").ap()

    with ExitStack() as ctx:
        def sb(name, shape, dt=F32):
            return ctx.enter_context(nc.sbuf_tensor(name, shape, dt))

        def pb(name, shape, dt=F32):
            return ctx.enter_context(nc.psum_tensor(name, shape, dt))

        def sem(name):
            return ctx.enter_context(nc.semaphore(name))

        ident = sb("ident", [P, P])
        iota = sb("iota", [P, P])
        imj = sb("imj", [P, P])
        iota_b = sb("iota_b", [P, LO], BF16)
        ones_row = sb("ones_row", [1, P])
        zero_rows = sb("zero_rows", [NPAD - N, D + 1])
        wqkv_s = sb("wqkv_s", [P, 3 * D])
        bqkv_s = sb("bqkv_s", [P, 3 * D])
        we4 = sb("we4", [P, 4 * H])
        be_r = sb("be_r", [1, T, H])
        be_s = sb("be_s", [1, H])
        wo_s = sb("wo_s", [P, D])
        bo_s = sb("bo_s", [1, D])
        w1_s = sb("w1_s", [P, D])
        b1_s = sb("b1_s", [P, D])
        dst_i = sb("dst_i", [P, GROUPS, T], I32)
        src_i = sb("src_i", [P, GROUPS, T], I32)
        before_i = sb("before_i", [P, GROUPS], I32)
        after_i = sb("after_i", [P, GROUPS], I32)
        first_i = sb("first_i", [P, GROUPS], I32)
        first_f = sb("first_f", [P, GROUPS])
        base_f = sb("base_f", [P, GROUPS])
        base_i = sb("base_i", [P, GROUPS], I32)
        delta = sb("delta", [P, GROUPS])
        ofirst = sb("ofirst", [P, GROUPS])
        dloc = sb("dloc", [P, GROUPS, T])
        fwd_reset = sb("fwd_reset", [P, GROUPS, T])
        bwd_reset = sb("bwd_reset", [P, GROUPS, T])
        fwd_reset8 = sb("fwd_reset8", [P, GROUPS, H, T])
        bwd_reset8 = sb("bwd_reset8", [P, GROUPS, H, T])
        fwd_mask = sb("fwd_mask", [P, GROUPS, T])
        bwd_mask = sb("bwd_mask", [P, GROUPS, T])
        part_reset = sb("part_reset", [P, 2, GROUPS])
        part_rows = sb("part_rows", [2 * GROUPS, P])
        line = sb("line", [H, 2 * GROUPS, P])
        lo_f = sb("lo_f", [P, GROUPS, T], BF16)
        hi_f = sb("hi_f", [P, GROUPS, T], BF16)
        od_s = sb("od_s", [HI, LO])
        oh_hi = sb("oh_hi", [P, 2, HI, T], BF16)
        rep_hi = sb("rep_hi", [P, LO, T], BF16)
        nloc = sb("nloc", [P, GROUPS, T])
        oh_lo = sb("oh_lo", [P, 2, LO, T], BF16)
        xt = sb("xt", [P, NT, D + 1])
        xn = sb("xn", [P, 4, D])
        hT = sb("hT", [P, 2, D])
        st6 = sb("st6", [P, NT, 6])
        mv = sb("mv", [P, NT, 2])
        ve = sb("ve", [P, NT])
        rs_a = sb("rs_a", [P, NT])
        rs_t = sb("rs_t", [P, NT])
        qkv = sb("qkv", [P, 2, PCH, 3 * D])
        idx = sb("idx", [P, 2, T], I32)
        attr_s = sb("attr_s", [P, 2, 4, P])
        qwin = sb("qwin", [P, 2, D])
        xwin = sb("xwin", [P, 2, D + 1])
        kv = sb("kv", [P, 2, T, 2 * D])
        S = sb("S", [P, 2, T, P])
        ST = sb("ST", [P, 2, T, P])
        prod = sb("prod", [P, 2, 4, D])
        part_i = prod[:].rearrange("p a t d -> p (a t d)").bitcast(I32)[:, 0:GROUPS * T].rearrange("p (g t) -> p g t", t=T)
        sc = sb("sc", [P, H, T])
        f1 = sb("f1", [P, H, T])
        f2 = sb("f2", [P, H, T])
        bx = sb("bx", [P, H, T])
        tmp8 = sb("tmp8", [P, H, T])
        c1 = sb("c1", [H, 2, P + 1])
        c2 = sb("c2", [H, P + 1])
        z = sb("z", [P, H, T])
        wv = sb("wv", [P, T, C + 1])
        dfac = sb("dfac", [H, 1])
        fac = sb("fac", [H, 1])
        facd = sb("facd", [H, H])
        isf = sb("isf", [H, P])
        shift = sb("shift", [P, 2, P])
        R = sb("R", [P, 2, C + 1])
        fb = sb("fb", [P, H])
        rden = sb("rden", [P, H])
        agn = sb("agn", [P, D])
        agT = sb("agT", [P, D])
        x2 = sb("x2", [P, 2, D + 1])
        od_t = sb("od_t", [P, NT])
        v2 = sb("v2", [P, 2, NT])
        y2 = sb("y2", [P, 2, NT])
        t2 = sb("t2", [P, 2, NT])
        hsq = sb("hsq", [P, 2, D])
        hsr = sb("hsr", [P, D])
        ss_t = sb("ss_t", [P, NT])
        dinv_t = sb("dinv_t", [P, NT])
        sm = sb("sm", [P, 8, NT])
        rat = sb("rat", [P, NT])
        lnv = sb("lnv", [P, NT])
        b1d = sb("b1d", [P, 2, D])
        hs_t = qkv[:].rearrange("p a c d -> p (a c d)")[:, 0:NT * D].rearrange("p (n d) -> p n d", d=D)
        y_out = sb("y_out", [P, 2, D])
        ss = sb("ss", [P, 1])
        sm1 = sb("sm1", [P, 4])
        th = sb("th", [P, 1])
        nrm = sb("nrm", [P, 1])

        ps_q = [pb(f"ps_q{i}", [P, 512]) for i in range(2)]
        ps_s = [pb(f"ps_s{i}", [P, 512]) for i in range(2)]
        ps_b = pb("ps_b", [P, 512])
        ps_r = pb("ps_r", [P, 512])
        ps_c = pb("ps_c", [P, 512])
        ps_f = pb("ps_f", [P, 512])
        p_bias = ps_c[:, 384:384 + HT]
        p_v1 = ps_b[0:H, 128:256]
        p_c1 = ps_b[:, 256:256 + H]
        p_v2 = ps_b[0:H, 288:416]
        p_c2 = ps_b[:, 416:416 + H]
        p_rc = ps_c[:, 0:C + 1]
        p_fb = ps_c[:, 256:256 + H]

        s_in = sem("s_in")
        s_w = sem("s_w")
        s_xin = [sem(f"s_xin{i}") for i in range(NT // PCH)]
        s_od_st = sem("s_od_st")
        s_line_st = sem("s_line_st")
        s_line = sem("s_line")
        s_pool0 = sem("s_pool0")
        s_dv0 = sem("s_dv0")
        s_reset = sem("s_reset")
        s_reset8 = sem("s_reset8")
        s_base = sem("s_base")
        s_part = sem("s_part")
        s_partT = sem("s_partT")
        s_partrow = sem("s_partrow")
        s_ber = sem("s_ber")
        s_zero = sem("s_zero")
        s_xn = sem("s_xn")
        s_xnT = sem("s_xnT")
        s_hT = sem("s_hT")
        s_qkvp = sem("s_qkvp")
        s_qkv = sem("s_qkv")
        s_tab = [sem(f"s_tab{i}") for i in range(2)]
        s_oh = sem("s_oh")
        s_hist = sem("s_hist")
        s_od = sem("s_od")
        s_idx = sem("s_idx")
        s_attr = [sem(f"s_attr{i}") for i in range(2)]
        s_qwin = [sem(f"s_qwin{i}") for i in range(2)]
        s_xwin = [sem(f"s_xwin{i}") for i in range(2)]
        s_kv = [[sem(f"s_kv{i}_{c}") for c in range(NCH)] for i in range(2)]
        s_S = sem("s_S")
        s_Sa = sem("s_Sa")
        s_Sab = sem("s_Sab")
        s_nloc = sem("s_nloc")
        s_stp = sem("s_stp")
        s_st = sem("s_st")
        s_qt = sem("s_qt")
        s_prod = sem("s_prod")
        s_bias = sem("s_bias")
        s_sc = sem("s_sc")
        s_v1 = sem("s_v1")
        s_v1T = sem("s_v1T")
        s_cf = sem("s_cf")
        s_cfT = sem("s_cfT")
        s_v2 = sem("s_v2")
        s_v2T = sem("s_v2T")
        s_cb = sem("s_cb")
        s_cbT = sem("s_cbT")
        s_dfac = sem("s_dfac")
        s_fac = sem("s_fac")
        s_facd = sem("s_facd")
        s_z = sem("s_z")
        s_p = sem("s_p")
        s_wv = sem("s_wv")
        s_agg = sem("s_agg")
        s_rc = sem("s_rc")
        s_R = sem("s_R")
        s_agn = sem("s_agn")
        s_agTp = sem("s_agTp")
        s_agT = sem("s_agT")
        s_o = sem("s_o")
        s_x2 = sem("s_x2")
        s_x2st = sem("s_x2st")
        s_xn2 = sem("s_xn2")
        s_xn2T = sem("s_xn2T")
        s_h2T = sem("s_h2T")
        s_h1 = sem("s_h1")
        s_nc = sem("s_nc")
        s_ln = sem("s_ln")
        s_dinv = sem("s_dinv")
        s_b1d = sem("s_b1d")
        s_hs = sem("s_hs")
        s_hsst = sem("s_hsst")
        s_dA = sem("s_dA")
        s_dB = sem("s_dB")
        s_dM = sem("s_dM")
        s_pad = sem("s_pad")
        s_x2l = [sem(f"s_x2l{i}") for i in range(NT // PCH)]
        s_odl = sem("s_odl")
        s_dvst = sem("s_dvst")
        s_odw = sem("s_odw")
        s_idx1 = sem("s_idx1")
        s_xw1 = [sem(f"s_xw1{i}") for i in range(2)]
        s_g1 = [sem(f"s_g1{i}") for i in range(2)]
        s_S1 = sem("s_S1")
        s_agg1 = sem("s_agg1")
        s_R1 = sem("s_R1")
        s_ss1 = sem("s_ss1")
        s_zz1 = sem("s_zz1")
        s_norm1 = sem("s_norm1")
        s_th1 = sem("s_th1")
        s_y1 = sem("s_y1")
        s_yst = sem("s_yst")
        s_d1 = sem("s_d1")

        block = ctx.enter_context(nc.Block())

        def node_rows(tab):
            return tab.rearrange("(p n) d -> p n d", n=NT)

        turned = [ps_f, ps_c]

        def h1_of(i):
            bank = [ps_q[0], ps_q[1], ps_s[0], ps_s[1], ps_b, ps_r, turned[1]][i // 4]
            return bank[:, i % 4 * D:(i % 4 + 1) * D]

        def known(g):
            return isinstance(g, int)

        @block.sync
        def _(sp):
            for c in range(NT // PCH):
                rows = slice(PCH * c, PCH * c + PCH)
                sp.dma_start(xt[:, rows, 0:D], node_rows(x)[:, rows, :]).then_inc(s_xin[c], 16)
            for dst, src in ((wqkv_s[:], wqkv), (bqkv_s[:], bqkv.partition_broadcast(P)), (ident[:], ident_in)):
                sp.dma_start(dst, src).then_inc(s_w, 16)
            for dst, src in ((iota[:], iota_in), (imj[:], imj_in),
                             (dst_i[:].rearrange("p g t -> p (g t)"), dst_t),
                             (src_i[:].rearrange("p g t -> p (g t)"), src_t),
                             (before_i[:], dst_before), (after_i[:], dst_after),
                             (first_i[:], dst_first.partition_broadcast(P)), (be_s[:], be), (wo_s[:], wo),
                             (bo_s[:], bo), (w1_s[:], w1t), (b1_s[:], b1.partition_broadcast(P))):
                sp.dma_start(dst, src).then_inc(s_in, 16)
            sp.wait_ge(s_pool0, 1)
            for k in range(4):
                sp.dma_start(we4[EF * k:EF * k + EF, H * k:H * k + H], we).then_inc(s_in, 16)
            for c in range(NT // PCH):
                sp.wait_ge(s_qkv, PCH * (c + 1))
                rows = slice(PCH * c, PCH * c + PCH)
                sp.dma_start(node_rows(q_tab)[:, rows, :], qkv[:, c % 2, :, 0:D]).then_inc(s_tab[c % 2], 16)
                sp.dma_start(node_rows(kv_tab)[:, rows, :], qkv[:, c % 2, :, D:3 * D]).then_inc(s_tab[c % 2], 16)
            sp.wait_ge(s_partrow, 2)
            sp.dma_start(line_tab, part_rows[:]).then_inc(s_line_st, 16)
            sp.wait_ge(s_line_st, 16)
            sp.dma_start(line[:], line_tab.partition_broadcast(H)).then_inc(s_line, 16)
            sp.wait_ge(s_base, 1)
            sp.wait_ge(s_tab[0], 32 * 3)
            sp.wait_ge(s_tab[1], 32 * 2)

            def base_of(g):
                return sp.value_load(base_i[0:1, g:g + 1] if known(g) else base_i[0:1, bass.ds(g, 1)],
                                     min_val=0, max_val=N - P)

            def load_edges(g, b):
                if not (known(g) and g < 2):
                    wait_apart(sp, s_bias, g - 1, (s_base, 1))
                sp.dma_start(attr_s[:, b, 0:3, :],
                             attr[bass.ds(g, 1), 0:3 * P, :].rearrange("o (k p) e -> p (o k) e", p=P)).then_inc(s_attr[b], 16)
                sp.dma_start(attr_s[0:EF, b, 3, :],
                             attr[bass.ds(g, 1), 3 * P:T * EF, :].rearrange("o p e -> p (o e)")).then_inc(s_attr[b], 16)
                w = base_of(g)
                if not (known(g) and g < 2):
                    wait_apart(sp, s_qt, NCH * (g - 1), (s_base, 1))
                sp.dma_start(qwin[:, b, :], q_tab[bass.ds(w, P), :]).then_inc(s_qwin[b], 16)

            def load_nodes(g, b):
                w = base_of(g)
                if not (known(g) and g < 2):
                    wait_apart(sp, s_x2, 2 * g - 2, (s_base, 1))
                sp.dma_start(xwin[:, b, 0:D], x[bass.ds(w, P), :]).then_inc(s_xwin[b], 16)

            def store_nodes(g, b):
                w = base_of(g)
                wait_apart(sp, s_x2, 2 * g + 2, (s_base, 1))
                if not (known(g) and g == 0):
                    wait_apart(sp, s_x2st, 16 * g, (s_base, 1))
                sp.dma_start(x2_tab[bass.ds(w, P), :], x2[:, b, :]).then_inc(s_x2st, 16)

            load_edges(0, 0)
            load_edges(1, 1)
            load_nodes(0, 0)
            load_nodes(1, 1)
            sp.wait_ge(s_zero, 1)
            sp.dma_start(x2_tab[N:NPAD, :], zero_rows[:]).then_inc(s_pad, 16)
            with sp.Fori(1, GROUPS // 2) as n:
                for b in range(2):
                    load_edges(2 * n + b, b)
                    store_nodes(2 * n + b - 2, b)
                    load_nodes(2 * n + b, b)
            store_nodes(GROUPS - 2, 0)
            sp.wait_ge(s_od, GROUPS)
            sp.dma_start(od_tab.rearrange("(h l) o -> h (l o)", l=LO), od_s[:]).then_inc(s_od_st, 16)
            sp.wait_ge(s_od_st, 16)
            sp.dma_start(od_t[:], od_tab.rearrange("(p n) o -> p (n o)", n=NT)).then_inc(s_odl, 16)
            store_nodes(GROUPS - 1, 1)
            sp.wait_ge(s_x2st, 16 * GROUPS)
            sp.wait_ge(s_pad, 16)
            for c in range(NT // PCH):
                rows = slice(PCH * c, PCH * c + PCH)
                sp.dma_start(xt[:, rows, :], node_rows(x2_tab)[:, rows, :]).then_inc(s_x2l[c], 16)
            sp.wait_ge(s_dinv, 1)
            sp.dma_start(dinv_tab.rearrange("(p n) o -> p (n o)", n=NT), dinv_t[:]).then_inc(s_dvst, 16)
            for c in range(NT // PCH):
                rows = slice(PCH * c, PCH * c + PCH)
                sp.wait_ge(s_hs, PCH * (c + 1))
                sp.dma_start(node_rows(hs_tab)[:, rows, :], hs_t[:, rows, :]).then_inc(s_hsst, 16)
            sp.wait_ge(s_dvst, 16)

            def load_window(g, b):
                w = base_of(g)
                if not (known(g) and g < 2):
                    wait_apart(sp, s_y1, g - 1, (s_base, 1))
                sp.dma_start(xwin[:, b, 0:D], x2_tab[bass.ds(w, P), 0:D]).then_inc(s_xw1[b], 16)
                sp.dma_start(xwin[:, b, D:D + 1], dinv_tab[bass.ds(w, P), :]).then_inc(s_xw1[b], 16)

            def store_out(g, b):
                w = base_of(g)
                wait_apart(sp, s_y1, g + 1, (s_base, 1))
                if not (known(g) and g == 0):
                    wait_apart(sp, s_yst, 16 * g, (s_base, 1))
                sp.dma_start(out[bass.ds(w, P), :], y_out[:, b, :]).then_inc(s_yst, 16)

            load_window(0, 0)
            load_window(1, 1)
            with sp.Fori(1, GROUPS // 2) as n:
                for b in range(2):
                    store_out(2 * n + b - 2, b)
                    load_window(2 * n + b, b)
            store_out(GROUPS - 2, 0)
            store_out(GROUPS - 1, 1)
            sp.wait_ge(s_yst, 16 * GROUPS)

        @block.gpsimd
        def _(pool):
            nc.gpsimd.memset(we4[:], 0.0).then_inc(s_pool0, 1)
            pool.wait_ge(s_tab[0], 32 * 3)
            pool.wait_ge(s_tab[1], 32 * 2)

            def gather(g, b):
                wait_apart(pool, s_idx, g + 1, (s_tab[0], 32 * 3))
                if not (known(g) and g < 2):
                    wait_apart(pool, s_wv, g - 1, (s_tab[0], 32 * 3))
                for c, (t0, t1) in enumerate(CH):
                    for t in range(t0, t1):
                        pool.indirect_dma_start(out=kv[:, b, t, :], out_offset=None, in_=kv_tab,
                                                in_offset=bass.IndirectOffsetOnAxis(ap=idx[:, b, t:t + 1], axis=0))\
                            .then_inc(s_kv[b][c], 16)

            gather(0, 0)
            gather(1, 1)
            with pool.Fori(1, GROUPS // 2) as n:
                gather(2 * n, 0)
                gather(2 * n + 1, 1)

            pool.wait_ge(s_hsst, 16 * (NT // PCH))

            def gather1(g, b):
                wait_apart(pool, s_idx1, g + 1, (s_tab[0], 32 * 3))
                if not (known(g) and g < 2):
                    wait_apart(pool, s_agg1, g - 1, (s_tab[0], 32 * 3))
                for t in range(T):
                    pool.indirect_dma_start(out=kv[:, b, t, 0:D], out_offset=None, in_=hs_tab,
                                            in_offset=bass.IndirectOffsetOnAxis(ap=idx[:, b, t:t + 1], axis=0))\
                        .then_inc(s_g1[b], 16)

            gather1(0, 0)
            gather1(1, 1)
            with pool.Fori(1, GROUPS // 2) as n:
                gather1(2 * n, 0)
                gather1(2 * n + 1, 1)

        @block.vector
        def _(dve):
            V = nc.vector
            pre = Steps(nc, dve, s_dv0, 0)

            pre.mark(V.memset(ones_row[:], 1.0))
            V.memset(zero_rows[:], 0.0).then_inc(s_zero, 1)
            pre.mark(V.memset(c1[:], BIG))
            pre.mark(V.memset(c2[:], BIG))
            pre.mark(V.memset(R[:], 0.0))
            pre.mark(V.memset(wv[:], 1.0))

            def set_idx(g, b, ready):
                V.tensor_copy(idx[:, b, :], src_i[:, g, :] if known(g) else
                              src_i[:, bass.ds(g, 1), :].rearrange("p g t -> p (g t)")).then_inc(ready, 1)

            def stats(st, arrived):
                for c in range(NT // PCH):
                    dve.wait_ge(arrived[c], 16)
                    for i in range(PCH * c, PCH * c + PCH):
                        st.mark(V.bn_stats(st6[:, i, :], xt[:, i, 0:D]))
                    if c:
                        for i in range(PCH * (c - 1), PCH * c):
                            st.mark(V.bn_aggr(mv[:, i, :], st6[:, i, :]))
                    st.sync()
                for i in range(NT - PCH, NT):
                    st.mark(V.bn_aggr(mv[:, i, :], st6[:, i, :]))
                st.sync()

            stats(pre, s_xin)
            pre.then(V.tensor_scalar(ve[:], mv[:, :, 1], EPS_LN, None, ALU.add))
            rsqrt(pre, rs_a[:], ve[:], rs_t[:])
            dve.wait_ge(s_w, 16 * 3)
            pre.mark(V.tensor_scalar(wqkv_s[:, 0:D], wqkv_s[:, 0:D], DH ** -0.5, None, ALU.mult))
            pre.then(V.tensor_scalar(bqkv_s[:, 0:D], bqkv_s[:, 0:D], DH ** -0.5, None, ALU.mult))

            def norm_tile(i):
                if i >= 4:
                    dve.wait_ge(s_xnT, i - 3)
                V.tensor_scalar(xn[:, i % 4, :], xt[:, i, 0:D], mv[:, i, 0:1], rs_a[:, i:i + 1],
                                ALU.subtract, ALU.mult).then_inc(s_xn, 1)

            def qkv_tile(i):
                c = i // PCH
                dve.wait_ge(s_qkvp, i + 1)
                if i % PCH == 0 and c >= 2:
                    dve.wait_ge(s_tab[c % 2], 32 * (c // 2))
                V.tensor_tensor(qkv[:, c % 2, i % PCH, :], ps_q[i % 2][:, 0:3 * D], bqkv_s[:],
                                ALU.add).then_inc(s_qkv, 1)

            for i in range(3):
                norm_tile(i)
            dve.wait_ge(s_in, 16 * 16)
            set_idx(0, 0, s_idx)
            set_idx(1, 1, s_idx)
            for i in range(NT):
                if i + 3 < NT:
                    norm_tile(i + 3)
                qkv_tile(i)

            GT3 = [P, GROUPS, T]
            pre.then(V.tensor_copy(first_f[:], first_i[:]))
            pre.then(V.tensor_scalar(base_f[:], first_f[:], float(N - P), None, ALU.min))
            V.tensor_copy(base_i[:], base_f[:]).then_inc(s_base, 1)
            pre.mark(V.memset(delta[:, 0:1], 0.0))
            pre.mark(V.tensor_tensor(delta[:, 1:], base_f[:, 1:], base_f[:, :-1], ALU.subtract))
            pre.mark(V.tensor_tensor(ofirst[:], first_f[:], base_f[:], ALU.subtract))
            pre.mark(V.tensor_tensor(dloc[:], dst_i[:], base_f[:].unsqueeze(2).to_broadcast(GT3), ALU.subtract))
            pre.mark(V.tensor_tensor(part_reset[:, 0, :], dst_i[:, :, T - 1], before_i[:], ALU.not_equal))
            pre.mark(V.tensor_tensor(part_reset[:, 1, :], dst_i[:, :, 0], after_i[:], ALU.not_equal))
            pre.mark(V.tensor_tensor(fwd_reset[:, :, 1:], dst_i[:, :, 1:], dst_i[:, :, :-1], ALU.not_equal))
            pre.mark(V.memset(fwd_reset[:, :, 0:1], 1.0))
            pre.mark(V.tensor_tensor(bwd_reset[:, :, :-1], dst_i[:, :, 1:], dst_i[:, :, :-1], ALU.not_equal))
            pre.mark(V.memset(bwd_reset[:, :, T - 1:T], 1.0))
            pre.mark(V.tensor_tensor(fwd_mask[:], dst_i[:], before_i[:].unsqueeze(2).to_broadcast(GT3), ALU.not_equal))
            pre.then(V.tensor_tensor(bwd_mask[:], dst_i[:], after_i[:].unsqueeze(2).to_broadcast(GT3), ALU.not_equal))
            V.tensor_scalar(nloc[:], dloc[:], -1.0, None, ALU.mult).then_inc(s_nloc, 1)
            V.tensor_scalar(part_reset[:], part_reset[:], BIG, None, ALU.mult).then_inc(s_part, 1)
            V.tensor_scalar(fwd_reset[:], fwd_reset[:], BIG, None, ALU.mult).then_inc(s_reset, 1)
            V.tensor_scalar(bwd_reset[:], bwd_reset[:], BIG, None, ALU.mult).then_inc(s_reset, 1)
            pre.mark(V.tensor_scalar(fwd_mask[:], fwd_mask[:], BIG, None, ALU.mult))
            pre.then(V.tensor_scalar(bwd_mask[:], bwd_mask[:], BIG, None, ALU.mult))

            def col(tile, g):
                return tile[:, g:g + 1] if known(g) else tile[:, bass.ds(g, 1)]

            def col3(tile, g):
                return (tile[:, g:g + 1, :] if known(g) else tile[:, bass.ds(g, 1), :]).rearrange("p g t -> p (g t)")

            def one_hots(g, b, used, ready, t0=0):
                if not (known(g) and g < 2):
                    dve.wait_ge(used, g - 1)
                V.tensor_scalar(shift[:, b, :], imj[:], col(delta, g), None, ALU.is_equal).then_inc(ready, 1)
                V.tensor_tensor(S[:, b, t0:T, :], col3(dloc, g)[:, t0:T].unsqueeze(2).to_broadcast([P, T - t0, P]),
                                iota[:].unsqueeze(1).to_broadcast([P, T - t0, P]), ALU.is_equal).then_inc(ready, 1)

            one_hots(0, 0, None, s_S, TA)
            dve.wait_ge(s_partT, 1)
            V.tensor_copy(part_rows[0:GROUPS, :], ps_b[0:GROUPS, 0:P]).then_inc(s_partrow, 1)
            V.tensor_copy(part_rows[GROUPS:, :], ps_b[GROUPS:2 * GROUPS, 0:P][:, ::-1]).then_inc(s_partrow, 1)
            pre.mark(V.tensor_copy(rep_hi[:], iota[:, 0:LO].unsqueeze(2).to_broadcast([P, LO, T])))
            pre.then(V.tensor_scalar(part_i, src_i[:], 6, None, ALU.logical_shift_right))
            pre.then(V.tensor_copy(hi_f[:], part_i))
            pre.then(V.tensor_scalar(part_i, src_i[:], LO - 1, None, ALU.bitwise_and))
            pre.then(V.tensor_copy(lo_f[:], part_i))
            pre.mark(V.memset(od_s[:], 0.0))
            dve.wait_ge(s_reset8, 2 * H)
            dve.wait_ge(s_line, 16)

            def source_one_hots(g, b):
                if not (known(g) and g < 2):
                    dve.wait_ge(s_hist, g - 1)
                for oh, part, m in ((oh_hi, hi_f, HI), (oh_lo, lo_f, LO)):
                    V.tensor_tensor(oh[:, b], col3(part, g).unsqueeze(1).to_broadcast([P, m, T]),
                                    rep_hi[:, 0:m, :], ALU.is_equal).then_inc(s_oh, 1)

            def add_counts(g):
                dve.wait_ge(s_hist, g + 1)
                if not (known(g) and g == 0):
                    dve.wait_ge(s_od, g)
                V.tensor_tensor(od_s[:], od_s[:], ps_f[0:HI, 3 * D:3 * D + LO], ALU.add).then_inc(s_od, 1)

            def flat(tile):
                return tile[:].rearrange("p h t -> p (h t)")

            def reset8(tile, g):
                return (tile[:, g:g + 1] if known(g) else tile[:, bass.ds(g, 1)]).rearrange("p g h t -> p (g h t)")

            def lines(g):
                return (line[:, g:g + 1, :] if known(g) else line[:, bass.ds(g, 1), :]).rearrange("p g t -> p (g t)")

            def mask8(tile, g):
                return col3(tile, g).unsqueeze(1).to_broadcast([P, H, T])

            def scores(g, b, st):
                def product(c):
                    t0, t1 = CH[c]
                    w = t1 - t0
                    dve.wait_ge(s_kv[b][c], 16 * w * ((g - b) // 2 + 1) if known(g) else (g + (2 - b)) * (8 * w))
                    dve.wait_ge(s_qt, NCH * g + c + 1)
                    if c >= 2:
                        st.sync()
                    V.tensor_tensor(prod[:, c % 2, 0:w, :], kv[:, b, t0:t1, 0:D],
                                    ps_q[c % 2][:, 0:w * D].rearrange("p (t d) -> p t d", d=D), ALU.mult).then_inc(s_prod, 1)

                def per_head(c):
                    t0, t1 = CH[c]
                    dve.wait_ge(s_prod, NCH * g + c + 1)
                    st.mark(V.tensor_reduce(sc[:, :, t0:t1].rearrange("p h t -> p t h"),
                                            prod[:, c % 2, 0:t1 - t0, :].rearrange("p t (h d) -> p t h d", d=DH),
                                            AX_X, ALU.add))

                product(0)
                for c in range(NCH):
                    if c + 1 < NCH:
                        product(c + 1)
                    per_head(c)
                st.sync()
                dve.wait_ge(s_bias, g + 1)
                V.tensor_tensor(sc[:], sc[:], p_bias.rearrange("p (t h) -> p h t", h=H), ALU.add).then_inc(s_sc, 1)
                dve.wait_ge(s_sc, g + 1)
                V.tensor_tensor_scan(out=flat(f1), data0=reset8(fwd_reset8, g), data1=flat(sc), initial=BIG,
                                     op0=ALU.add, op1=ALU.max).then_inc(s_v1, 1)

            def scan_partitions(g, b, st):
                dve.wait_ge(s_v1T, g + 1)
                if not (known(g) and g < 2):
                    dve.wait_ge(s_cfT, g - 1)
                st.mark(V.tensor_copy(c1[:, b, 0:1], c1[:, 1 - b, P:P + 1]))
                V.tensor_tensor_scan(out=c1[:, b, 1:P + 1], data0=lines(g), data1=p_v1, initial=c1[:, 1 - b, P:P + 1],
                                     op0=ALU.add, op1=ALU.max).then_inc(s_cf, 1)

            def backward(g, b, st):
                dve.wait_ge(s_cfT, g + 1)
                st.then(V.tensor_tensor(tmp8[:], mask8(fwd_mask, g), p_c1.unsqueeze(2).to_broadcast([P, H, T]), ALU.add))
                st.then(V.tensor_tensor(f2[:], f1[:], tmp8[:], ALU.max))
                V.tensor_tensor_scan(out=flat(bx)[:, ::-1], data0=reset8(bwd_reset8, g), data1=flat(f2)[:, ::-1],
                                     initial=BIG, op0=ALU.add, op1=ALU.max).then_inc(s_v2, 1)

            def scan_partitions_back(g, b, st):
                if not (known(g) and g == 0):
                    dve.wait_ge(s_rc, g)
                st.mark(V.tensor_scalar(isf[:], iota[0:H, :], col(ofirst[0:H], g), None, ALU.is_equal))
                dve.wait_ge(s_v2T, g + 1)
                V.tensor_tensor_scan(out=c2[:, 0:P][:, ::-1], data0=lines(g + GROUPS), data1=p_v2[:, ::-1],
                                     initial=BIG, op0=ALU.add, op1=ALU.max).then_inc(s_cb, 1)
                dve.wait_ge(s_cb, g + 1)
                st.then(V.tensor_tensor(dfac[:], c1[:, b, 0:1], c2[:, 0:1], ALU.subtract))
                V.tensor_scalar(dfac[:], dfac[:], 0.0, None, ALU.min).then_inc(s_dfac, 1)

            def shifted(g, b, st):
                dve.wait_ge(s_cbT, g + 1)
                st.then(V.tensor_tensor(tmp8[:], mask8(bwd_mask, g), p_c2.unsqueeze(2).to_broadcast([P, H, T]), ALU.add))
                st.then(V.tensor_tensor(tmp8[:], bx[:], tmp8[:], ALU.max))
                V.tensor_tensor(z[:], sc[:], tmp8[:], ALU.subtract).then_inc(s_z, 1)
                dve.wait_ge(s_fac, g + 1)
                V.scalar_tensor_tensor(out=facd[:], in0=ident[0:H, 0:H], scalar=fac[:], in1=ident[0:H, 0:H],
                                       op0=ALU.mult, op1=ALU.subtract).then_inc(s_facd, 1)

            def weigh(g, b):
                dve.wait_ge(s_p, g + 1)
                w4 = wv[:, :, 0:C].rearrange("p t (h e) -> p t h e", e=DH + 1)
                V.tensor_tensor(w4[:, :, :, 0:DH], kv[:, b, :, D:2 * D].rearrange("p t (h d) -> p t h d", d=DH),
                                w4[:, :, :, DH:DH + 1].to_broadcast([P, T, H, DH]), ALU.mult).then_inc(s_wv, 1)

            def combine(g, b, st):
                dve.wait_ge(s_rc, g + 1)
                st.mark(V.tensor_scalar(fb[:], p_fb, 1.0, None, ALU.add))
                st.then(V.tensor_copy(R[:, b, C:C + 1], p_rc[:, C:C + 1]))
                st.then(V.tensor_tensor(R[:, b, 0:C].rearrange("p (h e) -> p h e", h=H),
                                        p_rc[:, 0:C].rearrange("p (h e) -> p h e", h=H),
                                        fb[:].unsqueeze(2).to_broadcast([P, H, DH + 1]), ALU.mult))
                V.tensor_tensor(R[:, b, :], R[:, b, :], ps_r[:, 0:C + 1], ALU.add).then_inc(s_R, 1)
                dve.wait_ge(s_R, g + 1)
                r3 = R[:, b, 0:C].rearrange("p (h e) -> p h e", h=H)
                st.then(V.tensor_scalar(rden[:].unsqueeze(2), r3[:, :, DH:DH + 1], 1e-10, None, ALU.add))
                st.then(V.reciprocal(rden[:], rden[:]))
                V.tensor_tensor(agn[:].rearrange("p (h d) -> p h d", h=H), r3[:, :, 0:DH],
                                rden[:].unsqueeze(2).to_broadcast([P, H, DH]), ALU.mult).then_inc(s_agn, 1)

            def new_rows(g, b):
                dve.wait_ge(s_o, g + 1)
                dve.wait_ge(s_xwin[b], 16 * ((g - b) // 2 + 1) if known(g) else (g + (2 - b)) * 8)
                if not (known(g) and g < 2):
                    dve.wait_ge(s_x2st, 16 * (g - 1))
                V.tensor_tensor(x2[:, b, 0:D], ps_f[:, D:2 * D], xwin[:, b, 0:D], ALU.add).then_inc(s_x2, 1)
                V.tensor_copy(x2[:, b, D:D + 1], R[:, b, C:C + 1]).then_inc(s_x2, 1)

            def square_norm(i):
                dve.wait_ge(s_xn2, i + 1)
                M_.mark(V.scalar_tensor_tensor(out=hsq[:, i % 2, :], in0=xn[:, i % 4, :], scalar=0.0, in1=xn[:, i % 4, :],
                                               op0=ALU.max, op1=ALU.mult, accum_out=ss_t[:, i:i + 1]))

            def step(g, b, edges=True, nodes=True, more=True, far=True):
                A = Steps(nc, dve, s_dA, NA * g)
                B = Steps(nc, dve, s_dB, NB * (g - 1))
                if edges:
                    scores(g, b, A)
                if nodes:
                    combine(g - 1, 1 - b, B)
                    B.check(NB)
                if edges:
                    scan_partitions(g, b, A)
                    if more:
                        one_hots(g + 1, 1 - b, s_rc, s_S, TA)
                    if more:
                        source_one_hots(g + 1, 1 - b)
                    backward(g, b, A)
                    if far:
                        set_idx(g + 2, b, s_idx)
                    scan_partitions_back(g, b, A)
                    shifted(g, b, A)
                if nodes:
                    new_rows(g - 1, 1 - b)
                if edges:
                    add_counts(g)
                    weigh(g, b)
                    A.check(NA)

            source_one_hots(0, 0)
            step(0, 0, nodes=False)
            step(1, 1)
            with dve.Fori(1, GROUPS // 2 - 1) as n:
                step(2 * n, 0)
                step(2 * n + 1, 1)
            step(GROUPS - 2, 0, far=False)
            step(GROUPS - 1, 1, more=False, far=False)
            step(GROUPS, 0, edges=False)

            set_idx(0, 0, s_idx1)
            set_idx(1, 1, s_idx1)
            one_hots(0, 0, None, s_S1)
            one_hots(1, 1, None, s_S1)

            M_ = Steps(nc, dve, s_dM, 0)
            stats(M_, s_x2l)
            dve.wait_ge(s_odl, 16)
            M_.mark(V.tensor_scalar(v2[:, 0, :], mv[:, :, 1], EPS_LN, None, ALU.add))
            M_.then(V.tensor_tensor(v2[:, 1, :], xt[:, :, D], od_t[:], ALU.add))
            M_.then(V.tensor_scalar(v2[:, 1, :], v2[:, 1, :], 1.0, None, ALU.max))
            rsqrt(M_, y2[:], v2[:], t2[:])
            V.tensor_copy(dinv_t[:], y2[:, 1, :]).then_inc(s_dinv, 1)
            for i in range(NT):
                if i >= 4:
                    dve.wait_ge(s_xn2T, i - 3)
                V.tensor_scalar(xn[:, i % 4, :], xt[:, i, 0:D], mv[:, i, 0:1], y2[:, 0, i:i + 1],
                                ALU.subtract, ALU.mult).then_inc(s_xn2, 1)
                if i:
                    square_norm(i - 1)
            square_norm(NT - 1)
            M_.sync()

            v_, y_, t_, nc_, q_, ser, at_, a_ = [sm[:, i, :] for i in range(8)]
            M_.then(V.tensor_scalar(v_, ss_t[:], 1e-30, None, ALU.max))
            rsqrt(M_, y_, v_, t_)
            M_.then(V.tensor_tensor(t_, ss_t[:], y_, ALU.mult))
            M_.then(V.tensor_scalar(nc_, t_, 1e-15, ATANH_MAX, ALU.max, ALU.min))
            M_.mark(V.tensor_tensor(q_, nc_, nc_, ALU.mult))
            M_.then(V.tensor_scalar(t_, nc_, -1.0, 1.0, ALU.mult, ALU.add))
            M_.mark(V.tensor_scalar(ser, q_, 1.0 / 9, 1.0 / 7, ALU.mult, ALU.add))
            M_.then(V.reciprocal(t_, t_))
            V.scalar_tensor_tensor(out=rat[:], in0=nc_, scalar=2.0, in1=t_, op0=ALU.mult, op1=ALU.mult).then_inc(s_nc, 1)
            for k in (1.0 / 5, 1.0 / 3, 1.0):
                M_.then(V.tensor_tensor(ser, ser, q_, ALU.mult))
                M_.then(V.tensor_scalar(ser, ser, k, None, ALU.add))
            M_.then(V.tensor_tensor(ser, ser, nc_, ALU.mult))
            dve.wait_ge(s_ln, 1)
            M_.then(V.scalar_tensor_tensor(out=t_, in0=lnv[:], scalar=-0.5, in1=ser, op0=ALU.mult, op1=ALU.add))
            M_.then(V.scalar_tensor_tensor(out=t_, in0=nc_, scalar=SERIES_BELOW, in1=t_, op0=ALU.is_lt, op1=ALU.mult))
            M_.then(V.scalar_tensor_tensor(out=at_, in0=lnv[:], scalar=0.5, in1=t_, op0=ALU.mult, op1=ALU.add))
            M_.then(V.tensor_tensor(a_, at_, y_, ALU.mult))
            M_.then(V.tensor_tensor(a_, a_, y2[:, 1, :], ALU.mult))
            dve.wait_ge(s_h1, NT)
            for i in range(NT):
                dve.wait_ge(s_b1d, i + 1)
                V.scalar_tensor_tensor(out=hs_t[:, i, :], in0=h1_of(i), scalar=a_[:, i:i + 1], in1=b1d[:, i % 2, :],
                                       op0=ALU.mult, op1=ALU.add).then_inc(s_hs, 1)

            V.memset(R[:, 1, :], 0.0).then_inc(s_R1, 1)
            v_, y_, t_, a_ = [sm1[:, i:i + 1] for i in range(4)]

            def out_rows(g, b, more=True):
                st = Steps(nc, dve, s_d1, N1 * g)
                dve.wait_ge(s_agg1, g + 1)
                V.tensor_copy(R[:, b, 0:D], [ps_r, ps_c][b][:, 0:D]).then_inc(s_R1, 1)
                dve.wait_ge(s_R1, g + 2)
                dve.wait_ge(s_xw1[b], 32 * ((g - b) // 2 + 1) if known(g) else (g + (2 - b)) * 16)
                V.tensor_scalar(agn[:], R[:, b, 0:D], xwin[:, b, D:D + 1], None, ALU.mult).then_inc(s_zz1, 1)
                if more:
                    one_hots(g + 2, b, s_agg1, s_S1)
                    dve.wait_ge(s_g1[b], 16 * T * ((g - b) // 2 + 1) if known(g) else (g + (2 - b)) * (8 * T))
                    set_idx(g + 2, b, s_idx1)
                dve.wait_ge(s_ss1, g + 1)
                st.then(V.tensor_scalar(v_, ss[:], 1e-30, None, ALU.max))
                rsqrt(st, y_, v_, t_)
                V.tensor_tensor(nrm[:], ss[:], y_, ALU.mult).then_inc(s_norm1, 1)
                dve.wait_ge(s_th1, g + 1)
                st.then(V.tensor_scalar(a_, y_, 1e15, th[:], ALU.min, ALU.mult))
                if not (known(g) and g < 2):
                    dve.wait_ge(s_yst, 16 * (g - 1))
                V.scalar_tensor_tensor(out=y_out[:, b, :], in0=agn[:], scalar=a_, in1=xwin[:, b, 0:D],
                                       op0=ALU.mult, op1=ALU.add).then_inc(s_y1, 1)
                st.check(N1)

            out_rows(0, 0)
            out_rows(1, 1)
            with dve.Fori(1, GROUPS // 2 - 1) as n:
                out_rows(2 * n, 0)
                out_rows(2 * n + 1, 1)
            out_rows(GROUPS - 2, 0, more=False)
            out_rows(GROUPS - 1, 1, more=False)

        @block.scalar
        def _(act):
            A = nc.scalar
            for i in range(NT):
                act.wait_ge(s_xnT, i + 1)
                if i >= 2:
                    act.wait_ge(s_qkvp, i - 1)
                A.activation(hT[:, i % 2, :], ps_s[i % 2][:, 0:D], ACT.Relu).then_inc(s_hT, 1)
            act.wait_ge(s_in, 16 * 16)
            for t in range(T):
                A.copy(be_r[:, t, :], be_s[:]).then_inc(s_ber, 1)

            def one_hots(g, b, chunks):
                if 0 in chunks and not (known(g) and g < 2):
                    act.wait_ge(s_agg, g - 1)
                for c in chunks:
                    t0, t1 = CH[c]
                    for t in range(t0, t1):
                        A.activation(S[:, b, t, :], iota[:], ACT.Abs, bias=nloc[:, g, t:t + 1] if known(g) else
                                     nloc[:, bass.ds(g, 1), t:t + 1].rearrange("p g t -> p (g t)")).then_inc(s_Sab, 1)
                    act.wait_ge(s_Sab, TA * g + t1)
                    A.activation(S[:, b, t0:t1, :], S[:, b, t0:t1, :], ACT.Relu, bias=1.0, scale=-1.0).then_inc(s_Sa, 1)

            def turn_copies(g, b, chunks):
                if 0 in chunks and not (known(g) and g < 2):
                    act.wait_ge(s_qt, NCH * (g - 1))
                for c in chunks:
                    t0, t1 = CH[c]
                    w = (t1 - t0) * P
                    act.wait_ge(s_stp, NCH * g + c + 1)
                    A.copy(ST[:, b, t0:t1, :].rearrange("p t e -> p (t e)"), ps_s[c % 2][:, 0:w]).then_inc(s_st, 1)

            def agg_copy(g):
                act.wait_ge(s_agTp, g + 1)
                if not (known(g) and g == 0):
                    act.wait_ge(s_o, g)
                A.copy(agT[:], ps_f[:, 0:D]).then_inc(s_agT, 1)

            def edge_part(g, b):
                act.wait_ge(s_dfac, g + 1)
                A.activation(fac[:], dfac[:], ACT.Exp).then_inc(s_fac, 1)
                act.wait_ge(s_z, g + 1)
                if not (known(g) and g == 0):
                    act.wait_ge(s_agg, g)
                A.activation(wv[:, :, 0:C].rearrange("p t (h e) -> p h t e", e=DH + 1)[:, :, :, DH], z[:], ACT.Exp)\
                    .then_inc(s_p, 1)

            def step(g, b, nodes=True, more=True):
                if more:
                    one_hots(g + 1, 1 - b, (0, 1))
                    turn_copies(g + 1, 1 - b, (0,))
                if nodes:
                    agg_copy(g - 1)
                if more:
                    one_hots(g + 1, 1 - b, (2,))
                    turn_copies(g + 1, 1 - b, (1,))
                edge_part(g, b)
                if more:
                    turn_copies(g + 1, 1 - b, (2, 3))

            act.wait_ge(s_nloc, 1)
            one_hots(0, 0, (0, 1, 2))
            act.wait_ge(s_reset, 2)
            for h in range(H):
                A.copy(fwd_reset8[:, :, h, :], fwd_reset[:]).then_inc(s_reset8, 1)
                A.copy(bwd_reset8[:, :, h, :], bwd_reset[:, :, ::-1]).then_inc(s_reset8, 1)
            turn_copies(0, 0, (0, 1, 2, 3))
            step(0, 0, nodes=False)
            with act.Fori(0, GROUPS // 2 - 1) as n:
                step(2 * n + 1, 1)
                step(2 * n + 2, 0)
            step(GROUPS - 1, 1, more=False)
            agg_copy(GROUPS - 1)

            for i in range(NT):
                act.wait_ge(s_xn2T, i + 1)
                if i >= 2:
                    act.wait_ge(s_h1, i - 1)
                A.activation(hT[:, i % 2, :], turned[i % 2][:, 0:D], ACT.Relu).then_inc(s_h2T, 1)
            act.wait_ge(s_dinv, 1)
            for i in range(2):
                A.activation(b1d[:, i, :], b1_s[:], ACT.Copy, scale=dinv_t[:, i:i + 1]).then_inc(s_b1d, 1)
            act.wait_ge(s_nc, 1)
            A.activation(lnv[:], rat[:], ACT.Ln, bias=1.0).then_inc(s_ln, 1)
            for i in range(2, NT):
                act.wait_ge(s_hs, i - 1)
                A.activation(b1d[:, i % 2, :], b1_s[:], ACT.Copy, scale=dinv_t[:, i:i + 1]).then_inc(s_b1d, 1)

            def norm_part(g):
                act.wait_ge(s_zz1, g + 1)
                A.activation(hsq[:, 0, :], agn[:], ACT.Square, accum_out=ss[:]).then_inc(s_ss1, 1)
                act.wait_ge(s_norm1, g + 1)
                A.activation(th[:], nrm[:], ACT.Tanh).then_inc(s_th1, 1)

            norm_part(0)
            norm_part(1)
            with act.Fori(1, GROUPS // 2) as n:
                norm_part(2 * n)
                norm_part(2 * n + 1)

        @block.tensor
        def _(pe):
            M = nc.tensor
            pe.wait_ge(s_w, 16 * 3)

            def turn_tile(i):
                pe.wait_ge(s_xn, i + 1)
                if i >= 2:
                    pe.wait_ge(s_hT, i - 1)
                M.transpose(ps_s[i % 2][:, 0:D], xn[:, i % 4, :], ident[:]).then_inc(s_xnT, 1)

            turn_tile(0)
            for i in range(NT):
                if i + 1 < NT:
                    turn_tile(i + 1)
                pe.wait_ge(s_hT, i + 1)
                if i >= 2:
                    pe.wait_ge(s_qkv, i - 1)
                M.matmul(ps_q[i % 2][:, 0:3 * D], hT[:, i % 2, :], wqkv_s[:], start=True, stop=True).then_inc(s_qkvp, 1)
            pe.wait_ge(s_in, 16 * 16)
            pe.wait_ge(s_part, 1)
            M.transpose(ps_b[0:2 * GROUPS, 0:P], part_reset[:].rearrange("p k g -> p (k g)"), ident[:]).then_inc(s_partT, 1)

            def turn(g, b, chunks):
                for c in chunks:
                    t0, t1 = CH[c]
                    if t1 <= TA:
                        pe.wait_ge(s_Sa, (NCH - 1) * g + c + 1)
                    else:
                        pe.wait_ge(s_S, 2 * g + 2)
                    if not (known(g) and g == 0 and c < 2):
                        pe.wait_ge(s_st, NCH * g + c - 1)
                    for t in range(t0, t1):
                        mm = M.transpose(ps_s[c % 2][:, (t - t0) * P:(t - t0 + 1) * P], S[:, b, t, :], ident[:])
                    mm.then_inc(s_stp, 1)

            def bias(g, b, parts):
                if 0 in parts:
                    if not (known(g) and g == 0):
                        pe.wait_ge(s_sc, g)
                    M.matmul(p_bias, ones_row[:], be_r[:].rearrange("p t h -> p (t h)"), start=True, stop=False)
                    pe.wait_ge(s_attr[b], 32 * ((g - b) // 2 + 1) if known(g) else (g + (2 - b)) * 16)
                for k in parts:
                    r, w = (P, 4 * H) if k < 3 else (EF, H)
                    mm = M.matmul(p_bias[:, 4 * H * k:4 * H * k + w], attr_s[0:r, b, k, :], we4[0:r, 0:w],
                                  start=False, stop=k == 3)
                if 3 in parts:
                    mm.then_inc(s_bias, 1)

            def query(g, b, chunks):
                if 0 in chunks:
                    pe.wait_ge(s_qwin[b], 16 * ((g - b) // 2 + 1) if known(g) else (g + (2 - b)) * 8)
                for c in chunks:
                    t0, t1 = CH[c]
                    pe.wait_ge(s_st, NCH * g + c + 1)
                    if not (known(g) and g == 0 and c < 2):
                        pe.wait_ge(s_prod, NCH * g + c - 1)
                    for t in range(t0, t1):
                        mm = M.matmul(ps_q[c % 2][:, (t - t0) * D:(t - t0 + 1) * D], ST[:, b, t, :], qwin[:, b, :],
                                      start=True, stop=True)
                    mm.then_inc(s_qt, 1)

            def window_sums(g, b, bias_read=True):
                pe.wait_ge(s_wv, g + 1)
                for t in range(T):
                    mm = M.matmul(ps_r[:, 0:C + 1], S[:, b, t, :], wv[:, t, :], start=(t == 0), stop=(t == T - 1))
                mm.then_inc(s_agg, 1)
                if not (known(g) and g == 0):
                    pe.wait_ge(s_R, g)
                if bias_read:
                    pe.wait_ge(s_sc, g + 2)
                M.matmul(p_rc, shift[:, b, :], R[:, 1 - b, :], start=True, stop=True)
                pe.wait_ge(s_facd, g + 1)
                M.matmul(p_fb, isf[:], facd[:], start=True, stop=True).then_inc(s_rc, 1)

            def step(g, b, edges=True, nodes=True, more=True):
                if edges:
                    query(g, b, (2, 3))
                if nodes:
                    window_sums(g - 1, 1 - b, edges)
                if edges:
                    pe.wait_ge(s_oh, 2 * g + 2)
                    if not (known(g) and g == 0):
                        pe.wait_ge(s_od, g)
                    for t in range(T):
                        mm = M.matmul(ps_f[0:HI, 3 * D:3 * D + LO], oh_hi[:, b, :, t], oh_lo[:, b, :, t],
                                      start=(t == 0), stop=(t == T - 1))
                    mm.then_inc(s_hist, 1)
                    pe.wait_ge(s_v1, g + 1)
                    M.transpose(p_v1, f1[:, :, T - 1], ident[:]).then_inc(s_v1T, 1)
                if nodes:
                    pe.wait_ge(s_agn, g)
                    M.transpose(ps_f[:, 0:D], agn[:], ident[:]).then_inc(s_agTp, 1)
                if edges:
                    wait_apart(pe, s_cf, g + 1, (s_part, 1))
                    M.transpose(p_c1, c1[:, b, 0:P], ident[0:H, 0:H]).then_inc(s_cfT, 1)
                    if more:
                        turn(g + 1, 1 - b, (0,))
                        bias(g + 1, 1 - b, (0, 1))
                    pe.wait_ge(s_v2, g + 1)
                    M.transpose(p_v2, bx[:, :, 0], ident[:]).then_inc(s_v2T, 1)
                    if more:
                        turn(g + 1, 1 - b, (1,))
                    wait_apart(pe, s_cb, g + 1, (s_part, 1))
                    M.transpose(p_c2, c2[:, 1:P + 1], ident[0:H, 0:H]).then_inc(s_cbT, 1)
                if nodes:
                    pe.wait_ge(s_agT, g)
                    if not (known(g) and g == 1):
                        pe.wait_ge(s_x2, 2 * g - 2)
                    M.matmul(ps_f[:, D:2 * D], ones_row[:], bo_s[:], start=True, stop=False)
                    M.matmul(ps_f[:, D:2 * D], agT[:], wo_s[:], start=False, stop=True).then_inc(s_o, 1)
                if edges and more:
                    turn(g + 1, 1 - b, (2, 3))
                    query(g + 1, 1 - b, (0, 1))
                    bias(g + 1, 1 - b, (2, 3))

            pe.wait_ge(s_ber, T)
            bias(0, 0, (0, 1, 2, 3))
            turn(0, 0, (0, 1, 2, 3))
            query(0, 0, (0, 1))
            step(0, 0, nodes=False)
            step(1, 1)
            with pe.Fori(1, GROUPS // 2 - 1) as n:
                step(2 * n, 0)
                step(2 * n + 1, 1)
            step(GROUPS - 2, 0)
            step(GROUPS - 1, 1, more=False)
            step(GROUPS, 0, edges=False)

            def turn_node(i):
                pe.wait_ge(s_xn2, i + 1)
                if i >= 2:
                    pe.wait_ge(s_h2T, i - 1)
                M.transpose(turned[i % 2][:, 0:D], xn[:, i % 4, :], ident[:]).then_inc(s_xn2T, 1)

            turn_node(0)
            for i in range(NT):
                if i + 1 < NT:
                    turn_node(i + 1)
                pe.wait_ge(s_h2T, i + 1)
                M.matmul(h1_of(i), hT[:, i % 2, :], w1_s[:], start=True, stop=True).then_inc(s_h1, 1)

            def sums(g, b):
                pe.wait_ge(s_S1, 2 * g + 2)
                pe.wait_ge(s_g1[b], 16 * T * ((g - b) // 2 + 1) if known(g) else (g + (2 - b)) * (8 * T))
                bank = [ps_r, ps_c][b]
                for t in range(T):
                    M.matmul(bank[:, 0:D], S[:, b, t, :], kv[:, b, t, 0:D], start=(t == 0), stop=False)
                pe.wait_ge(s_R1, g + 1)
                M.matmul(bank[:, 0:D], shift[:, b, :], R[:, 1 - b, 0:D], start=False, stop=True).then_inc(s_agg1, 1)

            sums(0, 0)
            sums(1, 1)
            with pe.Fori(1, GROUPS // 2) as n:
                sums(2 * n, 0)
                sums(2 * n + 1, 1)


def kernel(**inputs):
    import concourse.bacc as _bacc
    from concourse.bass_utils import run_bass_kernel_spmd as _run

    a = {k: np.ascontiguousarray(v) for k, v in inputs.items()}

    def filled(v, rows, value=0):
        full = np.full((rows,) + v.shape[1:], value, v.dtype)
        full[:len(v)] = v
        return full

    def lanes(v):
        return v.reshape(GROUPS, P, T).transpose(1, 0, 2)

    src = filled(a["src"], GROUPS * GE, N)
    dst = filled(a["dst"], GROUPS * GE, N)
    runs = dst.reshape(GROUPS * P, T)
    before = np.concatenate([np.full(1, -1, np.int32), runs[:-1, T - 1]]).reshape(GROUPS, P).T
    after = np.concatenate([runs[1:, 0], np.full(1, -1, np.int32)]).reshape(GROUPS, P).T
    attr = filled(a["edge_attr_32"], GROUPS * GE).reshape(GROUPS, P, T * EF).transpose(0, 2, 1)
    rows, cols = np.indices((P, P)).astype(np.float32)
    ins = {
        "x": filled(a["x"], NPAD),
        "src_t": lanes(src).reshape(P, GROUPS * T),
        "dst_t": lanes(dst).reshape(P, GROUPS * T),
        "dst_before": before, "dst_after": after,
        "dst_first": dst[::GE][None, :],
        "attr": attr,
        "wqkv": np.concatenate([a["L0_gnn_Wq"], a["L0_gnn_Wk"], a["L0_gnn_Wv"]], axis=1),
        "bqkv": np.concatenate([a["L0_gnn_bq"], a["L0_gnn_bk"], a["L0_gnn_bv"]])[None, :],
        "we": a["L0_gnn_We"], "be": a["L0_gnn_be"][None, :],
        "wo": a["L0_gnn_Wo"], "bo": a["L0_gnn_bo"][None, :],
        "w1t": a["L1_gnn_W"].T, "b1": a["L1_gnn_b"][None, :],
        "ident_in": np.eye(P, dtype=np.float32), "iota_in": cols, "imj_in": rows - cols,
    }
    ins = {k: np.ascontiguousarray(v) for k, v in ins.items()}
    nc = _bacc.Bacc("TRN2", target_bir_lowering=False, num_devices=1)
    aps = {k: nc.dram_tensor(f"in_{k}", v.shape, mybir.dt.from_np(v.dtype), kind="ExternalInput").ap()
           for k, v in ins.items()}
    out = nc.dram_tensor("out", (N, D), F32, kind="ExternalOutput").ap()
    build(nc, out=out, **aps)
    r = _run(nc, [{f"in_{k}": v for k, v in ins.items()}], core_ids=[0])
    return r.results[0]["out"]
```

```python
from contextlib import ExitStack

import numpy as np

import concourse.bass as bass
from concourse import mybir

F32 = mybir.dt.float32
BF16 = mybir.dt.bfloat16
F16 = mybir.dt.float16
I32 = mybir.dt.int32
ALU = mybir.AluOpType
ACT = mybir.ActivationFunctionType
AX_X = mybir.AxisListType.X

P = 128
N = 3125
NT = 25
NPAD = NT * P
E = 53125
T = 13
GE = P * T
GROUPS = -(-E // GE)
H = 8
DH = 16
D = 128
EF = 32
C = H * (DH + 1)
HT = H * T
BIG = -1.0e30
EPS_LN = 1e-5
ATANH_MAX = 1.0 - 1e-5
SERIES_BELOW = 0.125
HI, LO = 50, 64
PCH = 5
CH = [(0, 4), (4, 8), (8, 12), (12, 13)]
NCH = len(CH)
TA = CH[2][1]


class Steps:

    def __init__(self, nc, eng, sem, base):
        self.nc, self.eng, self.sem, self.base, self.k = nc, eng, sem, base, 0

    def mark(self, ins):
        self.k += 1
        ins.then_inc(self.sem, 1)

    def sync(self):
        self.eng.wait_ge(self.sem, self.base + self.k)

    def then(self, ins):
        self.mark(ins)
        self.eng.wait_ge(self.sem, self.base + self.k)

    def check(self, total):
        assert self.k == total, (self.k, total)


def wait_apart(eng, sem, value, passed):
    if not isinstance(value, int):
        value = eng.to_reg(value)
    eng.wait_ge(*passed)
    eng.wait_ge(sem, value)


NA = 11
NB = 5
N1 = 15
DG = GROUPS // 2
W = 32
ROW0 = [min(max(round((t + 0.5) * P * N / E - W / 2), 0), P - W) for t in range(T)]
BANKS = [(0, 4), (4, 8), (8, 12), (12, 16), (16, 20), (20, 24), (24, NT)]
HALVES = [(0, 4), (4, 7)]
ROUND = 12582912.0
SC = H + C + 1
TILES = GROUPS * T
NE = 14
NN = 2
NE1 = 1
NN1 = 13


def rsqrt(link, y, v, t, meanwhile=None):
    nc_v = link.nc.vector

    def then(ins):
        link.mark(ins)
        if meanwhile:
            meanwhile()
        link.sync()

    then(nc_v.tensor_scalar(y.bitcast(I32), v.bitcast(I32), 1, None, ALU.logical_shift_right))
    then(nc_v.tensor_scalar(y.bitcast(I32), y.bitcast(I32), -1.0, float(0x5F3759DF), ALU.mult, ALU.add))
    for _ in range(3):
        then(nc_v.tensor_tensor(t, y, y, ALU.mult))
        then(nc_v.scalar_tensor_tensor(out=t, in0=t, scalar=-0.5, in1=v, op0=ALU.mult, op1=ALU.mult))
        then(nc_v.scalar_tensor_tensor(out=y, in0=t, scalar=1.5, in1=y, op0=ALU.add, op1=ALU.mult))


def build(nc, x, src_t, dst_t, dst_before, dst_after, dst_first, dst_run, src_run, attr, wqkv, bqkv, we, be, wo, bo, w1t, b1,
          ident_in, iota_in, imj_in, out):
    q_tab = nc.dram_tensor("q_tab", (NPAD, D), F32, kind="Internal").ap()
    kv_tab = nc.dram_tensor("kv_tab", (NPAD, 2 * D), F32, kind="Internal").ap()
    x2_tab = nc.dram_tensor("x2_tab", (NPAD, D + 1), F32, kind="Internal").ap()
    hs_tab = nc.dram_tensor("hs_tab", (NPAD, D), F32, kind="Internal").ap()
    dinv_tab = nc.dram_tensor("dinv_tab", (NPAD, 1), F32, kind="Internal").ap()
    od_tab = nc.dram_tensor("od_tab", (NPAD, 1), F32, kind="Internal").ap()
    state_tab = nc.dram_tensor("state_tab", (NPAD, SC), F32, kind="Internal").ap()
    sum_tab = nc.dram_tensor("sum_tab", (NPAD, D), F32, kind="Internal").ap()
    line_tab = nc.dram_tensor("line_tab", (2 * GROUPS, P), F32, kind="Internal").ap()

    with ExitStack() as ctx:
        def sb(name, shape, dt=F32):
            return ctx.enter_context(nc.sbuf_tensor(name, shape, dt))

        def pb(name, shape, dt=F32):
            return ctx.enter_context(nc.psum_tensor(name, shape, dt))

        def sem(name):
            return ctx.enter_context(nc.semaphore(name))

        ident = sb("ident", [P, P])
        iota = sb("iota", [P, P])
        imj = sb("imj", [P, P])
        iota_b = sb("iota_b", [P, P], BF16)
        ones_row = sb("ones_row", [1, P])
        zero_rows = sb("zero_rows", [NPAD - N, D + 1])
        wqkv_s = sb("wqkv_s", [P, 3 * D])
        bqkv_s = sb("bqkv_s", [P, 3 * D])
        we4 = sb("we4", [P, 4 * H])
        be_r = sb("be_r", [1, T, H])
        be_s = sb("be_s", [1, H])
        wo_s = sb("wo_s", [P, D])
        bo_s = sb("bo_s", [1, D])
        w1_s = sb("w1_s", [P, D])
        b1_s = sb("b1_s", [P, D])
        dst_i = sb("dst_i", [P, GROUPS, T], I32)
        src_i = sb("src_i", [P, GROUPS, T], I32)
        before_i = sb("before_i", [P, GROUPS], I32)
        after_i = sb("after_i", [P, GROUPS], I32)
        first_i = sb("first_i", [P, GROUPS], I32)
        first_f = sb("first_f", [P, GROUPS])
        base_f = sb("base_f", [P, GROUPS])
        base_i = sb("base_i", [P, GROUPS], I32)
        delta = sb("delta", [P, GROUPS])
        ofirst = sb("ofirst", [P, GROUPS])
        dloc = sb("dloc", [P, GROUPS, T])
        fwd_reset = sb("fwd_reset", [P, GROUPS, T])
        bwd_reset = sb("bwd_reset", [P, GROUPS, T])
        fwd_reset8 = sb("fwd_reset8", [P, GROUPS, H, T])
        bwd_reset8 = sb("bwd_reset8", [P, GROUPS, H, T])
        fwd_mask = sb("fwd_mask", [P, GROUPS, T])
        bwd_mask = sb("bwd_mask", [P, GROUPS, T])
        part_reset = sb("part_reset", [P, 2, GROUPS])
        part_rows = sb("part_rows", [2 * GROUPS, P])
        line = sb("line", [H, 2 * GROUPS, P])
        lo_f = sb("lo_f", [P, GROUPS, T], BF16)
        hi_f = sb("hi_f", [P, GROUPS, T], BF16)
        od_s = sb("od_s", [HI, LO])
        oh_hi = sb("oh_hi", [P, 2, HI, T], BF16)
        rep_hi = sb("rep_hi", [P, LO, T], BF16)
        nloc = sb("nloc", [P, GROUPS, T])
        oh_lo = sb("oh_lo", [P, 2, LO, T], BF16)
        xt = sb("xt", [P, NT, D + 1])
        xn = sb("xn", [P, 4, D])
        hT = sb("hT", [P, 2, D])
        st6 = sb("st6", [P, NT, 6])
        mv = sb("mv", [P, NT, 2])
        ve = sb("ve", [P, NT])
        rs_a = sb("rs_a", [P, NT])
        rs_t = sb("rs_t", [P, NT])
        qkv = sb("qkv", [P, 2, PCH, 3 * D])
        idx = sb("idx", [P, 2, T], I32)
        attr_s = sb("attr_s", [P, 2, 4, P])
        qwin = sb("qwin", [P, 2, D])
        xwin = sb("xwin", [P, 2, D + 1])
        kv = sb("kv", [P, 2, T, 2 * D])
        S = sb("S", [P, 2, T, P])
        ST = sb("ST", [P, 2, T, P])
        prod = sb("prod", [P, 2, 4, D])
        part_i = prod[:].rearrange("p a t d -> p (a t d)").bitcast(I32)[:, 0:GROUPS * T].rearrange("p (g t) -> p g t", t=T)
        sc = sb("sc", [P, H, T])
        f1 = sb("f1", [P, H, T])
        f2 = sb("f2", [P, H, T])
        bx = sb("bx", [P, H, T])
        tmp8 = sb("tmp8", [P, H, T])
        c1 = sb("c1", [H, 2, P + 1])
        c2 = sb("c2", [H, P + 1])
        z = sb("z", [P, H, T])
        wv = sb("wv", [P, T, C + 1])
        dfac = sb("dfac", [H, 1])
        fac = sb("fac", [H, 1])
        facd = sb("facd", [H, H])
        isf = sb("isf", [H, P])
        shift = sb("shift", [P, 2, P])
        R = sb("R", [P, 2, C + 1])
        fb = sb("fb", [P, H])
        rden = sb("rden", [P, H])
        agn = sb("agn", [P, D])
        agT = sb("agT", [P, D])
        x2 = sb("x2", [P, 2, D + 1])
        od_t = sb("od_t", [P, NT])
        v2 = sb("v2", [P, 2, NT])
        y2 = sb("y2", [P, 2, NT])
        t2 = sb("t2", [P, 2, NT])
        hsq = sb("hsq", [P, 2, D])
        ss_t = sb("ss_t", [P, NT])
        dinv_t = sb("dinv_t", [P, NT])
        sm = sb("sm", [P, 8, NT])
        rat = sb("rat", [P, NT])
        lnv = sb("lnv", [P, NT])
        y_out = sb("y_out", [P, 2, D])
        hs_t = qkv[:].rearrange("p a c d -> p (a c d)")[:, 0:NT * D].rearrange("p (n d) -> p n d", d=D)
        ss = sb("ss", [P, 1])
        sm1 = sb("sm1", [P, 4])
        th = sb("th", [P, 1])
        nrm = sb("nrm", [P, 1])

        src_run_i = sb("src_run_i", [P, DG, T], I32)
        run_row = sb("run_row", [P, DG, T])

        def place(tile, at, n=DG * T):
            return tile[:, at * DG * T:at * DG * T + n]

        def runs(words):
            return words.rearrange("p (g t) -> p g t", g=DG)

        early = S[:, 1].rearrange("p t e -> p (t e)")
        dst_run_i = runs(place(early, 1)).bitcast(I32)
        row0 = runs(place(early, 2))
        late = bwd_reset8[:].rearrange("p g h t -> p (g h t)")
        src_hi = runs(place(late, 0))
        src_key = runs(place(late, 1))
        iota_key = place(late, 2, NT * W // 2).bitcast(F16)
        zeros_b = place(late, 4, 256)[0:1, :].bitcast(BF16)
        oh_keys = [ST[:].rearrange("p a t e -> p (a t e)").bitcast(BF16),
                   fwd_reset8[:].rearrange("p g h t -> p (g h t)").bitcast(BF16)]

        def oh_key(t):
            at = t % 7 * NT * W
            return oh_keys[t // 7][:, at:at + NT * W]

        oh_node = wv[:].rearrange("p t c -> p (t c)").bitcast(BF16)[:, 0:T * P].rearrange("p (t k) -> p t k", t=T)
        counts = xt[:, :, 0:D]
        b1d = ST[:].rearrange("p a t e -> p (a t e)")[:, 0:NT * D].rearrange("p (n d) -> p n d", d=D)
        checks = S[:, 0].rearrange("p t e -> p (t e)")[:, 0:2 * GROUPS * T + GROUPS + 2 + 2 * DG * T]
        faults = sb("faults", [P, 1])
        faults_row = sb("faults_row", [1, P])
        orderly_i = sb("orderly_i", [1, 1], I32)
        e_query = kv[:, 0, 0, 0:D]
        e_kv = kv[:, 0, 1, :]
        e_old = kv[:, 0, 2, 0:SC]
        e_new = kv[:, 0, 3, 0:SC]
        e_prod = kv[:, 0, 4, 0:D]
        same_dst, same_src, far_dst, dst_rep, src_rep = [ST[:, 0, i, :] for i in range(5)]
        sc_rep = S[:, 0, 0:H, :]
        sc_seen = S[:, 1, 0:H, :]
        e_wv = wv[:, 0, :]
        e_attr = attr_s[0:EF, 0, 3, :]
        e_idx = sb("e_idx", [P, 2], I32)
        e_ids = sb("e_ids", [P, 2])
        e_sc, e_max = fb, rden
        e_exp = sb("e_exp", [P, 2, H])
        e_od = sb("e_od", [P, 2])

        ps_q = [pb(f"ps_q{i}", [P, 512]) for i in range(2)]
        ps_s = [pb(f"ps_s{i}", [P, 512]) for i in range(2)]
        ps_b = pb("ps_b", [P, 512])
        ps_r = pb("ps_r", [P, 512])
        ps_c = pb("ps_c", [P, 512])
        ps_f = pb("ps_f", [P, 512])
        p_bias = ps_c[:, 384:384 + HT]
        p_v1 = ps_b[0:H, 128:256]
        p_c1 = ps_b[:, 256:256 + H]
        p_v2 = ps_b[0:H, 288:416]
        p_c2 = ps_b[:, 416:416 + H]
        p_rc = ps_c[:, 0:C + 1]
        p_fb = ps_c[:, 256:256 + H]

        s_in = sem("s_in")
        s_w = sem("s_w")
        s_xin = [sem(f"s_xin{i}") for i in range(NT // PCH)]
        s_od_st = sem("s_od_st")
        s_line_st = sem("s_line_st")
        s_line = sem("s_line")
        s_pool0 = sem("s_pool0")
        s_dv0 = sem("s_dv0")
        s_reset = sem("s_reset")
        s_reset8 = sem("s_reset8")
        s_base = sem("s_base")
        s_part = sem("s_part")
        s_partT = sem("s_partT")
        s_partrow = sem("s_partrow")
        s_ber = sem("s_ber")
        s_zero = sem("s_zero")
        s_xn = sem("s_xn")
        s_xnT = sem("s_xnT")
        s_hT = sem("s_hT")
        s_qkvp = sem("s_qkvp")
        s_qkv = sem("s_qkv")
        s_tab = [sem(f"s_tab{i}") for i in range(2)]
        s_oh = sem("s_oh")
        s_hist = sem("s_hist")
        s_od = sem("s_od")
        s_idx = sem("s_idx")
        s_attr = [sem(f"s_attr{i}") for i in range(2)]
        s_qwin = [sem(f"s_qwin{i}") for i in range(2)]
        s_xwin = [sem(f"s_xwin{i}") for i in range(2)]
        s_kv = [[sem(f"s_kv{i}_{c}") for c in range(NCH)] for i in range(2)]
        s_S = sem("s_S")
        s_Sa = sem("s_Sa")
        s_Sab = sem("s_Sab")
        s_nloc = sem("s_nloc")
        s_stp = sem("s_stp")
        s_st = sem("s_st")
        s_qt = sem("s_qt")
        s_prod = sem("s_prod")
        s_bias = sem("s_bias")
        s_sc = sem("s_sc")
        s_v1 = sem("s_v1")
        s_v1T = sem("s_v1T")
        s_cf = sem("s_cf")
        s_cfT = sem("s_cfT")
        s_v2 = sem("s_v2")
        s_v2T = sem("s_v2T")
        s_cb = sem("s_cb")
        s_cbT = sem("s_cbT")
        s_dfac = sem("s_dfac")
        s_fac = sem("s_fac")
        s_facd = sem("s_facd")
        s_z = sem("s_z")
        s_p = sem("s_p")
        s_wv = sem("s_wv")
        s_agg = sem("s_agg")
        s_rc = sem("s_rc")
        s_R = sem("s_R")
        s_agn = sem("s_agn")
        s_agTp = sem("s_agTp")
        s_agT = sem("s_agT")
        s_o = sem("s_o")
        s_x2 = sem("s_x2")
        s_x2st = sem("s_x2st")
        s_xn2 = sem("s_xn2")
        s_xn2T = sem("s_xn2T")
        s_h2T = sem("s_h2T")
        s_h1 = sem("s_h1")
        s_nc = sem("s_nc")
        s_ln = sem("s_ln")
        s_dinv = sem("s_dinv")
        s_b1d = sem("s_b1d")
        s_hs = sem("s_hs")
        s_hsst = sem("s_hsst")
        s_dA = sem("s_dA")
        s_dB = sem("s_dB")
        s_dM = sem("s_dM")
        s_pad = sem("s_pad")
        s_x2l = [sem(f"s_x2l{i}") for i in range(NT // PCH)]
        s_odl = sem("s_odl")
        s_dvst = sem("s_dvst")
        s_faults = sem("s_faults")
        s_faultsT = sem("s_faultsT")
        s_orderly = sem("s_orderly")
        s_idx1 = sem("s_idx1")
        s_shift1 = sem("s_shift1")
        s_ohr = sem("s_ohr")
        s_cnt = sem("s_cnt")
        s_cntc = sem("s_cntc")
        s_xw1 = [sem(f"s_xw1{i}") for i in range(2)]
        s_g1 = [sem(f"s_g1{i}") for i in range(2)]
        s_S1 = sem("s_S1")
        s_agg1 = sem("s_agg1")
        s_R1 = sem("s_R1")
        s_ss1 = sem("s_ss1")
        s_zz1 = sem("s_zz1")
        s_norm1 = sem("s_norm1")
        s_th1 = sem("s_th1")
        s_y1 = sem("s_y1")
        s_yst = sem("s_yst")
        s_d1 = sem("s_d1")

        (s_e_blank, s_e_init, s_e_idx, s_e_attr, s_e_rep, s_e_repT, s_e_bias, s_e_sc, s_e_scT, s_e_z, s_e_exp, s_e_wv,
         s_e_sum, s_e_new, s_e_own) = (s_stp, s_st, s_qt, s_prod, s_bias, s_sc, s_v1, s_v1T, s_cf, s_cfT, s_v2, s_v2T,
                                       s_cb, s_cbT, s_dA)
        s_e_got = s_kv[0]
        s_e_put = s_attr
        (s_n_got, s_n_agn, s_n_agTp, s_n_agT, s_n_o, s_n_x2, s_n_put, s_n_own) = (
            s_xwin[0], s_agn, s_agTp, s_agT, s_o, s_x2, s_x2st, s_dB)
        (s_e_blank1, s_e_init1, s_e_idx1, s_e_put1, s_e_rep1, s_e_repT1, s_e_same1, s_e_sum1, s_e_new1, s_e_own1) = (
            s_dfac, s_fac, s_facd, s_z, s_p, s_wv, s_agg, s_agg1, s_rc, s_R)
        s_e_got1 = s_g1
        (s_n_got1, s_n_z1, s_n_ss1, s_n_norm1, s_n_th1, s_n_y1, s_n_put1, s_n_own1) = (
            s_xw1[0], s_zz1, s_ss1, s_norm1, s_th1, s_y1, s_yst, s_d1)

        block = ctx.enter_context(nc.Block())

        def node_rows(tab):
            return tab.rearrange("(p n) d -> p n d", n=NT)

        sum_banks = [ps_r, ps_q[0]]
        count_banks = [ps_q[0], ps_q[1], ps_s[0], ps_s[1], ps_b, ps_c, ps_f]
        turned = [ps_f, ps_c]

        def h1_of(i):
            bank = [ps_q[0], ps_q[1], ps_s[0], ps_s[1], ps_b, ps_r, turned[1]][i // 4]
            return bank[:, i % 4 * D:(i % 4 + 1) * D]

        def known(g):
            return isinstance(g, int)

        def orderly(eng, passed):
            wait_apart(eng, s_orderly, 1, passed)
            return eng.to_reg(eng.value_load(orderly_i[0:1, 0:1], min_val=0, max_val=1))

        @block.sync
        def _(sp):
            for c in range(NT // PCH):
                rows = slice(PCH * c, PCH * c + PCH)
                sp.dma_start(xt[:, rows, 0:D], node_rows(x)[:, rows, :]).then_inc(s_xin[c], 16)
            for dst, src in ((wqkv_s[:], wqkv), (bqkv_s[:], bqkv.partition_broadcast(P)), (ident[:], ident_in)):
                sp.dma_start(dst, src).then_inc(s_w, 16)
            for dst, src in ((iota[:], iota_in), (imj[:], imj_in),
                             (dst_i[:].rearrange("p g t -> p (g t)"), dst_t),
                             (src_i[:].rearrange("p g t -> p (g t)"), src_t),
                             (before_i[:], dst_before), (after_i[:], dst_after),
                             (first_i[:], dst_first.partition_broadcast(P)),
                             (dst_run_i, dst_run.rearrange("p (g t) -> p g t", g=DG)),
                             (src_run_i[:].rearrange("p g t -> p (g t)"), src_run),
                             (be_s[:], be), (wo_s[:], wo),
                             (bo_s[:], bo), (w1_s[:], w1t), (b1_s[:], b1.partition_broadcast(P))):
                sp.dma_start(dst, src).then_inc(s_in, 16)
            sp.wait_ge(s_pool0, 1)
            for k in range(4):
                sp.dma_start(we4[EF * k:EF * k + EF, H * k:H * k + H], we).then_inc(s_in, 16)
            for c in range(NT // PCH):
                sp.wait_ge(s_qkv, PCH * (c + 1))
                rows = slice(PCH * c, PCH * c + PCH)
                sp.dma_start(node_rows(q_tab)[:, rows, :], qkv[:, c % 2, :, 0:D]).then_inc(s_tab[c % 2], 16)
                sp.dma_start(node_rows(kv_tab)[:, rows, :], qkv[:, c % 2, :, D:3 * D]).then_inc(s_tab[c % 2], 16)
            sp.wait_ge(s_partrow, 2)
            sp.dma_start(line_tab, part_rows[:]).then_inc(s_line_st, 16)
            sp.wait_ge(s_line_st, 16)
            sp.dma_start(line[:], line_tab.partition_broadcast(H)).then_inc(s_line, 16)
            sp.wait_ge(s_base, 1)
            sp.wait_ge(s_tab[0], 32 * 3)
            sp.wait_ge(s_tab[1], 32 * 2)

            def base_of(g):
                return sp.value_load(base_i[0:1, g:g + 1] if known(g) else base_i[0:1, bass.ds(g, 1)],
                                     min_val=0, max_val=N - P)

            def load_edges(g, b):
                if not (known(g) and g < 2):
                    wait_apart(sp, s_bias, g - 1, (s_base, 1))
                sp.dma_start(attr_s[:, b, 0:3, :],
                             attr[bass.ds(g, 1), 0:3 * P, :].rearrange("o (k p) e -> p (o k) e", p=P)).then_inc(s_attr[b], 16)
                sp.dma_start(attr_s[0:EF, b, 3, :],
                             attr[bass.ds(g, 1), 3 * P:T * EF, :].rearrange("o p e -> p (o e)")).then_inc(s_attr[b], 16)
                w = base_of(g)
                if not (known(g) and g < 2):
                    wait_apart(sp, s_qt, NCH * (g - 1), (s_base, 1))
                sp.dma_start(qwin[:, b, :], q_tab[bass.ds(w, P), :]).then_inc(s_qwin[b], 16)

            def load_nodes(g, b):
                w = base_of(g)
                if not (known(g) and g < 2):
                    wait_apart(sp, s_x2, 2 * g - 2, (s_base, 1))
                sp.dma_start(xwin[:, b, 0:D], x[bass.ds(w, P), :]).then_inc(s_xwin[b], 16)

            def store_nodes(g, b):
                w = base_of(g)
                wait_apart(sp, s_x2, 2 * g + 2, (s_base, 1))
                if not (known(g) and g == 0):
                    wait_apart(sp, s_x2st, 16 * g, (s_base, 1))
                sp.dma_start(x2_tab[bass.ds(w, P), :], x2[:, b, :]).then_inc(s_x2st, 16)

            in_order = orderly(sp, (s_base, 1))
            with sp.If_eq(in_order, 1):
                load_edges(0, 0)
                load_edges(1, 1)
                load_nodes(0, 0)
                load_nodes(1, 1)
                sp.wait_ge(s_zero, 1)
                sp.dma_start(x2_tab[N:NPAD, :], zero_rows[:]).then_inc(s_pad, 16)
                with sp.Fori(1, GROUPS // 2) as n:
                    for b in range(2):
                        load_edges(2 * n + b, b)
                        store_nodes(2 * n + b - 2, b)
                        load_nodes(2 * n + b, b)
                store_nodes(GROUPS - 2, 0)
                sp.wait_ge(s_od, GROUPS)
                sp.dma_start(od_tab.rearrange("(h l) o -> h (l o)", l=LO), od_s[:]).then_inc(s_od_st, 16)
                sp.wait_ge(s_od_st, 16)
                sp.dma_start(od_t[:], od_tab.rearrange("(p n) o -> p (n o)", n=NT)).then_inc(s_odl, 16)
                store_nodes(GROUPS - 1, 1)
                sp.wait_ge(s_x2st, 16 * GROUPS)
                sp.wait_ge(s_pad, 16)
            with sp.Else():
                sp.wait_ge(s_e_blank, 3)
                for i in range(NT):
                    sp.dma_start(state_tab[P * i:P * i + P, :], e_new).then_inc(s_e_init, 16)
                sp.dma_start(od_tab.rearrange("(p n) o -> p (n o)", n=NT), od_t[:]).then_inc(s_e_init, 16)
                with sp.Fori(0, TILES) as k:
                    wait_apart(sp, s_e_idx, 2 * k + 2, (s_base, 1))
                    sp.dma_start(e_attr, attr.rearrange("g (t e) p -> (g t) e p", e=EF)[bass.ds(k, 1)]
                                 .rearrange("o e p -> e (o p)")).then_inc(s_e_attr, 16)
                sp.wait_ge(s_e_put[0], 16 * TILES)
                sp.wait_ge(s_e_put[1], 16 * TILES)
                with sp.Fori(0, NT) as n:
                    sp.dma_start(e_old, state_tab[bass.ds(n * P, P), :]).then_inc(s_n_got, 16)
                    sp.dma_start(e_kv[:, 0:D], x[bass.ds(n * P, P), :]).then_inc(s_n_got, 16)
                    wait_apart(sp, s_n_x2, 2 * n + 2, (s_base, 1))
                    sp.dma_start(x2_tab[bass.ds(n * P, P), :], x2[:, 0, :]).then_inc(s_n_put, 16)
                    wait_apart(sp, s_n_put, 16 * n + 16, (s_base, 1))
                sp.dma_start(od_t[:], od_tab.rearrange("(p n) o -> p (n o)", n=NT)).then_inc(s_odl, 16)

            for c in range(NT // PCH):
                rows = slice(PCH * c, PCH * c + PCH)
                sp.dma_start(xt[:, rows, :], node_rows(x2_tab)[:, rows, :]).then_inc(s_x2l[c], 16)
            sp.wait_ge(s_dinv, 1)
            sp.dma_start(dinv_tab.rearrange("(p n) o -> p (n o)", n=NT), dinv_t[:]).then_inc(s_dvst, 16)
            for c in range(NT // PCH):
                rows = slice(PCH * c, PCH * c + PCH)
                sp.wait_ge(s_hs, PCH * (c + 1))
                sp.dma_start(node_rows(hs_tab)[:, rows, :], hs_t[:, rows, :]).then_inc(s_hsst, 16)
            sp.wait_ge(s_dvst, 16)

            def load_window(g, b):
                w = base_of(g)
                if not (known(g) and g < 2):
                    wait_apart(sp, s_y1, g - 1, (s_base, 1))
                sp.dma_start(xwin[:, b, 0:D], x2_tab[bass.ds(w, P), 0:D]).then_inc(s_xw1[b], 16)
                sp.dma_start(xwin[:, b, D:D + 1], dinv_tab[bass.ds(w, P), :]).then_inc(s_xw1[b], 16)

            def store_out(g, b):
                w = base_of(g)
                wait_apart(sp, s_y1, g + 1, (s_base, 1))
                if not (known(g) and g == 0):
                    wait_apart(sp, s_yst, 16 * g, (s_base, 1))
                sp.dma_start(out[bass.ds(w, P), :], y_out[:, b, :]).then_inc(s_yst, 16)

            with sp.If_eq(in_order, 1):
                load_window(0, 0)
                load_window(1, 1)
                with sp.Fori(1, GROUPS // 2) as n:
                    for b in range(2):
                        store_out(2 * n + b - 2, b)
                        load_window(2 * n + b, b)
                store_out(GROUPS - 2, 0)
                store_out(GROUPS - 1, 1)
                sp.wait_ge(s_yst, 16 * GROUPS)
            with sp.Else():
                sp.wait_ge(s_e_blank1, 1)
                for i in range(NT):
                    sp.dma_start(sum_tab[P * i:P * i + P, :], e_new[:, 0:D]).then_inc(s_e_init1, 16)
                sp.wait_ge(s_e_put1, 16 * TILES)

                def node_tile(n, rows=P):
                    sp.dma_start(e_old[:, 0:D], sum_tab[bass.ds(n * P, P), :]).then_inc(s_n_got1, 16)
                    sp.dma_start(xwin[:, 0, 0:D], x2_tab[bass.ds(n * P, P), 0:D]).then_inc(s_n_got1, 16)
                    sp.dma_start(xwin[:, 0, D:D + 1], dinv_tab[bass.ds(n * P, P), :]).then_inc(s_n_got1, 16)
                    wait_apart(sp, s_n_y1, n + 1, (s_base, 1))
                    sp.dma_start(out[bass.ds(n * P, rows), :], y_out[0:rows, 0, :]).then_inc(s_n_put1, 16)
                    wait_apart(sp, s_n_put1, 16 * n + 16, (s_base, 1))

                with sp.Fori(0, NT - 1) as n:
                    node_tile(n)
                node_tile(NT - 1, N - (NT - 1) * P)


        @block.gpsimd
        def _(pool):
            nc.gpsimd.memset(we4[:], 0.0).then_inc(s_pool0, 1)
            pool.wait_ge(s_tab[0], 32 * 3)
            pool.wait_ge(s_tab[1], 32 * 2)

            def at(j):
                return bass.IndirectOffsetOnAxis(ap=e_idx[:, j:j + 1], axis=0)

            def gather(g, b):
                wait_apart(pool, s_idx, g + 1, (s_tab[0], 32 * 3))
                if not (known(g) and g < 2):
                    wait_apart(pool, s_wv, g - 1, (s_tab[0], 32 * 3))
                for c, (t0, t1) in enumerate(CH):
                    for t in range(t0, t1):
                        pool.indirect_dma_start(out=kv[:, b, t, :], out_offset=None, in_=kv_tab,
                                                in_offset=bass.IndirectOffsetOnAxis(ap=idx[:, b, t:t + 1], axis=0))\
                            .then_inc(s_kv[b][c], 16)

            in_order = orderly(pool, (s_tab[0], 32 * 3))
            with pool.If_eq(in_order, 1):
                gather(0, 0)
                gather(1, 1)
                with pool.Fori(1, GROUPS // 2) as n:
                    gather(2 * n, 0)
                    gather(2 * n + 1, 1)
            with pool.Else():
                pool.wait_ge(s_e_init, 16 * (NT + 1))
                with pool.Fori(0, TILES) as k:
                    wait_apart(pool, s_e_idx, 2 * k + 2, (s_tab[0], 32 * 3))
                    for i, (rows, tab, j) in enumerate(((e_query, q_tab, 0), (e_kv, kv_tab, 1), (e_old, state_tab, 0),
                                                        (e_od[:, 0:1], od_tab, 1))):
                        pool.indirect_dma_start(out=rows, out_offset=None, in_=tab, in_offset=at(j)).then_inc(s_e_got[i], 16)
                    wait_apart(pool, s_e_new, k + 1, (s_tab[0], 32 * 3))
                    pool.indirect_dma_start(out=state_tab, out_offset=at(0), in_=e_new, in_offset=None).then_inc(s_e_put[0], 16)
                    pool.indirect_dma_start(out=od_tab, out_offset=at(1), in_=e_od[:, 1:2], in_offset=None)\
                        .then_inc(s_e_put[1], 16)

            pool.wait_ge(s_hsst, 16 * (NT // PCH))

            def gather1(n, j):
                wait_apart(pool, s_idx1, n + 1, (s_tab[0], 32 * 3))
                if not (known(n) and n < 2):
                    wait_apart(pool, s_agg1, 2 * n - 2, (s_tab[0], 32 * 3))
                for t in range(T):
                    pool.indirect_dma_start(out=kv[:, j, t, 0:D], out_offset=None, in_=hs_tab,
                                            in_offset=bass.IndirectOffsetOnAxis(ap=idx[:, j, t:t + 1], axis=0))\
                        .then_inc(s_g1[j], 16)

            with pool.If_eq(in_order, 1):
                gather1(0, 0)
                gather1(1, 1)
                with pool.Fori(1, DG // 2) as m:
                    gather1(2 * m, 0)
                    gather1(2 * m + 1, 1)
            with pool.Else():
                pool.wait_ge(s_e_init1, 16 * NT)
                with pool.Fori(0, TILES) as k:
                    wait_apart(pool, s_e_idx1, 2 * k + 2, (s_tab[0], 32 * 3))
                    pool.indirect_dma_start(out=e_kv[:, 0:D], out_offset=None, in_=hs_tab, in_offset=at(1)).then_inc(s_e_got1[0], 16)
                    pool.indirect_dma_start(out=e_old[:, 0:D], out_offset=None, in_=sum_tab, in_offset=at(0))\
                        .then_inc(s_e_got1[1], 16)
                    wait_apart(pool, s_e_new1, k + 1, (s_tab[0], 32 * 3))
                    pool.indirect_dma_start(out=sum_tab, out_offset=at(0), in_=e_new[:, 0:D], in_offset=None)\
                        .then_inc(s_e_put1, 16)

        @block.vector
        def _(dve):
            V = nc.vector
            pre = Steps(nc, dve, s_dv0, 0)

            pre.mark(V.memset(ones_row[:], 1.0))
            for t in range(T):
                pre.mark(V.memset(row0[:, :, t:t + 1], float(ROW0[t])))
            V.memset(zero_rows[:], 0.0).then_inc(s_zero, 1)
            pre.mark(V.memset(c1[:], BIG))
            pre.mark(V.memset(c2[:], BIG))
            pre.mark(V.memset(R[:], 0.0))
            pre.mark(V.memset(wv[:], 1.0))

            def set_idx(g, b, ready):
                V.tensor_copy(idx[:, b, :], src_i[:, g, :] if known(g) else
                              src_i[:, bass.ds(g, 1), :].rearrange("p g t -> p (g t)")).then_inc(ready, 1)

            def stats(st, arrived):
                for c in range(NT // PCH):
                    dve.wait_ge(arrived[c], 16)
                    for i in range(PCH * c, PCH * c + PCH):
                        st.mark(V.bn_stats(st6[:, i, :], xt[:, i, 0:D]))
                    if c:
                        for i in range(PCH * (c - 1), PCH * c):
                            st.mark(V.bn_aggr(mv[:, i, :], st6[:, i, :]))
                    st.sync()
                for i in range(NT - PCH, NT):
                    st.mark(V.bn_aggr(mv[:, i, :], st6[:, i, :]))
                st.sync()

            stats(pre, s_xin)
            pre.then(V.tensor_scalar(ve[:], mv[:, :, 1], EPS_LN, None, ALU.add))
            rsqrt(pre, rs_a[:], ve[:], rs_t[:])
            dve.wait_ge(s_w, 16 * 3)
            pre.mark(V.tensor_scalar(wqkv_s[:, 0:D], wqkv_s[:, 0:D], DH ** -0.5, None, ALU.mult))
            pre.then(V.tensor_scalar(bqkv_s[:, 0:D], bqkv_s[:, 0:D], DH ** -0.5, None, ALU.mult))

            def norm_tile(i):
                if i >= 4:
                    dve.wait_ge(s_xnT, i - 3)
                V.tensor_scalar(xn[:, i % 4, :], xt[:, i, 0:D], mv[:, i, 0:1], rs_a[:, i:i + 1],
                                ALU.subtract, ALU.mult).then_inc(s_xn, 1)

            def qkv_tile(i):
                c = i // PCH
                dve.wait_ge(s_qkvp, i + 1)
                if i % PCH == 0 and c >= 2:
                    dve.wait_ge(s_tab[c % 2], 32 * (c // 2))
                V.tensor_tensor(qkv[:, c % 2, i % PCH, :], ps_q[i % 2][:, 0:3 * D], bqkv_s[:],
                                ALU.add).then_inc(s_qkv, 1)

            for i in range(3):
                norm_tile(i)
            dve.wait_ge(s_in, 16 * 18)
            set_idx(0, 0, s_idx)
            set_idx(1, 1, s_idx)
            GT3 = [P, GROUPS, T]
            c0, c1_, c2_, c3 = 0, GROUPS * (T - 1), GROUPS * T, 2 * GROUPS * T
            c4, c5 = c3 + GROUPS + 2, c3 + GROUPS + 2 + DG * T

            def structure(i):
                pre.sync()
                if i == 2:
                    pre.mark(V.tensor_copy(first_f[:], first_i[:]))
                if i == 3:
                    pre.mark(V.tensor_scalar(base_f[:], first_f[:], float(N - P), None, ALU.min))
                    pre.mark(V.memset(delta[:, 0:1], 0.0))
                if i == 4:
                    V.tensor_copy(base_i[:], base_f[:]).then_inc(s_base, 1)
                    pre.mark(V.tensor_tensor(delta[:, 1:], base_f[:, 1:], base_f[:, :-1], ALU.subtract))
                    pre.mark(V.tensor_tensor(run_row[:], dst_run_i, base_f[:, ::2].unsqueeze(2).to_broadcast([P, DG, T]),
                                             ALU.subtract))
                if i == 5:
                    pre.mark(V.tensor_tensor(dloc[:], dst_i[:], base_f[:].unsqueeze(2).to_broadcast(GT3), ALU.subtract))
                if i == 6:
                    pre.mark(V.tensor_tensor(run_row[:], run_row[:], row0, ALU.subtract))
                    pre.mark(V.tensor_scalar(fwd_mask[:], dst_i[:], float(N), None, ALU.is_lt))
                if i == 7:
                    pre.mark(V.tensor_tensor(checks[:, c0:c1_].rearrange("p (g t) -> p g t", g=GROUPS),
                                             dst_i[:, :, 1:], dst_i[:, :, :-1], ALU.is_lt))
                if i == 8:
                    pre.mark(V.tensor_tensor(checks[:, c1_:c2_], dst_i[:, :, 0], before_i[:], ALU.is_lt))
                    pre.mark(V.tensor_scalar(checks[:, c4:c5].rearrange("p (g t) -> p g t", g=DG), run_row[:], float(W - 1),
                                             None, ALU.is_gt))
                if i == 9:
                    pre.mark(V.scalar_tensor_tensor(out=checks[:, c2_:c3].rearrange("p (g t) -> p g t", g=GROUPS),
                                                    in0=dloc[:], scalar=float(P - 1), in1=fwd_mask[:], op0=ALU.is_gt,
                                                    op1=ALU.mult))
                if i == 10:
                    pre.mark(V.tensor_scalar(checks[:, c5:].rearrange("p (g t) -> p g t", g=DG), run_row[:], 0.0, None,
                                             ALU.is_lt))
                    pre.mark(V.tensor_scalar(checks[:, c3:c3 + GROUPS], delta[:], float(P), None, ALU.is_gt))
                    pre.mark(V.tensor_scalar(checks[:, c3 + GROUPS:c3 + GROUPS + 1], base_f[:, 0:1], 0.0, None, ALU.is_gt))
                    pre.mark(V.tensor_scalar(checks[:, c3 + GROUPS + 1:c4], base_f[:, GROUPS - 1:], float(N - P), None,
                                             ALU.is_lt))
                if i == 11:
                    V.tensor_reduce(faults[:], checks, AX_X, ALU.add).then_inc(s_faults, 1)
                if i == 20:
                    dve.wait_ge(s_faultsT, 1)
                    pre.then(V.tensor_reduce(faults_row[:, 0:1], ps_b[0:1, 0:P], AX_X, ALU.add))
                    V.tensor_scalar(orderly_i[:], faults_row[:, 0:1], 0.5, None, ALU.is_lt).then_inc(s_orderly, 1)

            for i in range(NT):
                if i + 3 < NT:
                    norm_tile(i + 3)
                qkv_tile(i)
                structure(i)

            pre.mark(V.tensor_tensor(ofirst[:], first_f[:], base_f[:], ALU.subtract))
            pre.mark(V.tensor_tensor(part_reset[:, 0, :], dst_i[:, :, T - 1], before_i[:], ALU.not_equal))
            pre.mark(V.tensor_tensor(part_reset[:, 1, :], dst_i[:, :, 0], after_i[:], ALU.not_equal))
            pre.mark(V.tensor_tensor(fwd_reset[:, :, 1:], dst_i[:, :, 1:], dst_i[:, :, :-1], ALU.not_equal))
            pre.mark(V.memset(fwd_reset[:, :, 0:1], 1.0))
            pre.mark(V.tensor_tensor(bwd_reset[:, :, :-1], dst_i[:, :, 1:], dst_i[:, :, :-1], ALU.not_equal))
            pre.mark(V.memset(bwd_reset[:, :, T - 1:T], 1.0))
            pre.mark(V.tensor_tensor(fwd_mask[:], dst_i[:], before_i[:].unsqueeze(2).to_broadcast(GT3), ALU.not_equal))
            pre.then(V.tensor_tensor(bwd_mask[:], dst_i[:], after_i[:].unsqueeze(2).to_broadcast(GT3), ALU.not_equal))
            V.tensor_scalar(nloc[:], dloc[:], -1.0, None, ALU.mult).then_inc(s_nloc, 1)
            V.tensor_scalar(part_reset[:], part_reset[:], BIG, None, ALU.mult).then_inc(s_part, 1)
            V.tensor_scalar(fwd_reset[:], fwd_reset[:], BIG, None, ALU.mult).then_inc(s_reset, 1)
            V.tensor_scalar(bwd_reset[:], bwd_reset[:], BIG, None, ALU.mult).then_inc(s_reset, 1)
            pre.mark(V.tensor_scalar(fwd_mask[:], fwd_mask[:], BIG, None, ALU.mult))
            pre.then(V.tensor_scalar(bwd_mask[:], bwd_mask[:], BIG, None, ALU.mult))

            def col(tile, g):
                return tile[:, g:g + 1] if known(g) else tile[:, bass.ds(g, 1)]

            def col3(tile, g):
                return (tile[:, g:g + 1, :] if known(g) else tile[:, bass.ds(g, 1), :]).rearrange("p g t -> p (g t)")

            def shift_matrix(g, b, used, ready):
                if not (known(g) and g < 2):
                    dve.wait_ge(used, g - 1)
                V.tensor_scalar(shift[:, b, :], imj[:], col(delta, g), None, ALU.is_equal).then_inc(ready, 1)

            def edge_one_hots(g, b, ready, t0):
                V.tensor_tensor(S[:, b, t0:T, :], col3(dloc, g)[:, t0:T].unsqueeze(2).to_broadcast([P, T - t0, P]),
                                iota[:].unsqueeze(1).to_broadcast([P, T - t0, P]), ALU.is_equal).then_inc(ready, 1)

            shift_matrix(0, 0, None, s_S)
            edge_one_hots(0, 0, s_S, TA)
            dve.wait_ge(s_partT, 1)
            V.tensor_copy(part_rows[0:GROUPS, :], ps_b[0:GROUPS, 0:P]).then_inc(s_partrow, 1)
            V.tensor_copy(part_rows[GROUPS:, :], ps_b[GROUPS:2 * GROUPS, 0:P][:, ::-1]).then_inc(s_partrow, 1)
            pre.mark(V.tensor_copy(iota_b[:], iota[:]))
            pre.mark(V.tensor_copy(rep_hi[:], iota[:, 0:LO].unsqueeze(2).to_broadcast([P, LO, T])))
            pre.then(V.tensor_scalar(part_i, src_i[:], 6, None, ALU.logical_shift_right))
            pre.then(V.tensor_copy(hi_f[:], part_i))
            pre.then(V.tensor_scalar(part_i, src_i[:], LO - 1, None, ALU.bitwise_and))
            pre.then(V.tensor_copy(lo_f[:], part_i))
            pre.mark(V.memset(od_s[:], 0.0))
            dve.wait_ge(s_reset8, 2 * H)
            dve.wait_ge(s_line, 16)

            def source_one_hots(g, b, parts=(0, 1)):
                if 0 in parts and not (known(g) and g < 2):
                    dve.wait_ge(s_hist, g - 1)
                for i in parts:
                    oh, part, m = ((oh_hi, hi_f, HI), (oh_lo, lo_f, LO))[i]
                    V.tensor_tensor(oh[:, b], col3(part, g).unsqueeze(1).to_broadcast([P, m, T]),
                                    rep_hi[:, 0:m, :], ALU.is_equal).then_inc(s_oh, 1)

            def add_counts(g):
                dve.wait_ge(s_hist, g + 1)
                if not (known(g) and g == 0):
                    dve.wait_ge(s_od, g)
                V.tensor_tensor(od_s[:], od_s[:], ps_f[0:HI, 3 * D:3 * D + LO], ALU.add).then_inc(s_od, 1)

            def flat(tile):
                return tile[:].rearrange("p h t -> p (h t)")

            def reset8(tile, g):
                return (tile[:, g:g + 1] if known(g) else tile[:, bass.ds(g, 1)]).rearrange("p g h t -> p (g h t)")

            def lines(g):
                return (line[:, g:g + 1, :] if known(g) else line[:, bass.ds(g, 1), :]).rearrange("p g t -> p (g t)")

            def mask8(tile, g):
                return col3(tile, g).unsqueeze(1).to_broadcast([P, H, T])

            def scores(g, b, st, more):
                def product(c):
                    t0, t1 = CH[c]
                    w = t1 - t0
                    dve.wait_ge(s_kv[b][c], 16 * w * ((g - b) // 2 + 1) if known(g) else (g + (2 - b)) * (8 * w))
                    dve.wait_ge(s_qt, NCH * g + c + 1)
                    if c >= 2:
                        st.sync()
                    V.tensor_tensor(prod[:, c % 2, 0:w, :], kv[:, b, t0:t1, 0:D],
                                    ps_q[c % 2][:, 0:w * D].rearrange("p (t d) -> p t d", d=D), ALU.mult).then_inc(s_prod, 1)

                def per_head(c):
                    t0, t1 = CH[c]
                    dve.wait_ge(s_prod, NCH * g + c + 1)
                    st.mark(V.tensor_reduce(sc[:, :, t0:t1].rearrange("p h t -> p t h"),
                                            prod[:, c % 2, 0:t1 - t0, :].rearrange("p t (h d) -> p t h d", d=DH),
                                            AX_X, ALU.add))

                product(0)
                for c in range(NCH):
                    if c + 1 < NCH:
                        product(c + 1)
                    per_head(c)
                st.sync()
                dve.wait_ge(s_bias, g + 1)
                V.tensor_tensor(sc[:], sc[:], p_bias.rearrange("p (t h) -> p h t", h=H), ALU.add).then_inc(s_sc, 1)
                if more:
                    source_one_hots(g + 1, 1 - b, (0,))
                dve.wait_ge(s_sc, g + 1)
                V.tensor_tensor_scan(out=flat(f1), data0=reset8(fwd_reset8, g), data1=flat(sc), initial=BIG,
                                     op0=ALU.add, op1=ALU.max).then_inc(s_v1, 1)
                if more:
                    source_one_hots(g + 1, 1 - b, (1,))

            def scan_partitions(g, b, st):
                dve.wait_ge(s_v1T, g + 1)
                if not (known(g) and g < 2):
                    dve.wait_ge(s_cfT, g - 1)
                st.mark(V.tensor_copy(c1[:, b, 0:1], c1[:, 1 - b, P:P + 1]))
                V.tensor_tensor_scan(out=c1[:, b, 1:P + 1], data0=lines(g), data1=p_v1, initial=c1[:, 1 - b, P:P + 1],
                                     op0=ALU.add, op1=ALU.max).then_inc(s_cf, 1)

            def backward(g, b, st):
                dve.wait_ge(s_cfT, g + 1)
                st.then(V.tensor_tensor(tmp8[:], mask8(fwd_mask, g), p_c1.unsqueeze(2).to_broadcast([P, H, T]), ALU.add))
                st.then(V.tensor_tensor(f2[:], f1[:], tmp8[:], ALU.max))
                V.tensor_tensor_scan(out=flat(bx)[:, ::-1], data0=reset8(bwd_reset8, g), data1=flat(f2)[:, ::-1],
                                     initial=BIG, op0=ALU.add, op1=ALU.max).then_inc(s_v2, 1)

            def first_row(g, st):
                if not (known(g) and g == 0):
                    dve.wait_ge(s_rc, g)
                st.mark(V.tensor_scalar(isf[:], iota[0:H, :], col(ofirst[0:H], g), None, ALU.is_equal))

            def scan_partitions_back(g, b, st):
                dve.wait_ge(s_v2T, g + 1)
                V.tensor_tensor_scan(out=c2[:, 0:P][:, ::-1], data0=lines(g + GROUPS), data1=p_v2[:, ::-1],
                                     initial=BIG, op0=ALU.add, op1=ALU.max).then_inc(s_cb, 1)
                dve.wait_ge(s_cb, g + 1)
                st.then(V.tensor_tensor(dfac[:], c1[:, b, 0:1], c2[:, 0:1], ALU.subtract))
                V.tensor_scalar(dfac[:], dfac[:], 0.0, None, ALU.min).then_inc(s_dfac, 1)

            def shifted(g, b, st):
                dve.wait_ge(s_cbT, g + 1)
                st.then(V.tensor_tensor(tmp8[:], mask8(bwd_mask, g), p_c2.unsqueeze(2).to_broadcast([P, H, T]), ALU.add))
                st.then(V.tensor_tensor(tmp8[:], bx[:], tmp8[:], ALU.max))
                V.tensor_tensor(z[:], sc[:], tmp8[:], ALU.subtract).then_inc(s_z, 1)

            def factor(g):
                dve.wait_ge(s_fac, g + 1)
                V.scalar_tensor_tensor(out=facd[:], in0=ident[0:H, 0:H], scalar=fac[:], in1=ident[0:H, 0:H],
                                       op0=ALU.mult, op1=ALU.subtract).then_inc(s_facd, 1)

            def weigh(g, b):
                dve.wait_ge(s_p, g + 1)
                w4 = wv[:, :, 0:C].rearrange("p t (h e) -> p t h e", e=DH + 1)
                V.tensor_tensor(w4[:, :, :, 0:DH], kv[:, b, :, D:2 * D].rearrange("p t (h d) -> p t h d", d=DH),
                                w4[:, :, :, DH:DH + 1].to_broadcast([P, T, H, DH]), ALU.mult).then_inc(s_wv, 1)

            def combine(g, b, st, edges, more, next_st):
                dve.wait_ge(s_rc, g + 1)
                st.mark(V.tensor_scalar(fb[:], p_fb, 1.0, None, ALU.add))
                st.mark(V.tensor_copy(R[:, b, C:C + 1], p_rc[:, C:C + 1]))
                if more:
                    shift_matrix(g + 2, b, s_rc, s_S)
                st.sync()
                st.mark(V.tensor_tensor(R[:, b, 0:C].rearrange("p (h e) -> p h e", h=H),
                                        p_rc[:, 0:C].rearrange("p (h e) -> p h e", h=H),
                                        fb[:].unsqueeze(2).to_broadcast([P, H, DH + 1]), ALU.mult))
                if more:
                    edge_one_hots(g + 2, b, s_S, TA)
                st.sync()
                V.tensor_tensor(R[:, b, :], R[:, b, :], ps_r[:, 0:C + 1], ALU.add).then_inc(s_R, 1)
                if edges:
                    scan_partitions(g + 1, 1 - b, next_st)
                dve.wait_ge(s_R, g + 1)
                r3 = R[:, b, 0:C].rearrange("p (h e) -> p h e", h=H)
                st.mark(V.tensor_scalar(rden[:].unsqueeze(2), r3[:, :, DH:DH + 1], 1e-10, None, ALU.add))
                if edges:
                    first_row(g + 1, next_st)
                st.sync()
                st.then(V.reciprocal(rden[:], rden[:]))
                V.tensor_tensor(agn[:].rearrange("p (h d) -> p h d", h=H), r3[:, :, 0:DH],
                                rden[:].unsqueeze(2).to_broadcast([P, H, DH]), ALU.mult).then_inc(s_agn, 1)

            def new_rows(g, b):
                dve.wait_ge(s_o, g + 1)
                dve.wait_ge(s_xwin[b], 16 * ((g - b) // 2 + 1) if known(g) else (g + (2 - b)) * 8)
                if not (known(g) and g < 2):
                    dve.wait_ge(s_x2st, 16 * (g - 1))
                V.tensor_tensor(x2[:, b, 0:D], ps_f[:, D:2 * D], xwin[:, b, 0:D], ALU.add).then_inc(s_x2, 1)
                V.tensor_copy(x2[:, b, D:D + 1], R[:, b, C:C + 1]).then_inc(s_x2, 1)

            def square_norm(i):
                dve.wait_ge(s_xn2, i + 1)
                M_.mark(V.scalar_tensor_tensor(out=hsq[:, i % 2, :], in0=xn[:, i % 4, :], scalar=0.0, in1=xn[:, i % 4, :],
                                               op0=ALU.max, op1=ALU.mult, accum_out=ss_t[:, i:i + 1]))

            def step(g, b, edges=True, nodes=True, more=True, far=True):
                A = Steps(nc, dve, s_dA, NA * g)
                B = Steps(nc, dve, s_dB, NB * (g - 1))
                if edges:
                    scores(g, b, A, more)
                if nodes:
                    combine(g - 1, 1 - b, B, edges, edges and more, A)
                    B.check(NB)
                else:
                    scan_partitions(g, b, A)
                    first_row(g, A)
                    shift_matrix(g + 1, 1 - b, s_rc, s_S)
                    edge_one_hots(g + 1, 1 - b, s_S, TA)
                if edges:
                    backward(g, b, A)
                    if far:
                        set_idx(g + 2, b, s_idx)
                    scan_partitions_back(g, b, A)
                    shifted(g, b, A)
                if nodes:
                    new_rows(g - 1, 1 - b)
                if edges:
                    add_counts(g)
                    factor(g)
                    weigh(g, b)
                    A.check(NA)

            source_one_hots(0, 0)
            def tile_ids(k, st, idx_ready, rep_ready):
                V.tensor_copy(e_idx[:, 0:1], dst_i[:].rearrange("p g t -> p (g t)")[:, bass.ds(k, 1)]).then_inc(idx_ready, 1)
                V.tensor_copy(e_idx[:, 1:2], src_i[:].rearrange("p g t -> p (g t)")[:, bass.ds(k, 1)]).then_inc(idx_ready, 1)
                dve.wait_ge(idx_ready, 2 * k + 2)
                st.then(V.tensor_copy(e_ids[:], e_idx[:]))
                V.tensor_scalar(dst_rep, iota[:], 0.0, e_ids[:, 0:1], ALU.mult, ALU.add).then_inc(rep_ready, 1)
                V.tensor_scalar(src_rep, iota[:], 0.0, e_ids[:, 1:2], ALU.mult, ALU.add).then_inc(rep_ready, 1)

            def edge_tile(k):
                st = Steps(nc, dve, s_e_own, NE * k)
                tile_ids(k, st, s_e_idx, s_e_rep)
                dve.wait_ge(s_e_repT, k + 1)
                st.mark(V.tensor_scalar(same_dst, ps_s[0][:, 0:P], e_ids[:, 0:1], None, ALU.is_equal))
                st.then(V.tensor_scalar(same_src, ps_s[0][:, P:2 * P], e_ids[:, 1:2], None, ALU.is_equal))
                st.mark(V.tensor_scalar(far_dst, same_dst, 1.0, -BIG, ALU.subtract, ALU.mult))
                for s_got in s_e_got:
                    dve.wait_ge(s_got, 16 * k + 16)
                st.then(V.tensor_tensor(e_prod, e_query, e_kv[:, 0:D], ALU.mult))
                st.then(V.tensor_reduce(e_sc[:], e_prod.rearrange("p (h d) -> p h d", d=DH), AX_X, ALU.add))
                dve.wait_ge(s_e_bias, k + 1)
                st.then(V.tensor_tensor(e_sc[:], e_sc[:], ps_b[:, 0:H], ALU.add))
                V.tensor_copy(sc_rep, e_sc[:].unsqueeze(2).to_broadcast([P, H, P])).then_inc(s_e_sc, 1)
                dve.wait_ge(s_e_scT, k + 1)
                for i in range(2):
                    st.then(V.tensor_tensor(sc_seen[:, 4 * i:4 * i + 4, :], ps_q[i][:].rearrange("p (h e) -> p h e", e=P),
                                            far_dst.unsqueeze(1).to_broadcast([P, 4, P]), ALU.add))
                st.then(V.tensor_reduce(e_max[:], sc_seen, AX_X, ALU.max))
                st.then(V.tensor_tensor(e_new[:, 0:H], e_old[:, 0:H], e_max[:], ALU.max))
                V.tensor_tensor(e_exp[:, 0, :], e_old[:, 0:H], e_new[:, 0:H], ALU.subtract).then_inc(s_e_z, 1)
                V.tensor_tensor(e_exp[:, 1, :], e_sc[:], e_new[:, 0:H], ALU.subtract).then_inc(s_e_z, 1)
                dve.wait_ge(s_e_exp, k + 1)
                w3 = e_wv[:, 0:C].rearrange("p (h e) -> p h e", h=H)
                old3 = e_old[:, H:H + C].rearrange("p (h e) -> p h e", h=H)
                new3 = e_new[:, H:H + C].rearrange("p (h e) -> p h e", h=H)
                V.tensor_copy(w3[:, :, DH:DH + 1], e_exp[:, 1, :].unsqueeze(2)).then_inc(s_e_wv, 1)
                V.tensor_tensor(w3[:, :, 0:DH], e_kv[:, D:2 * D].rearrange("p (h d) -> p h d", h=H),
                                e_exp[:, 1, :].unsqueeze(2).to_broadcast([P, H, DH]), ALU.mult).then_inc(s_e_wv, 1)
                st.then(V.tensor_tensor(new3, old3, e_exp[:, 0, :].unsqueeze(2).to_broadcast([P, H, DH + 1]), ALU.mult))
                dve.wait_ge(s_e_sum, k + 1)
                st.mark(V.tensor_tensor(e_new[:, H:H + C], e_new[:, H:H + C], ps_r[:, 0:C], ALU.add))
                st.mark(V.tensor_tensor(e_new[:, H + C:SC], e_old[:, H + C:SC], ps_r[:, C:C + 1], ALU.add))
                st.sync()
                V.tensor_tensor(e_od[:, 1:2], e_od[:, 0:1], ps_r[:, C + 1:C + 2], ALU.add).then_inc(s_e_new, 1)
                dve.wait_ge(s_e_put[0], 16 * k + 16)
                dve.wait_ge(s_e_put[1], 16 * k + 16)
                st.check(NE)

            def node_tile(n):
                st = Steps(nc, dve, s_n_own, NN * n)
                dve.wait_ge(s_n_got, 32 * n + 32)
                old3 = e_old[:, H:H + C].rearrange("p (h e) -> p h e", h=H)
                st.then(V.tensor_scalar(rden[:].unsqueeze(2), old3[:, :, DH:DH + 1], 1e-10, None, ALU.add))
                st.then(V.reciprocal(rden[:], rden[:]))
                V.tensor_tensor(agn[:].rearrange("p (h d) -> p h d", h=H), old3[:, :, 0:DH],
                                rden[:].unsqueeze(2).to_broadcast([P, H, DH]), ALU.mult).then_inc(s_n_agn, 1)
                dve.wait_ge(s_n_o, n + 1)
                V.tensor_tensor(x2[:, 0, 0:D], ps_f[:, D:2 * D], e_kv[:, 0:D], ALU.add).then_inc(s_n_x2, 1)
                V.tensor_copy(x2[:, 0, D:D + 1], e_old[:, H + C:SC]).then_inc(s_n_x2, 1)
                st.check(NN)

            def edge_tile1(k):
                st = Steps(nc, dve, s_e_own1, NE1 * k)
                tile_ids(k, st, s_e_idx1, s_e_rep1)
                dve.wait_ge(s_e_repT1, k + 1)
                V.tensor_scalar(same_dst, ps_s[0][:, 0:P], e_ids[:, 0:1], None, ALU.is_equal).then_inc(s_e_same1, 1)
                for s_got in s_e_got1:
                    dve.wait_ge(s_got, 16 * k + 16)
                dve.wait_ge(s_e_sum1, k + 1)
                V.tensor_tensor(e_new[:, 0:D], e_old[:, 0:D], ps_r[:, 0:D], ALU.add).then_inc(s_e_new1, 1)
                dve.wait_ge(s_e_put1, 16 * k + 16)

            def node_tile1(n):
                st = Steps(nc, dve, s_n_own1, NN1 * n)
                v_, y_, t_, a_ = [sm1[:, i:i + 1] for i in range(4)]
                dve.wait_ge(s_n_got1, 48 * n + 48)
                V.tensor_scalar(agn[:], e_old[:, 0:D], xwin[:, 0, D:D + 1], None, ALU.mult).then_inc(s_n_z1, 1)
                dve.wait_ge(s_n_ss1, n + 1)
                st.then(V.tensor_scalar(v_, ss[:], 1e-30, None, ALU.max))
                rsqrt(st, y_, v_, t_)
                V.tensor_tensor(nrm[:], ss[:], y_, ALU.mult).then_inc(s_n_norm1, 1)
                dve.wait_ge(s_n_th1, n + 1)
                st.then(V.tensor_scalar(a_, y_, 1e15, th[:], ALU.min, ALU.mult))
                V.scalar_tensor_tensor(out=y_out[:, 0, :], in0=agn[:], scalar=a_, in1=xwin[:, 0, 0:D],
                                       op0=ALU.mult, op1=ALU.add).then_inc(s_n_y1, 1)
                st.check(NN1)

            in_order = orderly(dve, (s_tab[0], 32))
            with dve.If_eq(in_order, 1):
                step(0, 0, nodes=False)
                step(1, 1)
                with dve.Fori(1, GROUPS // 2 - 1) as n:
                    step(2 * n, 0)
                    step(2 * n + 1, 1)
                step(GROUPS - 2, 0, far=False)
                step(GROUPS - 1, 1, more=False, far=False)
                step(GROUPS, 0, edges=False)
            with dve.Else():
                dve.wait_ge(s_Sa, NCH - 1)
                V.memset(e_new, 0.0).then_inc(s_e_blank, 1)
                dve.wait_ge(s_e_blank, 1)
                V.memset(e_new[:, 0:H], BIG).then_inc(s_e_blank, 1)
                V.memset(od_t[:], 0.0).then_inc(s_e_blank, 1)
                dve.wait_ge(s_e_init, 16 * (NT + 1))
                with dve.Fori(0, TILES) as k:
                    edge_tile(k)
                with dve.Fori(0, NT) as n:
                    node_tile(n)

            M_ = Steps(nc, dve, s_dM, 0)
            set_idx(1, 0, s_idx1)
            set_idx(3, 1, s_idx1)
            M_.then(V.tensor_scalar(src_hi, src_run_i[:], -(NT // 2), 1.0 / NT, ALU.add, ALU.mult))
            M_.then(V.tensor_scalar(src_hi, src_hi, ROUND, None, ALU.add))
            M_.then(V.tensor_scalar(src_hi, src_hi, ROUND, None, ALU.subtract))
            M_.then(V.scalar_tensor_tensor(out=src_key, in0=src_hi, scalar=-float(NT), in1=src_run_i[:],
                                           op0=ALU.mult, op1=ALU.add))
            M_.then(V.scalar_tensor_tensor(out=src_key, in0=src_key, scalar=float(W), in1=run_row[:],
                                           op0=ALU.mult, op1=ALU.add))
            for k in range(0, NT * W, P):
                w = min(P, NT * W - k)
                M_.mark(V.tensor_scalar(iota_key[:, k:k + w], iota[:, 0:w], float(k), None, ALU.add))
            M_.then(V.memset(zeros_b, 0.0))

            stats(M_, s_x2l)
            dve.wait_ge(s_odl, 16)
            M_.mark(V.tensor_scalar(v2[:, 0, :], mv[:, :, 1], EPS_LN, None, ALU.add))
            M_.then(V.tensor_tensor(v2[:, 1, :], xt[:, :, D], od_t[:], ALU.add))
            M_.then(V.tensor_scalar(v2[:, 1, :], v2[:, 1, :], 1.0, None, ALU.max))
            rsqrt(M_, y2[:], v2[:], t2[:])
            V.tensor_copy(dinv_t[:], y2[:, 1, :]).then_inc(s_dinv, 1)
            for i in range(NT):
                if i >= 4:
                    dve.wait_ge(s_xn2T, i - 3)
                V.tensor_scalar(xn[:, i % 4, :], xt[:, i, 0:D], mv[:, i, 0:1], y2[:, 0, i:i + 1],
                                ALU.subtract, ALU.mult).then_inc(s_xn2, 1)
                if i:
                    square_norm(i - 1)
            square_norm(NT - 1)
            M_.sync()

            v_, y_, t_, nc_, q_, ser, at_, a_ = [sm[:, i, :] for i in range(8)]
            M_.then(V.tensor_scalar(v_, ss_t[:], 1e-30, None, ALU.max))
            rsqrt(M_, y_, v_, t_)
            M_.then(V.tensor_tensor(t_, ss_t[:], y_, ALU.mult))
            M_.then(V.tensor_scalar(nc_, t_, 1e-15, ATANH_MAX, ALU.max, ALU.min))
            M_.mark(V.tensor_tensor(q_, nc_, nc_, ALU.mult))
            M_.then(V.tensor_scalar(t_, nc_, -1.0, 1.0, ALU.mult, ALU.add))
            M_.mark(V.tensor_scalar(ser, q_, 1.0 / 9, 1.0 / 7, ALU.mult, ALU.add))
            M_.then(V.reciprocal(t_, t_))
            V.scalar_tensor_tensor(out=rat[:], in0=nc_, scalar=2.0, in1=t_, op0=ALU.mult, op1=ALU.mult).then_inc(s_nc, 1)
            for k in (1.0 / 5, 1.0 / 3, 1.0):
                M_.then(V.tensor_tensor(ser, ser, q_, ALU.mult))
                M_.then(V.tensor_scalar(ser, ser, k, None, ALU.add))
            M_.then(V.tensor_tensor(ser, ser, nc_, ALU.mult))
            dve.wait_ge(s_ln, 1)
            M_.then(V.scalar_tensor_tensor(out=t_, in0=lnv[:], scalar=-0.5, in1=ser, op0=ALU.mult, op1=ALU.add))
            M_.then(V.scalar_tensor_tensor(out=t_, in0=nc_, scalar=SERIES_BELOW, in1=t_, op0=ALU.is_lt, op1=ALU.mult))
            M_.then(V.scalar_tensor_tensor(out=at_, in0=lnv[:], scalar=0.5, in1=t_, op0=ALU.mult, op1=ALU.add))
            M_.then(V.tensor_tensor(a_, at_, y_, ALU.mult))
            M_.then(V.tensor_tensor(a_, a_, y2[:, 1, :], ALU.mult))
            dve.wait_ge(s_h1, NT)
            for i in range(NT):
                dve.wait_ge(s_b1d, i + 1)
                V.scalar_tensor_tensor(out=hs_t[:, i, :], in0=h1_of(i), scalar=a_[:, i:i + 1], in1=b1d[:, i, :],
                                       op0=ALU.mult, op1=ALU.add).then_inc(s_hs, 1)

            V.memset(R[:, 1, :], 0.0).then_inc(s_R1, 1)
            dve.wait_ge(s_hs, NT)
            v_, y_, t_, a_ = [sm1[:, i:i + 1] for i in range(4)]

            def shift1(g, b):
                if not (known(g) and g < 2):
                    dve.wait_ge(s_agg1, g - 1)
                V.tensor_scalar(shift[:, b, :], imj[:], col(delta, g), None, ALU.is_equal).then_inc(s_shift1, 1)

            def run_one_hots(n, t):
                if t == 0 and not (known(n) and n == 0):
                    dve.wait_ge(s_cnt, 2 * n)
                V.tensor_scalar(oh_key(t), iota_key, run_col(src_key, n, t), None, ALU.is_equal).then_inc(s_ohr, 1)
                V.tensor_scalar(oh_node[:, t, :], iota_b[:], run_col(src_hi, n, t), None, ALU.is_equal).then_inc(s_ohr, 1)

            def run_col(tile, n, t):
                flat_ = tile.rearrange("p g t -> p (g t)")
                return flat_[:, n * T + t:n * T + t + 1] if known(n) else flat_[:, bass.ds(n * T + t, 1)]

            def out_rows(g, b, more=True, run=None):
                tiles = iter(range(T) if run is not None else ())

                def meanwhile():
                    for t in tiles:
                        run_one_hots(run, t)
                        break

                st = Steps(nc, dve, s_d1, N1 * g)
                dve.wait_ge(s_agg1, g + 1)
                V.tensor_copy(R[:, b, 0:D], sum_banks[b][:, 0:D]).then_inc(s_R1, 1)
                dve.wait_ge(s_R1, g + 2)
                dve.wait_ge(s_xw1[b], 16 * (g + 2 - b))
                st.then(V.tensor_scalar(agn[:], R[:, b, 0:D], xwin[:, b, D:D + 1], None, ALU.mult))
                if more:
                    shift1(g + 2, b)
                st.mark(V.scalar_tensor_tensor(out=hsq[:, 0, :], in0=agn[:], scalar=1.0, in1=agn[:], op0=ALU.mult,
                                               op1=ALU.mult, accum_out=ss[:]))
                meanwhile()
                st.sync()
                st.mark(V.tensor_scalar(v_, ss[:], 1e-30, None, ALU.max))
                meanwhile()
                st.sync()
                rsqrt(st, y_, v_, t_, meanwhile)
                V.tensor_tensor(nrm[:], ss[:], y_, ALU.mult).then_inc(s_norm1, 1)
                for _ in range(T):
                    meanwhile()
                dve.wait_ge(s_th1, g + 1)
                st.then(V.tensor_scalar(a_, y_, 1e15, th[:], ALU.min, ALU.mult))
                if not (known(g) and g < 2):
                    dve.wait_ge(s_yst, 16 * (g - 1))
                V.scalar_tensor_tensor(out=y_out[:, b, :], in0=agn[:], scalar=a_, in1=xwin[:, b, 0:D],
                                       op0=ALU.mult, op1=ALU.add).then_inc(s_y1, 1)
                st.check(N1)

            def pair(n, j, more=True, far=True):
                out_rows(2 * n, 0, more=more)
                if far:
                    dve.wait_ge(s_g1[j], 8 * T * (n + 2 - j))
                    set_idx(2 * n + 5, j, s_idx1)
                out_rows(2 * n + 1, 1, more=more, run=n + 2 if far else None)

            with dve.If_eq(in_order, 1):
                for t in range(T):
                    run_one_hots(0, t)
                for t in range(T):
                    run_one_hots(1, t)
                shift1(0, 0)
                shift1(1, 1)
                pair(0, 0)
                pair(1, 1)
                with dve.Fori(1, DG // 2 - 1) as m:
                    pair(2 * m, 0)
                    pair(2 * m + 1, 1)
                pair(DG - 2, 0, far=False)
                pair(DG - 1, 1, more=False, far=False)
            with dve.Else():
                V.memset(e_new, 0.0).then_inc(s_e_blank1, 1)
                dve.wait_ge(s_e_init1, 16 * NT)
                with dve.Fori(0, TILES) as k:
                    edge_tile1(k)
                with dve.Fori(0, NT) as n:
                    node_tile1(n)

        @block.scalar
        def _(act):
            A = nc.scalar
            for i in range(NT):
                act.wait_ge(s_xnT, i + 1)
                if i >= 2:
                    act.wait_ge(s_qkvp, i - 1)
                A.activation(hT[:, i % 2, :], ps_s[i % 2][:, 0:D], ACT.Relu).then_inc(s_hT, 1)
            act.wait_ge(s_in, 16 * 18)
            for t in range(T):
                A.copy(be_r[:, t, :], be_s[:]).then_inc(s_ber, 1)

            def one_hots(g, b, chunks):
                if 0 in chunks and not (known(g) and g < 2):
                    act.wait_ge(s_agg, g - 1)
                for c in chunks:
                    t0, t1 = CH[c]
                    for t in range(t0, t1):
                        A.activation(S[:, b, t, :], iota[:], ACT.Abs, bias=nloc[:, g, t:t + 1] if known(g) else
                                     nloc[:, bass.ds(g, 1), t:t + 1].rearrange("p g t -> p (g t)")).then_inc(s_Sab, 1)
                    act.wait_ge(s_Sab, TA * g + t1)
                    A.activation(S[:, b, t0:t1, :], S[:, b, t0:t1, :], ACT.Relu, bias=1.0, scale=-1.0).then_inc(s_Sa, 1)

            def turn_copies(g, b, chunks):
                if 0 in chunks and not (known(g) and g < 2):
                    act.wait_ge(s_qt, NCH * (g - 1))
                for c in chunks:
                    t0, t1 = CH[c]
                    w = (t1 - t0) * P
                    act.wait_ge(s_stp, NCH * g + c + 1)
                    A.copy(ST[:, b, t0:t1, :].rearrange("p t e -> p (t e)"), ps_s[c % 2][:, 0:w]).then_inc(s_st, 1)

            def agg_copy(g):
                act.wait_ge(s_agTp, g + 1)
                if not (known(g) and g == 0):
                    act.wait_ge(s_o, g)
                A.copy(agT[:], ps_f[:, 0:D]).then_inc(s_agT, 1)

            def carry_factor(g):
                act.wait_ge(s_dfac, g + 1)
                A.activation(fac[:], dfac[:], ACT.Exp).then_inc(s_fac, 1)

            def weights(g):
                act.wait_ge(s_z, g + 1)
                if not (known(g) and g == 0):
                    act.wait_ge(s_agg, g)
                A.activation(wv[:, :, 0:C].rearrange("p t (h e) -> p h t e", e=DH + 1)[:, :, :, DH], z[:], ACT.Exp)\
                    .then_inc(s_p, 1)

            def step(g, b, nodes=True, more=True):
                if more:
                    one_hots(g + 1, 1 - b, (0, 1))
                    turn_copies(g + 1, 1 - b, (0,))
                if nodes:
                    agg_copy(g - 1)
                if more:
                    one_hots(g + 1, 1 - b, (2,))
                carry_factor(g)
                weights(g)
                if more:
                    turn_copies(g + 1, 1 - b, (1, 2, 3))

            act.wait_ge(s_nloc, 1)
            one_hots(0, 0, (0, 1, 2))
            act.wait_ge(s_reset, 2)
            for h in range(H):
                A.copy(fwd_reset8[:, :, h, :], fwd_reset[:]).then_inc(s_reset8, 1)
                A.copy(bwd_reset8[:, :, h, :], bwd_reset[:, :, ::-1]).then_inc(s_reset8, 1)
            in_order = orderly(act, (s_reset, 2))
            with act.If_eq(in_order, 1):
                turn_copies(0, 0, (0, 1, 2, 3))
                step(0, 0, nodes=False)
                with act.Fori(0, GROUPS // 2 - 1) as n:
                    step(2 * n + 1, 1)
                    step(2 * n + 2, 0)
                step(GROUPS - 1, 1, more=False)
                agg_copy(GROUPS - 1)
            with act.Else():
                with act.Fori(0, TILES) as k:
                    wait_apart(act, s_e_z, 2 * k + 2, (s_reset, 2))
                    A.activation(e_exp[:], e_exp[:], ACT.Exp).then_inc(s_e_exp, 1)
                with act.Fori(0, NT) as n:
                    wait_apart(act, s_n_agTp, n + 1, (s_reset, 2))
                    A.copy(agT[:], ps_f[:, 0:D]).then_inc(s_n_agT, 1)

            for i in range(NT):
                act.wait_ge(s_xn2T, i + 1)
                if i >= 2:
                    act.wait_ge(s_h1, i - 1)
                A.activation(hT[:, i % 2, :], turned[i % 2][:, 0:D], ACT.Relu).then_inc(s_h2T, 1)
                if i == 0:
                    act.wait_ge(s_dinv, 1)
                A.activation(b1d[:, i, :], b1_s[:], ACT.Copy, scale=dinv_t[:, i:i + 1]).then_inc(s_b1d, 1)
            act.wait_ge(s_nc, 1)
            A.activation(lnv[:], rat[:], ACT.Ln, bias=1.0).then_inc(s_ln, 1)

            def norm_part(g):
                act.wait_ge(s_norm1, g + 1)
                A.activation(th[:], nrm[:], ACT.Tanh).then_inc(s_th1, 1)

            def one_hots1(n, j):
                if not (known(n) and n < 2):
                    act.wait_ge(s_agg1, 2 * n - 2)
                g = 2 * n + 1
                for t0, t1 in CH:
                    for t in range(t0, t1):
                        A.activation(S[:, j, t, :], iota[:], ACT.Abs, bias=nloc[:, g, t:t + 1] if known(g) else
                                     nloc[:, bass.ds(g, 1), t:t + 1].rearrange("p g t -> p (g t)")).then_inc(s_Sab, 1)
                    act.wait_ge(s_Sab, TA * GROUPS + T * n + t1)
                    A.activation(S[:, j, t0:t1, :], S[:, j, t0:t1, :], ACT.Relu, bias=1.0, scale=-1.0).then_inc(s_S1, 1)

            def count_copies(n, k):
                if k == 0 and not (known(n) and n == 0):
                    act.wait_ge(s_agg1, 2 * n - 1)
                act.wait_ge(s_cnt, 2 * n + k + 1)
                i0, i1 = HALVES[k]
                for (h0, h1), bank in zip(BANKS[i0:i1], count_banks[i0:i1]):
                    A.copy(counts[:, h0:h1, :], bank[:, 0:(h1 - h0) * P].rearrange("p (h e) -> p h e", e=P))\
                        .then_inc(s_cntc, 1)

            with act.If_eq(in_order, 1):
                one_hots1(0, 0)
                one_hots1(1, 1)
                count_copies(0, 0)
                count_copies(0, 1)

                def pair(n, j, more=True, far=True):
                    if more:
                        count_copies(n + 1, 0)
                    norm_part(2 * n)
                    if more:
                        count_copies(n + 1, 1)
                    if far:
                        one_hots1(n + 2, j)
                    norm_part(2 * n + 1)

                with act.Fori(0, DG // 2 - 1) as m:
                    pair(2 * m, 0)
                    pair(2 * m + 1, 1)
                pair(DG - 2, 0, far=False)
                pair(DG - 1, 1, more=False, far=False)
            with act.Else():
                with act.Fori(0, NT) as n:
                    wait_apart(act, s_n_z1, n + 1, (s_reset, 2))
                    A.activation(hsq[:, 0, :], agn[:], ACT.Square, accum_out=ss[:]).then_inc(s_n_ss1, 1)
                    wait_apart(act, s_n_norm1, n + 1, (s_reset, 2))
                    A.activation(th[:], nrm[:], ACT.Tanh).then_inc(s_n_th1, 1)

        @block.tensor
        def _(pe):
            M = nc.tensor
            pe.wait_ge(s_w, 16 * 3)

            def turn_tile(i):
                pe.wait_ge(s_xn, i + 1)
                if i >= 2:
                    pe.wait_ge(s_hT, i - 1)
                M.transpose(ps_s[i % 2][:, 0:D], xn[:, i % 4, :], ident[:]).then_inc(s_xnT, 1)

            turn_tile(0)
            for i in range(NT):
                if i + 1 < NT:
                    turn_tile(i + 1)
                pe.wait_ge(s_hT, i + 1)
                if i >= 2:
                    pe.wait_ge(s_qkv, i - 1)
                M.matmul(ps_q[i % 2][:, 0:3 * D], hT[:, i % 2, :], wqkv_s[:], start=True, stop=True).then_inc(s_qkvp, 1)
                if i == 15:
                    pe.wait_ge(s_in, 16 * 18)
                    pe.wait_ge(s_faults, 1)
                    M.transpose(ps_b[0:1, 0:P], faults[:], ident[:]).then_inc(s_faultsT, 1)
            pe.wait_ge(s_part, 1)
            M.transpose(ps_b[0:2 * GROUPS, 0:P], part_reset[:].rearrange("p k g -> p (k g)"), ident[:]).then_inc(s_partT, 1)

            def turn(g, b, chunks):
                for c in chunks:
                    t0, t1 = CH[c]
                    if t1 <= TA:
                        pe.wait_ge(s_Sa, (NCH - 1) * g + c + 1)
                    else:
                        pe.wait_ge(s_S, 2 * g + 2)
                    if not (known(g) and g == 0 and c < 2):
                        pe.wait_ge(s_st, NCH * g + c - 1)
                    for t in range(t0, t1):
                        mm = M.transpose(ps_s[c % 2][:, (t - t0) * P:(t - t0 + 1) * P], S[:, b, t, :], ident[:])
                    mm.then_inc(s_stp, 1)

            def bias(g, b, parts):
                if 0 in parts:
                    if not (known(g) and g == 0):
                        pe.wait_ge(s_sc, g)
                    M.matmul(p_bias, ones_row[:], be_r[:].rearrange("p t h -> p (t h)"), start=True, stop=False)
                    pe.wait_ge(s_attr[b], 32 * ((g - b) // 2 + 1) if known(g) else (g + (2 - b)) * 16)
                for k in parts:
                    r, w = (P, 4 * H) if k < 3 else (EF, H)
                    mm = M.matmul(p_bias[:, 4 * H * k:4 * H * k + w], attr_s[0:r, b, k, :], we4[0:r, 0:w],
                                  start=False, stop=k == 3)
                if 3 in parts:
                    mm.then_inc(s_bias, 1)

            def query(g, b, chunks):
                if 0 in chunks:
                    pe.wait_ge(s_qwin[b], 16 * ((g - b) // 2 + 1) if known(g) else (g + (2 - b)) * 8)
                for c in chunks:
                    t0, t1 = CH[c]
                    pe.wait_ge(s_st, NCH * g + c + 1)
                    if not (known(g) and g == 0 and c < 2):
                        pe.wait_ge(s_prod, NCH * g + c - 1)
                    for t in range(t0, t1):
                        mm = M.matmul(ps_q[c % 2][:, (t - t0) * D:(t - t0 + 1) * D], ST[:, b, t, :], qwin[:, b, :],
                                      start=True, stop=True)
                    mm.then_inc(s_qt, 1)

            def window_sums(g, b, bias_read=True):
                pe.wait_ge(s_wv, g + 1)
                for t in range(T):
                    mm = M.matmul(ps_r[:, 0:C + 1], S[:, b, t, :], wv[:, t, :], start=(t == 0), stop=(t == T - 1))
                mm.then_inc(s_agg, 1)
                if not (known(g) and g == 0):
                    pe.wait_ge(s_R, g)
                if bias_read:
                    pe.wait_ge(s_sc, g + 2)
                M.matmul(p_rc, shift[:, b, :], R[:, 1 - b, :], start=True, stop=True)
                pe.wait_ge(s_facd, g + 1)
                M.matmul(p_fb, isf[:], facd[:], start=True, stop=True).then_inc(s_rc, 1)

            def step(g, b, edges=True, nodes=True, more=True):
                if edges:
                    query(g, b, (2, 3))
                if nodes:
                    window_sums(g - 1, 1 - b, edges)
                if edges:
                    pe.wait_ge(s_oh, 2 * g + 2)
                    if not (known(g) and g == 0):
                        pe.wait_ge(s_od, g)
                    for t in range(T):
                        mm = M.matmul(ps_f[0:HI, 3 * D:3 * D + LO], oh_hi[:, b, :, t], oh_lo[:, b, :, t],
                                      start=(t == 0), stop=(t == T - 1))
                    mm.then_inc(s_hist, 1)
                    pe.wait_ge(s_v1, g + 1)
                    M.transpose(p_v1, f1[:, :, T - 1], ident[:]).then_inc(s_v1T, 1)
                if edges:
                    wait_apart(pe, s_cf, g + 1, (s_part, 1))
                    M.transpose(p_c1, c1[:, b, 0:P], ident[0:H, 0:H]).then_inc(s_cfT, 1)
                if nodes:
                    pe.wait_ge(s_agn, g)
                    M.transpose(ps_f[:, 0:D], agn[:], ident[:]).then_inc(s_agTp, 1)
                if edges:
                    if more:
                        turn(g + 1, 1 - b, (0,))
                    pe.wait_ge(s_v2, g + 1)
                    M.transpose(p_v2, bx[:, :, 0], ident[:]).then_inc(s_v2T, 1)
                    if more:
                        turn(g + 1, 1 - b, (1,))
                    wait_apart(pe, s_cb, g + 1, (s_part, 1))
                    M.transpose(p_c2, c2[:, 1:P + 1], ident[0:H, 0:H]).then_inc(s_cbT, 1)
                if nodes:
                    pe.wait_ge(s_agT, g)
                    if not (known(g) and g == 1):
                        pe.wait_ge(s_x2, 2 * g - 2)
                    M.matmul(ps_f[:, D:2 * D], ones_row[:], bo_s[:], start=True, stop=False)
                    M.matmul(ps_f[:, D:2 * D], agT[:], wo_s[:], start=False, stop=True).then_inc(s_o, 1)
                if edges and more:
                    query(g + 1, 1 - b, (0,))
                    bias(g + 1, 1 - b, (0, 1))
                    turn(g + 1, 1 - b, (2,))
                    query(g + 1, 1 - b, (1,))
                    turn(g + 1, 1 - b, (3,))
                    bias(g + 1, 1 - b, (2, 3))

            pe.wait_ge(s_ber, T)
            in_order = orderly(pe, (s_part, 1))
            with pe.If_eq(in_order, 1):
                bias(0, 0, (0, 1, 2, 3))
                turn(0, 0, (0, 1, 2, 3))
                query(0, 0, (0, 1))
                step(0, 0, nodes=False)
                step(1, 1)
                with pe.Fori(1, GROUPS // 2 - 1) as n:
                    step(2 * n, 0)
                    step(2 * n + 1, 1)
                step(GROUPS - 2, 0)
                step(GROUPS - 1, 1, more=False)
                step(GROUPS, 0, edges=False)
            with pe.Else():
                past = (s_part, 1)
                with pe.Fori(0, TILES) as k:
                    wait_apart(pe, s_e_rep, 2 * k + 2, past)
                    M.transpose(ps_s[0][:, 0:P], dst_rep, ident[:])
                    M.transpose(ps_s[0][:, P:2 * P], src_rep, ident[:]).then_inc(s_e_repT, 1)
                    wait_apart(pe, s_e_attr, 16 * k + 16, past)
                    M.matmul(ps_b[:, 0:H], ones_row[:], be_s[:], start=True, stop=False)
                    M.matmul(ps_b[:, 0:H], e_attr, we4[0:EF, 0:H], start=False, stop=True).then_inc(s_e_bias, 1)
                    wait_apart(pe, s_e_sc, k + 1, past)
                    for h in range(H):
                        mm = M.transpose(ps_q[h // 4][:, h % 4 * P:(h % 4 + 1) * P], sc_rep[:, h, :], ident[:])
                    mm.then_inc(s_e_scT, 1)
                    wait_apart(pe, s_e_wv, 2 * k + 2, past)
                    M.matmul(ps_r[:, 0:C + 1], same_dst, e_wv, start=True, stop=True)
                    M.matmul(ps_r[:, C + 1:C + 2], same_src, e_wv[:, C:C + 1], start=True, stop=True).then_inc(s_e_sum, 1)
                with pe.Fori(0, NT) as n:
                    wait_apart(pe, s_n_agn, n + 1, past)
                    M.transpose(ps_f[:, 0:D], agn[:], ident[:]).then_inc(s_n_agTp, 1)
                    wait_apart(pe, s_n_agT, n + 1, past)
                    M.matmul(ps_f[:, D:2 * D], ones_row[:], bo_s[:], start=True, stop=False)
                    M.matmul(ps_f[:, D:2 * D], agT[:], wo_s[:], start=False, stop=True).then_inc(s_n_o, 1)

            def turn_node(i):
                pe.wait_ge(s_xn2, i + 1)
                if i >= 2:
                    pe.wait_ge(s_h2T, i - 1)
                M.transpose(turned[i % 2][:, 0:D], xn[:, i % 4, :], ident[:]).then_inc(s_xn2T, 1)

            turn_node(0)
            for i in range(NT):
                if i + 1 < NT:
                    turn_node(i + 1)
                pe.wait_ge(s_h2T, i + 1)
                M.matmul(h1_of(i), hT[:, i % 2, :], w1_s[:], start=True, stop=True).then_inc(s_h1, 1)

            def count(n):
                if not (known(n) and n == 0):
                    pe.wait_ge(s_cntc, len(BANKS) * n)
                if not (known(n) and n < 2):
                    pe.wait_ge(s_R1, 2 * n - 1)
                for (h0, h1), bank in zip(BANKS, count_banks):
                    M.matmul(bank[:, 0:(h1 - h0) * P], zeros_b[:, 0:P], zeros_b[:, 0:(h1 - h0) * P], start=True, stop=False)
                for k, (i0, i1) in enumerate(HALVES):
                    for t in range(T):
                        if k == 0 and t % 4 == 0:
                            pe.wait_ge(s_ohr, 2 * T * n + 2 * min(t + 4, T))
                        for (h0, h1), bank in zip(BANKS[i0:i1], count_banks[i0:i1]):
                            mm = M.matmul(bank[:, 0:(h1 - h0) * P].rearrange("p (h e) -> p h e", e=P)
                                          [:, :, ROW0[t]:ROW0[t] + W],
                                          oh_node[:, t, :], oh_key(t)[:, h0 * W:h1 * W], start=False, stop=t == T - 1)
                    mm.then_inc(s_cnt, 1)

            def carried(g, b):
                pe.wait_ge(s_shift1, g + 1)
                pe.wait_ge(s_R1, g + 1)
                M.matmul(sum_banks[b][:, 0:D], shift[:, b, :], R[:, 1 - b, 0:D], start=False, stop=True).then_inc(s_agg1, 1)

            def counted_sums(n):
                for i in range(NT):
                    if i in (0, BANKS[HALVES[1][0]][0]):
                        pe.wait_ge(s_cntc, len(BANKS) * n + HALVES[0 if i == 0 else 1][1])
                    M.matmul(ps_r[:, 0:D], counts[:, i, :], hs_t[:, i, :], start=(i == 0), stop=False)
                carried(2 * n, 0)

            def gathered_sums(n, j, more=True):
                pe.wait_ge(s_cntc, len(BANKS) * (n + 1) + (1 if more else 0))
                pe.wait_ge(s_S1, NCH * (n + 1))
                pe.wait_ge(s_g1[j], 8 * T * (n + 2 - j))
                for t in range(T):
                    M.matmul(sum_banks[1][:, 0:D], S[:, j, t, :], kv[:, j, t, 0:D], start=(t == 0), stop=False)
                carried(2 * n + 1, 1)

            def pair(n, j, more=True):
                counted_sums(n)
                if more:
                    count(n + 1)
                gathered_sums(n, j, more)

            with pe.If_eq(in_order, 1):
                pe.wait_ge(s_hs, NT)
                count(0)
                pair(0, 0)
                pair(1, 1)
                with pe.Fori(1, DG // 2 - 1) as m:
                    pair(2 * m, 0)
                    pair(2 * m + 1, 1)
                pair(DG - 2, 0)
                pair(DG - 1, 1, more=False)
            with pe.Else():
                with pe.Fori(0, TILES) as k:
                    wait_apart(pe, s_e_rep1, 2 * k + 2, past)
                    M.transpose(ps_s[0][:, 0:P], dst_rep, ident[:]).then_inc(s_e_repT1, 1)
                    wait_apart(pe, s_e_same1, k + 1, past)
                    wait_apart(pe, s_e_got1[0], 16 * k + 16, past)
                    M.matmul(ps_r[:, 0:D], same_dst, e_kv[:, 0:D], start=True, stop=True).then_inc(s_e_sum1, 1)


def kernel(**inputs):
    import concourse.bacc as _bacc
    from concourse.bass_utils import run_bass_kernel_spmd as _run

    a = {k: np.ascontiguousarray(v) for k, v in inputs.items()}

    def filled(v, rows, value=0):
        full = np.full((rows,) + v.shape[1:], value, v.dtype)
        full[:len(v)] = v
        return full

    def lanes(v):
        return v.reshape(GROUPS, P, T).transpose(1, 0, 2)

    def in_runs(v):
        return v.reshape(DG, 2, T, P)[:, 0]

    src = filled(a["src"], GROUPS * GE, N)
    dst = filled(a["dst"], GROUPS * GE, N)
    runs = dst.reshape(GROUPS * P, T)
    before = np.concatenate([np.full(1, -1, np.int32), runs[:-1, T - 1]]).reshape(GROUPS, P).T
    after = np.concatenate([runs[1:, 0], np.full(1, -1, np.int32)]).reshape(GROUPS, P).T
    attr = filled(a["edge_attr_32"], GROUPS * GE).reshape(GROUPS, P, T * EF).transpose(0, 2, 1)
    rows, cols = np.indices((P, P)).astype(np.float32)
    ins = {
        "x": filled(a["x"], NPAD),
        "src_t": lanes(src).reshape(P, GROUPS * T),
        "dst_t": lanes(dst).reshape(P, GROUPS * T),
        "dst_before": before, "dst_after": after,
        "dst_first": dst[::GE][None, :],
        "dst_run": in_runs(dst).transpose(2, 0, 1).reshape(P, DG * T),
        "src_run": in_runs(src).transpose(2, 0, 1).reshape(P, DG * T),
        "attr": attr,
        "wqkv": np.concatenate([a["L0_gnn_Wq"], a["L0_gnn_Wk"], a["L0_gnn_Wv"]], axis=1),
        "bqkv": np.concatenate([a["L0_gnn_bq"], a["L0_gnn_bk"], a["L0_gnn_bv"]])[None, :],
        "we": a["L0_gnn_We"], "be": a["L0_gnn_be"][None, :],
        "wo": a["L0_gnn_Wo"], "bo": a["L0_gnn_bo"][None, :],
        "w1t": a["L1_gnn_W"].T, "b1": a["L1_gnn_b"][None, :],
        "ident_in": np.eye(P, dtype=np.float32), "iota_in": cols, "imj_in": rows - cols,
    }
    ins = {k: np.ascontiguousarray(v) for k, v in ins.items()}
    nc = _bacc.Bacc("TRN2", target_bir_lowering=False, num_devices=1)
    aps = {k: nc.dram_tensor(f"in_{k}", v.shape, mybir.dt.from_np(v.dtype), kind="ExternalInput").ap()
           for k, v in ins.items()}
    out = nc.dram_tensor("out", (N, D), F32, kind="ExternalOutput").ap()
    build(nc, out=out, **aps)
    r = _run(nc, [{f"in_{k}": v for k, v in ins.items()}], core_ids=[0])
    return r.results[0]["out"]
```
